# Optimizing a Trainium2 kernel written in Bass

```python
import numpy as np
import jax
import jax.numpy as jnp

def _softmax(x, axis=-1):
    return jax.nn.softmax(x, axis=axis)

def _gelu(x):
    return jax.nn.gelu(x, approximate=True)

def _silu(x):
    return jax.nn.silu(x)

def _sigmoid(x):
    return jax.nn.sigmoid(x)

def _layernorm(x, axis=-1, eps=1e-05):
    m = jnp.mean(x, axis=axis, keepdims=True)
    v = jnp.var(x, axis=axis, keepdims=True)
    return (x - m) / jnp.sqrt(v + eps)

def _scatter_add(tgt, idx, src, axis=0):
    return tgt.at[idx].add(src)

def _segment_sum(src, seg, n):
    return jax.ops.segment_sum(src, seg, n)
kernel_name = 'mk_xattn_seq_d4_seqx_r8_47b00c'

def setup_inputs(seed: int=0):
    np.random.seed(seed)
    _w = jnp.asarray

    def _rec_inputs():
        import jax
        import jax.numpy as jnp
        _rk = jax.random.key(seed)
        x = -0.000125 + 0.9999 * jax.random.normal(jax.random.fold_in(_rk, 1), (16, 56, 256), jnp.float32)
        _lenS = 56 - jax.random.randint(jax.random.fold_in(_rk, 7), (16,), 0, max(1, 56 // 4) + 1, jnp.int32)
        _lenS2 = 1500 - jax.random.randint(jax.random.fold_in(_rk, 8), (16,), 0, max(1, 1500 // 4) + 1, jnp.int32)
        _ctx_1024P = jax.random.normal(jax.random.fold_in(_rk, 11), (16, 16, 128), jnp.float32)
        _ctx_1024c = jax.random.dirichlet(jax.random.fold_in(_rk, 511), 0.3 * jnp.ones((16,), jnp.float32), (16, 1500))
        _ctx_1024t = jnp.einsum('bsk,bkd->bsd', _ctx_1024c, _ctx_1024P)
        _ctx_1024t = _ctx_1024t * jax.lax.rsqrt(jnp.mean(jnp.square(_ctx_1024t)) + 1e-12) * 0.953939
        ctx_1024 = 4.13588e-05 + 0.999923 * (_ctx_1024t + 0.3 * jax.random.normal(jax.random.fold_in(_rk, 611), (16, 1500, 128), jnp.float32))
        pos_1xS = jnp.broadcast_to(jnp.arange(56, dtype=jnp.int32), (1, 56))
        _validS = jnp.arange(56)[None, :] < _lenS[:, None]
        _validS2 = jnp.arange(1500)[None, :] < _lenS2[:, None]
        _causal = jnp.tril(jnp.ones((56, 56), dtype=bool))
        mask_BxS2_bk0 = jnp.logical_not(jnp.broadcast_to(_validS2[:, :], (16, 1500)))
        mask_BxS_ik0 = jnp.where(jnp.broadcast_to(_validS[:, :], (16, 56)), 0, 1).astype(jnp.int32)
        return (x, ctx_1024, pos_1xS, mask_BxS2_bk0, mask_BxS_ik0)
    x, ctx_1024, pos_1xS, mask_BxS2_bk0, mask_BxS_ik0 = _rec_inputs()

    def _L0_xattn_setup():
        import jax, jax.numpy as jnp
        import numpy as np
        EPS = 1e-06

        def _rmsnorm(x, w):
            var = jnp.mean(jnp.square(x), axis=-1, keepdims=True)
            return x * jax.lax.rsqrt(var + EPS) * w
        key = jax.random.key(seed)
        ks = jax.random.split(key, 6)
        B, N, M = (4, 512, 256)
        d_model, memory_dim = (256, 128)
        hidden_states = jax.random.normal(ks[0], (B, N, d_model), dtype=jnp.float32)
        memory = jax.random.normal(ks[1], (B, M, memory_dim), dtype=jnp.float32)
        W_mem = jax.random.normal(ks[2], (d_model, memory_dim), dtype=jnp.float32) / np.sqrt(memory_dim)
        W_gate = jax.random.normal(ks[3], (d_model, 2 * d_model), dtype=jnp.float32) / np.sqrt(2 * d_model)
        b_gate = jax.random.normal(ks[4], (d_model,), dtype=jnp.float32) * 0.01
        norm_w = jnp.ones((d_model,), dtype=jnp.float32)
        return {'hidden_states': hidden_states, 'memory': memory, 'W_mem': W_mem, 'W_gate': W_gate, 'b_gate': b_gate, 'norm_w': norm_w}
    _L0_xattn_all = _L0_xattn_setup()
    _L0_xattn_in = {k: v for k, v in _L0_xattn_all.items() if k in ('W_mem', 'W_gate', 'b_gate', 'norm_w')}
    del _L0_xattn_all

    def _L1_xattn_setup():
        import jax, jax.numpy as jnp
        import numpy as np
        DIM = 256
        DIM_MEDIA = 128
        HEADS = 16
        DIM_HEAD = 64
        INNER = HEADS * DIM_HEAD
        FF_INNER = 4 * DIM
        B, N_TOK, N_LAT = (4, 256, 64)
        EPS = 1e-05

        def layernorm(x, g, b):
            mu = jnp.mean(x, axis=-1, keepdims=True)
            var = jnp.var(x, axis=-1, keepdims=True)
            return (x - mu) * jax.lax.rsqrt(var + EPS) * g + b
        key = jax.random.key(seed)
        ks = jax.random.split(key, 12)
        x = jax.random.normal(ks[0], (B, N_TOK, DIM), dtype=jnp.float32)
        media = jax.random.normal(ks[1], (B, N_LAT, DIM_MEDIA), dtype=jnp.float32)
        media_mask = jax.random.randint(ks[2], (B, N_LAT), 0, 2).astype(bool)
        media_mask = media_mask.at[:, 0].set(True)
        s = lambda d: 1.0 / np.sqrt(d)
        Wq = jax.random.normal(ks[3], (DIM, INNER), dtype=jnp.float32) * s(DIM)
        Wkv = jax.random.normal(ks[4], (DIM_MEDIA, 2 * INNER), dtype=jnp.float32) * s(DIM_MEDIA)
        Wo = jax.random.normal(ks[5], (INNER, DIM), dtype=jnp.float32) * s(INNER)
        W1 = jax.random.normal(ks[6], (DIM, FF_INNER), dtype=jnp.float32) * s(DIM)
        W2 = jax.random.normal(ks[7], (FF_INNER, DIM), dtype=jnp.float32) * s(FF_INNER)
        return {'x': x, 'media': media, 'media_mask': media_mask, 'ln_q_g': jnp.ones((DIM,), jnp.float32), 'ln_q_b': jnp.zeros((DIM,), jnp.float32), 'Wq': Wq, 'Wkv': Wkv, 'Wo': Wo, 'attn_gate': jax.random.normal(ks[8], (1,), jnp.float32) * 0.5, 'ln_ff_g': jnp.ones((DIM,), jnp.float32), 'ln_ff_b': jnp.zeros((DIM,), jnp.float32), 'W1': W1, 'W2': W2, 'ff_gate': jax.random.normal(ks[9], (1,), jnp.float32) * 0.5}
    _L1_xattn_all = _L1_xattn_setup()
    _L1_xattn_in = {k: v for k, v in _L1_xattn_all.items() if k in ('ln_q_g', 'ln_q_b', 'Wq', 'Wkv', 'Wo', 'attn_gate', 'ln_ff_g', 'ln_ff_b', 'W1', 'W2', 'ff_gate')}
    del _L1_xattn_all

    def _L2_xattn_setup():
        import jax, jax.numpy as jnp
        import numpy as np
        H = 256
        NH = 16
        HD = H // NH
        CH = 128
        CC = 128
        CHD = CC // NH
        I = 688
        B = 2
        L = 256
        LE = 128
        EPS = 1e-06

        def rms_norm(x, w):
            xf = x.astype(jnp.float32)
            var = jnp.mean(xf * xf, axis=-1, keepdims=True)
            return (w * (xf * jax.lax.rsqrt(var + EPS))).astype(x.dtype)

        def expert_mask(tt):
            vm = jnp.zeros(tt.shape, dtype=bool)
            vm = vm.at[:, :-1].set((tt[:, :-1] == 1) & (tt[:, 1:] == 1))
            return vm

        def rotate_half(x):
            d = x.shape[-1] // 2
            return jnp.concatenate([-x[..., d:], x[..., :d]], axis=-1)

        def apply_rotary(q, k, position_ids, seq_len):
            inv = 1.0 / 10000.0 ** (jnp.arange(0, HD, 2, dtype=jnp.float32) / HD)
            t = jnp.arange(seq_len, dtype=jnp.float32)
            freqs = jnp.outer(t, inv)
            emb = jnp.concatenate([freqs, freqs], axis=-1)
            cos = jnp.cos(emb)[position_ids][:, None].astype(q.dtype)
            sin = jnp.sin(emb)[position_ids][:, None].astype(q.dtype)
            return (q * cos + rotate_half(q) * sin, k * cos + rotate_half(k) * sin)

        def sdpa(q, k, v, causal):
            scale = 1.0 / np.sqrt(q.shape[-1])
            scores = jnp.einsum('bhqd,bhkd->bhqk', q * scale, k)
            if causal:
                mask = jnp.tril(jnp.ones((q.shape[-2], k.shape[-2]), dtype=bool))
                scores = jnp.where(mask, scores, jnp.finfo(jnp.float32).min)
            p = jax.nn.softmax(scores.astype(jnp.float32), axis=-1).astype(q.dtype)
            return jnp.einsum('bhqk,bhkd->bhqd', p, v)

        def heads(x, nh, hd):
            b, l, _ = x.shape
            return x.reshape(b, l, nh, hd).transpose(0, 2, 1, 3)
        key = jax.random.key(seed)
        ks = jax.random.split(key, 20)
        s = 0.02
        f32 = jnp.float32
        return {'hidden_states': jax.random.normal(ks[0], (B, L, H), f32), 'encoder_outputs': jax.random.normal(ks[1], (B, LE, CH), f32), 'token_type_ids': jax.random.randint(ks[2], (B, L), 0, 2, jnp.int32), 'position_ids': jnp.arange(L, dtype=jnp.int32)[None, :], 'ln_in_w': jnp.ones((H,), f32), 'ln_post_attn_w': jnp.ones((H,), f32), 'ln_post_cross_w': jnp.ones((H,), f32), 'v_qkv': jax.random.normal(ks[3], (H, 3 * H), f32) * s, 'l_qkv': jax.random.normal(ks[4], (H, 3 * H), f32) * s, 'v_dense': jax.random.normal(ks[5], (H, H), f32) * s, 'l_dense': jax.random.normal(ks[6], (H, H), f32) * s, 'cq_w': jax.random.normal(ks[7], (H, CC), f32) * s, 'ckv_w': jax.random.normal(ks[8], (CH, 2 * CC), f32) * s, 'cdense_w': jax.random.normal(ks[9], (CC, H), f32) * s, 'v_gate': jax.random.normal(ks[10], (H, I), f32) * s, 'v_up': jax.random.normal(ks[11], (H, I), f32) * s, 'v_down': jax.random.normal(ks[12], (I, H), f32) * s, 'l_gate': jax.random.normal(ks[13], (H, I), f32) * s, 'l_up': jax.random.normal(ks[14], (H, I), f32) * s, 'l_down': jax.random.normal(ks[15], (I, H), f32) * s}
    _L2_xattn_all = _L2_xattn_setup()
    _L2_xattn_in = {k: v for k, v in _L2_xattn_all.items() if k in ('ln_in_w', 'ln_post_attn_w', 'ln_post_cross_w', 'v_qkv', 'l_qkv', 'v_dense', 'l_dense', 'cq_w', 'ckv_w', 'cdense_w', 'v_gate', 'v_up', 'v_down', 'l_gate', 'l_up', 'l_down')}
    del _L2_xattn_all

    def _L3_xattn_setup():
        import jax, jax.numpy as jnp
        import numpy as np
        DIM = 256
        DIM_MEDIA = 128
        HEADS = 16
        DIM_HEAD = 64
        INNER = HEADS * DIM_HEAD
        FF_INNER = 4 * DIM
        B, N_TOK, N_LAT = (4, 256, 64)
        EPS = 1e-05

        def layernorm(x, g, b):
            mu = jnp.mean(x, axis=-1, keepdims=True)
            var = jnp.var(x, axis=-1, keepdims=True)
            return (x - mu) * jax.lax.rsqrt(var + EPS) * g + b
        key = jax.random.key(seed)
        ks = jax.random.split(key, 12)
        x = jax.random.normal(ks[0], (B, N_TOK, DIM), dtype=jnp.float32)
        media = jax.random.normal(ks[1], (B, N_LAT, DIM_MEDIA), dtype=jnp.float32)
        media_mask = jax.random.randint(ks[2], (B, N_LAT), 0, 2).astype(bool)
        media_mask = media_mask.at[:, 0].set(True)
        s = lambda d: 1.0 / np.sqrt(d)
        Wq = jax.random.normal(ks[3], (DIM, INNER), dtype=jnp.float32) * s(DIM)
        Wkv = jax.random.normal(ks[4], (DIM_MEDIA, 2 * INNER), dtype=jnp.float32) * s(DIM_MEDIA)
        Wo = jax.random.normal(ks[5], (INNER, DIM), dtype=jnp.float32) * s(INNER)
        W1 = jax.random.normal(ks[6], (DIM, FF_INNER), dtype=jnp.float32) * s(DIM)
        W2 = jax.random.normal(ks[7], (FF_INNER, DIM), dtype=jnp.float32) * s(FF_INNER)
        return {'x': x, 'media': media, 'media_mask': media_mask, 'ln_q_g': jnp.ones((DIM,), jnp.float32), 'ln_q_b': jnp.zeros((DIM,), jnp.float32), 'Wq': Wq, 'Wkv': Wkv, 'Wo': Wo, 'attn_gate': jax.random.normal(ks[8], (1,), jnp.float32) * 0.5, 'ln_ff_g': jnp.ones((DIM,), jnp.float32), 'ln_ff_b': jnp.zeros((DIM,), jnp.float32), 'W1': W1, 'W2': W2, 'ff_gate': jax.random.normal(ks[9], (1,), jnp.float32) * 0.5}
    _L3_xattn_all = _L3_xattn_setup()
    _L3_xattn_in = {k: v for k, v in _L3_xattn_all.items() if k in ('ln_q_g', 'ln_q_b', 'Wq', 'Wkv', 'Wo', 'attn_gate', 'ln_ff_g', 'ln_ff_b', 'W1', 'W2', 'ff_gate')}
    del _L3_xattn_all
    return {'x': x, 'ctx_1024': ctx_1024, 'pos_1xS': pos_1xS, 'mask_BxS2_bk0': mask_BxS2_bk0, 'mask_BxS_ik0': mask_BxS_ik0, 'L0_xattn_W_mem': _L0_xattn_in['W_mem'], 'L0_xattn_W_gate': _L0_xattn_in['W_gate'], 'L0_xattn_b_gate': _L0_xattn_in['b_gate'], 'L0_xattn_norm_w': _L0_xattn_in['norm_w'], 'L1_xattn_ln_q_g': _L1_xattn_in['ln_q_g'], 'L1_xattn_ln_q_b': _L1_xattn_in['ln_q_b'], 'L1_xattn_Wq': _L1_xattn_in['Wq'], 'L1_xattn_Wkv': _L1_xattn_in['Wkv'], 'L1_xattn_Wo': _L1_xattn_in['Wo'], 'L1_xattn_attn_gate': _L1_xattn_in['attn_gate'], 'L1_xattn_ln_ff_g': _L1_xattn_in['ln_ff_g'], 'L1_xattn_ln_ff_b': _L1_xattn_in['ln_ff_b'], 'L1_xattn_W1': _L1_xattn_in['W1'], 'L1_xattn_W2': _L1_xattn_in['W2'], 'L1_xattn_ff_gate': _L1_xattn_in['ff_gate'], 'L2_xattn_ln_in_w': _L2_xattn_in['ln_in_w'], 'L2_xattn_ln_post_attn_w': _L2_xattn_in['ln_post_attn_w'], 'L2_xattn_ln_post_cross_w': _L2_xattn_in['ln_post_cross_w'], 'L2_xattn_v_qkv': _L2_xattn_in['v_qkv'], 'L2_xattn_l_qkv': _L2_xattn_in['l_qkv'], 'L2_xattn_v_dense': _L2_xattn_in['v_dense'], 'L2_xattn_l_dense': _L2_xattn_in['l_dense'], 'L2_xattn_cq_w': _L2_xattn_in['cq_w'], 'L2_xattn_ckv_w': _L2_xattn_in['ckv_w'], 'L2_xattn_cdense_w': _L2_xattn_in['cdense_w'], 'L2_xattn_v_gate': _L2_xattn_in['v_gate'], 'L2_xattn_v_up': _L2_xattn_in['v_up'], 'L2_xattn_v_down': _L2_xattn_in['v_down'], 'L2_xattn_l_gate': _L2_xattn_in['l_gate'], 'L2_xattn_l_up': _L2_xattn_in['l_up'], 'L2_xattn_l_down': _L2_xattn_in['l_down'], 'L3_xattn_ln_q_g': _L3_xattn_in['ln_q_g'], 'L3_xattn_ln_q_b': _L3_xattn_in['ln_q_b'], 'L3_xattn_Wq': _L3_xattn_in['Wq'], 'L3_xattn_Wkv': _L3_xattn_in['Wkv'], 'L3_xattn_Wo': _L3_xattn_in['Wo'], 'L3_xattn_attn_gate': _L3_xattn_in['attn_gate'], 'L3_xattn_ln_ff_g': _L3_xattn_in['ln_ff_g'], 'L3_xattn_ln_ff_b': _L3_xattn_in['ln_ff_b'], 'L3_xattn_W1': _L3_xattn_in['W1'], 'L3_xattn_W2': _L3_xattn_in['W2'], 'L3_xattn_ff_gate': _L3_xattn_in['ff_gate']}

def reference(x, ctx_1024, pos_1xS, mask_BxS2_bk0, mask_BxS_ik0, L0_xattn_W_mem, L0_xattn_W_gate, L0_xattn_b_gate, L0_xattn_norm_w, L1_xattn_ln_q_g, L1_xattn_ln_q_b, L1_xattn_Wq, L1_xattn_Wkv, L1_xattn_Wo, L1_xattn_attn_gate, L1_xattn_ln_ff_g, L1_xattn_ln_ff_b, L1_xattn_W1, L1_xattn_W2, L1_xattn_ff_gate, L2_xattn_ln_in_w, L2_xattn_ln_post_attn_w, L2_xattn_ln_post_cross_w, L2_xattn_v_qkv, L2_xattn_l_qkv, L2_xattn_v_dense, L2_xattn_l_dense, L2_xattn_cq_w, L2_xattn_ckv_w, L2_xattn_cdense_w, L2_xattn_v_gate, L2_xattn_v_up, L2_xattn_v_down, L2_xattn_l_gate, L2_xattn_l_up, L2_xattn_l_down, L3_xattn_ln_q_g, L3_xattn_ln_q_b, L3_xattn_Wq, L3_xattn_Wkv, L3_xattn_Wo, L3_xattn_attn_gate, L3_xattn_ln_ff_g, L3_xattn_ln_ff_b, L3_xattn_W1, L3_xattn_W2, L3_xattn_ff_gate):
    import jax
    import jax.numpy as jnp

    def _L0_xattn_ref(hidden_states, memory, W_mem, W_gate, b_gate, norm_w):
        import jax, jax.numpy as jnp
        import numpy as np
        EPS = 1e-06

        def _rmsnorm(x, w):
            var = jnp.mean(jnp.square(x), axis=-1, keepdims=True)
            return x * jax.lax.rsqrt(var + EPS) * w
        D = hidden_states.shape[-1]
        memory_proj = jnp.einsum('bme,de->bmd', memory, W_mem)
        scores = jnp.einsum('bnd,bmd->bnm', hidden_states, memory_proj) / jnp.sqrt(jnp.float32(D))
        attn = jax.nn.softmax(scores, axis=-1)
        memory_context = jnp.einsum('bnm,bmd->bnd', attn, memory_proj)
        gate_input = jnp.concatenate([hidden_states, memory_context], axis=-1)
        gate = jax.nn.sigmoid(jnp.einsum('bnf,df->bnd', gate_input, W_gate) + b_gate)
        fused = hidden_states + gate * memory_context
        return _rmsnorm(fused, norm_w)

    def _L1_xattn_ref(x, media, media_mask, ln_q_g, ln_q_b, Wq, Wkv, Wo, attn_gate, ln_ff_g, ln_ff_b, W1, W2, ff_gate):
        import jax, jax.numpy as jnp
        import numpy as np
        DIM = 256
        DIM_MEDIA = 128
        HEADS = 16
        DIM_HEAD = 64
        INNER = HEADS * DIM_HEAD
        FF_INNER = 4 * DIM
        B, N_TOK, N_LAT = (4, 256, 64)
        EPS = 1e-05

        def layernorm(x, g, b):
            mu = jnp.mean(x, axis=-1, keepdims=True)
            var = jnp.var(x, axis=-1, keepdims=True)
            return (x - mu) * jax.lax.rsqrt(var + EPS) * g + b
        scale = DIM_HEAD ** (-0.5)
        qn = layernorm(x, ln_q_g, ln_q_b)
        q = qn @ Wq * scale
        kv = media @ Wkv
        k, v = jnp.split(kv, 2, axis=-1)
        split_heads = lambda t: t.reshape(t.shape[0], t.shape[1], HEADS, DIM_HEAD).transpose(0, 2, 1, 3)
        q, k, v = (split_heads(q), split_heads(k), split_heads(v))
        sim = jnp.einsum('bhid,bhjd->bhij', q, k)
        neg_inf = jnp.finfo(sim.dtype).min
        sim = jnp.where(media_mask[:, None, None, :], sim, neg_inf)
        attn = jax.nn.softmax(sim, axis=-1)
        out = jnp.einsum('bhij,bhjd->bhid', attn, v)
        out = out.transpose(0, 2, 1, 3).reshape(x.shape[0], x.shape[1], INNER)
        attn_out = out @ Wo
        x = x + jnp.tanh(attn_gate) * attn_out
        h = layernorm(x, ln_ff_g, ln_ff_b)
        h = jax.nn.gelu(h @ W1, approximate=False) @ W2
        x = x + jnp.tanh(ff_gate) * h
        return x

    def _L2_xattn_ref(hidden_states, encoder_outputs, token_type_ids, position_ids, ln_in_w, ln_post_attn_w, ln_post_cross_w, v_qkv, l_qkv, v_dense, l_dense, cq_w, ckv_w, cdense_w, v_gate, v_up, v_down, l_gate, l_up, l_down):
        import jax, jax.numpy as jnp
        import numpy as np
        H = 256
        NH = 16
        HD = H // NH
        CH = 128
        CC = 128
        CHD = CC // NH
        I = 688
        B = 2
        L = 256
        LE = 128
        EPS = 1e-06

        def rms_norm(x, w):
            xf = x.astype(jnp.float32)
            var = jnp.mean(xf * xf, axis=-1, keepdims=True)
            return (w * (xf * jax.lax.rsqrt(var + EPS))).astype(x.dtype)

        def expert_mask(tt):
            vm = jnp.zeros(tt.shape, dtype=bool)
            vm = vm.at[:, :-1].set((tt[:, :-1] == 1) & (tt[:, 1:] == 1))
            return vm

        def rotate_half(x):
            d = x.shape[-1] // 2
            return jnp.concatenate([-x[..., d:], x[..., :d]], axis=-1)

        def apply_rotary(q, k, position_ids, seq_len):
            inv = 1.0 / 10000.0 ** (jnp.arange(0, HD, 2, dtype=jnp.float32) / HD)
            t = jnp.arange(seq_len, dtype=jnp.float32)
            freqs = jnp.outer(t, inv)
            emb = jnp.concatenate([freqs, freqs], axis=-1)
            cos = jnp.cos(emb)[position_ids][:, None].astype(q.dtype)
            sin = jnp.sin(emb)[position_ids][:, None].astype(q.dtype)
            return (q * cos + rotate_half(q) * sin, k * cos + rotate_half(k) * sin)

        def sdpa(q, k, v, causal):
            scale = 1.0 / np.sqrt(q.shape[-1])
            scores = jnp.einsum('bhqd,bhkd->bhqk', q * scale, k)
            if causal:
                mask = jnp.tril(jnp.ones((q.shape[-2], k.shape[-2]), dtype=bool))
                scores = jnp.where(mask, scores, jnp.finfo(jnp.float32).min)
            p = jax.nn.softmax(scores.astype(jnp.float32), axis=-1).astype(q.dtype)
            return jnp.einsum('bhqk,bhkd->bhqd', p, v)

        def heads(x, nh, hd):
            b, l, _ = x.shape
            return x.reshape(b, l, nh, hd).transpose(0, 2, 1, 3)
        b, l, _ = hidden_states.shape
        vm = expert_mask(token_type_ids)[..., None]
        residual = hidden_states
        x = rms_norm(hidden_states, ln_in_w)
        mixed = jnp.where(vm, x @ v_qkv, x @ l_qkv)
        q, k, v = jnp.split(mixed, 3, axis=-1)
        q, k, v = (heads(q, NH, HD), heads(k, NH, HD), heads(v, NH, HD))
        q, k = apply_rotary(q, k, position_ids, l)
        ctx = sdpa(q, k, v, causal=True)
        ctx = ctx.transpose(0, 2, 1, 3).reshape(b, l, H)
        attn_out = jnp.where(vm, ctx @ v_dense, ctx @ l_dense)
        hidden_states = residual + attn_out
        ci = rms_norm(hidden_states, ln_post_cross_w)
        cq = heads(ci @ cq_w, NH, CHD)
        ckv = encoder_outputs @ ckv_w
        ck, cv = jnp.split(ckv, 2, axis=-1)
        ck, cv = (heads(ck, NH, CHD), heads(cv, NH, CHD))
        cctx = sdpa(cq, ck, cv, causal=False)
        cctx = cctx.transpose(0, 2, 1, 3).reshape(b, l, CC)
        hidden_states = hidden_states + cctx @ cdense_w
        mi = rms_norm(hidden_states, ln_post_attn_w)
        v_out = jax.nn.silu(mi @ v_gate) * (mi @ v_up) @ v_down
        l_out = jax.nn.silu(mi @ l_gate) * (mi @ l_up) @ l_down
        hidden_states = hidden_states + jnp.where(vm, v_out, l_out)
        return hidden_states

    def _L3_xattn_ref(x, media, media_mask, ln_q_g, ln_q_b, Wq, Wkv, Wo, attn_gate, ln_ff_g, ln_ff_b, W1, W2, ff_gate):
        import jax, jax.numpy as jnp
        import numpy as np
        DIM = 256
        DIM_MEDIA = 128
        HEADS = 16
        DIM_HEAD = 64
        INNER = HEADS * DIM_HEAD
        FF_INNER = 4 * DIM
        B, N_TOK, N_LAT = (4, 256, 64)
        EPS = 1e-05

        def layernorm(x, g, b):
            mu = jnp.mean(x, axis=-1, keepdims=True)
            var = jnp.var(x, axis=-1, keepdims=True)
            return (x - mu) * jax.lax.rsqrt(var + EPS) * g + b
        scale = DIM_HEAD ** (-0.5)
        qn = layernorm(x, ln_q_g, ln_q_b)
        q = qn @ Wq * scale
        kv = media @ Wkv
        k, v = jnp.split(kv, 2, axis=-1)
        split_heads = lambda t: t.reshape(t.shape[0], t.shape[1], HEADS, DIM_HEAD).transpose(0, 2, 1, 3)
        q, k, v = (split_heads(q), split_heads(k), split_heads(v))
        sim = jnp.einsum('bhid,bhjd->bhij', q, k)
        neg_inf = jnp.finfo(sim.dtype).min
        sim = jnp.where(media_mask[:, None, None, :], sim, neg_inf)
        attn = jax.nn.softmax(sim, axis=-1)
        out = jnp.einsum('bhij,bhjd->bhid', attn, v)
        out = out.transpose(0, 2, 1, 3).reshape(x.shape[0], x.shape[1], INNER)
        attn_out = out @ Wo
        x = x + jnp.tanh(attn_gate) * attn_out
        h = layernorm(x, ln_ff_g, ln_ff_b)
        h = jax.nn.gelu(h @ W1, approximate=False) @ W2
        x = x + jnp.tanh(ff_gate) * h
        return x
    x = _L0_xattn_ref(x, ctx_1024, L0_xattn_W_mem, L0_xattn_W_gate, L0_xattn_b_gate, L0_xattn_norm_w)
    x = _L1_xattn_ref(x, ctx_1024, mask_BxS2_bk0, L1_xattn_ln_q_g, L1_xattn_ln_q_b, L1_xattn_Wq, L1_xattn_Wkv, L1_xattn_Wo, L1_xattn_attn_gate, L1_xattn_ln_ff_g, L1_xattn_ln_ff_b, L1_xattn_W1, L1_xattn_W2, L1_xattn_ff_gate)
    x = _L2_xattn_ref(x, ctx_1024, mask_BxS_ik0, pos_1xS, L2_xattn_ln_in_w, L2_xattn_ln_post_attn_w, L2_xattn_ln_post_cross_w, L2_xattn_v_qkv, L2_xattn_l_qkv, L2_xattn_v_dense, L2_xattn_l_dense, L2_xattn_cq_w, L2_xattn_ckv_w, L2_xattn_cdense_w, L2_xattn_v_gate, L2_xattn_v_up, L2_xattn_v_down, L2_xattn_l_gate, L2_xattn_l_up, L2_xattn_l_down)
    x = _L3_xattn_ref(x, ctx_1024, mask_BxS2_bk0, L3_xattn_ln_q_g, L3_xattn_ln_q_b, L3_xattn_Wq, L3_xattn_Wkv, L3_xattn_Wo, L3_xattn_attn_gate, L3_xattn_ln_ff_g, L3_xattn_ln_ff_b, L3_xattn_W1, L3_xattn_W2, L3_xattn_ff_gate)
    return x

_drawn_inputs = setup_inputs


def setup_inputs(seed=0):
    import zlib

    import numpy as np

    out = dict(_drawn_inputs(seed))
    spreads = {'L0_xattn_norm_w': (1.0, 0.2),
     'L1_xattn_ln_q_g': (1.0, 0.6),
     'L1_xattn_ln_q_b': (0.0, 0.8),
     'L1_xattn_ln_ff_g': (1.0, 0.6),
     'L1_xattn_ln_ff_b': (0.0, 0.8),
     'L2_xattn_ln_in_w': (1.0, 0.6),
     'L2_xattn_ln_post_attn_w': (1.0, 0.6),
     'L2_xattn_ln_post_cross_w': (1.0, 0.6),
     'L3_xattn_ln_q_g': (1.0, 0.6),
     'L3_xattn_ln_q_b': (0.0, 2.0),
     'L3_xattn_ln_ff_g': (1.0, 0.6),
     'L3_xattn_ln_ff_b': (0.0, 2.0)}
    factors = {'L0_xattn_b_gate': 8.0,
     'L1_xattn_W1': 2.827,
     'L2_xattn_v_qkv': 8.0,
     'L2_xattn_v_dense': 6.21,
     'L2_xattn_cq_w': 64.0,
     'L2_xattn_v_gate': 6.309,
     'L2_xattn_v_up': 6.191,
     'L2_xattn_v_down': 6.232,
     'L3_xattn_W1': 12.092,
     'L2_xattn_l_dense': 5.692,
     'L2_xattn_ckv_w': 7.612,
     'L2_xattn_cdense_w': 7.238,
     'L2_xattn_l_gate': 6.666,
     'L2_xattn_l_up': 6.555,
     'L2_xattn_l_down': 6.552,
     'L3_xattn_Wq': 14.494,
     'L3_xattn_W2': 3.427,
     'L3_xattn_Wkv': 3.838,
     'L3_xattn_Wo': 3.82}
    for name, (base, spread) in spreads.items():
        noise = np.random.default_rng([zlib.crc32(name.encode()), seed]).standard_normal(out[name].shape)
        drawn = base * np.exp(spread * noise) if base else spread * noise
        out[name] = jnp.asarray(drawn.astype(out[name].dtype))
    for name, factor in factors.items():
        out[name] = (out[name] * factor).astype(out[name].dtype)
    return out
```

```python
import numpy as np
import concourse.bass as bass
from concourse import mybir
from concourse.alu_op_type import AluOpType as ALU
from contextlib import ExitStack

F32 = mybir.dt.float32
U8 = mybir.dt.uint8
I32 = mybir.dt.int32
ACT = mybir.ActivationFunctionType
AX = mybir.AxisListType

B, S, D, C, KEYS = 16, 56, 256, 128, 1500
PAD = 64
NT = B * PAD // 128
HEADS = 16
HQ = HEADS * S
RT = HQ // 128
KP, KT = 125, 12
CH = 3
CHK = KEYS // CH
DH = 64
INNER = HEADS * DH
FF = 4 * D
HD2, CHD = 16, 8
II = 688
IT = [(i, min(128, II - i)) for i in range(0, II, 128)]
VECTORS = [f"L{l}_{n}" for l in (1, 3) for n in ("ln_q_g", "ln_q_b", "ln_ff_g", "ln_ff_b")] + [
    "L2_ln_in_w", "L2_ln_post_attn_w", "L2_ln_post_cross_w"]
BIG = 3.3895313892515355e38
HALF = B // 2


class Tally:

    def __init__(self, handle):
        self.handle, self.count = handle, 0


class Point:

    def __init__(self, tally, value, loop=None):
        self.tally, self.value, self.loop = tally, value, loop


class Loop:
    def __init__(self, trips, tallies):
        self.trips, self.at_start, self.per = trips, {s: s.count for s in tallies}, {}

    def close(self):
        for s, c in self.at_start.items():
            self.per[s] = s.count - c
            s.count += (self.trips - 1) * self.per[s]


class Queue:

    def __init__(self, tally, step):
        self.step = step
        self.items, self.stack, self.tally, self.held, self.loop = [], [], tally, [], None
        self.last = None

    def do(self, fn, *waits, tally=None, by=1, quiet=False, apart=False):
        waits = self.held + list(waits)
        self.held = []
        s = None if quiet else (tally or self.tally)
        if s:
            s.count += by
        self.items.append((fn, [w for w in waits if w], s, by, apart))
        p = Point(s, s.count, self.loop) if s else None
        if p:
            self.last = p
        return p

    def wait(self, *points):
        self.held += list(points)


def emit(eng, items, step):

    def write(items, it, loop):
        waited = {}
        for item in items:
            if isinstance(item[0], Loop):
                with eng.Fori(0, item[0].trips) as i:
                    write(item[1], i, item[0])
                waited = {}
                continue
            fn, waits, s, by, apart = item
            need, on_register = {}, False
            for w in waits:
                per, value = 0, w.value
                if w.loop is not None:
                    per = w.loop.per[w.tally]
                    if w.loop is not loop:
                        value, per = value + (w.loop.trips - 1) * per, 0
                assert value > 0 or not per
                key = (w.tally, per)
                need[key] = max(need.get(key, 0), value)
            for (sig, per), value in need.items():
                if waited.get((sig, per), -1) >= value:
                    continue
                waited[(sig, per)] = value
                eng.wait_ge(sig.handle, it * per + value if per else value)
                on_register = on_register or (per and loop is not None)
            if on_register and apart:
                eng.sem_inc(step.handle, 1)
            if fn is None:
                continue
            ins = fn(eng, it)
            if s:
                ins.then_inc(s.handle, by)

    write(items, 0, None)


class Program:

    def __init__(self, nc, ctx):
        self.nc, self.ctx, self.tallies = nc, ctx, []
        self.pe, self.act, self.dve, self.pool, self.sp = (
            Queue(self.tally(n), self.tally(n + "_step")) for n in ("s_pe", "s_act", "s_dve", "s_pool", "s_sp"))
        self.queues = [self.pe, self.act, self.dve, self.pool, self.sp]
        self.psum = [ctx.enter_context(nc.psum_tensor(f"bank{i}", [128, 512], F32)) for i in range(8)]
        self.bank_free = [None] * 8
        self.next_bank = 0

    def tally(self, name):
        s = Tally(self.ctx.enter_context(self.nc.semaphore(name)))
        self.tallies.append(s)
        return s

    def sbuf(self, name, width, dt=F32):
        return self.ctx.enter_context(self.nc.sbuf_tensor(name, [128, width], dt))

    def join(self, *more):
        last = [q.last for q in self.queues[:4]]
        for q in self.queues[:4]:
            q.wait(*last, *more)
        return last

    def bank(self):
        i = self.next_bank
        self.next_bank = (i + 1) % 8
        return i, self.psum[i], self.bank_free[i]

    def open_loop(self, trips):
        loop = Loop(trips, self.tallies)
        for q in self.queues:
            q.stack.append(q.items)
            q.items, q.loop = [], loop
        return loop

    def close_loop(self, loop):
        loop.close()
        for q in self.queues:
            body, q.items = q.items, q.stack.pop()
            q.items.append((loop, body))
            q.loop = None


def view(ap, dims, **sizes):
    return ap.rearrange(dims, **sizes)


def build(nc, io, out):
    ctx = ExitStack()
    with ctx:
        p = Program(nc, ctx)
        pe, act, dve, pool, sp = p.queues

        X = p.sbuf("x_nat", NT * D)[:, :].rearrange("p (t d) -> p t d", t=NT)
        XT = p.sbuf("x_T", 4 * B * PAD)[:, :].rearrange("p (k n) -> p k n", k=4)
        QO_flat = p.sbuf("q_and_o", B * HQ)[:, :]
        QO = QO_flat.rearrange("p (b r) -> p b r", b=B)
        KTb = p.sbuf("ctx_T", 2 * KEYS)[:, :]
        KNb = p.sbuf("ctx_nat", 2 * KT * C)[:, :]
        QS = p.sbuf("q_stage", 2 * HQ)[:, :]
        MU = p.sbuf("mask_bytes", 2 * KEYS, U8)[:, :]
        A = p.sbuf("area", 12 * B * PAD)[:, :]
        W = p.sbuf("weights", 10240)[:, :]
        ident = p.sbuf("ident", 128)[:, :]
        vecs = p.sbuf("vectors", 32)[:, :]
        gates = p.sbuf("gates", 4)[:, :]
        mv = p.sbuf("stats", NT * 6)[:, :].rearrange("p (t s) -> p t s", t=NT)
        mean_var = p.sbuf("mean_var", NT * 2)[:, :].rearrange("p (t s) -> p t s", t=NT)
        st = p.sbuf("row_stats", 16 * NT)[:, :].rearrange("p (a t) -> p a t", t=NT)
        expert = p.sbuf("expert", 2 * NT)[:, :].rearrange("p (a t) -> p a t", t=NT)
        rope = p.sbuf("rope", 2 * HD2)[:, :]
        causal = p.sbuf("causal", S)[:, :]
        head8 = p.sbuf("head8", HEADS)[:, :]
        head16 = p.sbuf("head16", 8)[:, :]
        mx = p.sbuf("row_max", 2 * 8)[:, :].rearrange("p (a c) -> p a c", a=2)
        self_st = p.sbuf("self_stats", 3 * 16)[:, :].rearrange("p (k c) -> p k c", k=3)

        PT = [A[:, i * 3072:(i + 1) * 3072].rearrange("p (k c) -> p k c", k=KT) for i in range(2)]
        SB = [A[:, 6144 + i * KEYS:6144 + (i + 1) * KEYS] for i in range(2)]
        MB = [A[:, 9144 + i * KEYS:9144 + (i + 1) * KEYS] for i in range(2)]

        s_const = p.tally("s_const")
        s_w = {n: p.tally(f"s_w_{n}") for n in ("l0", "l0b", "l1a", "l1b", "l2a", "l2b", "l3a", "l3b")}
        s_out = p.tally("s_out")

        def load(dst, src, sig, *waits):
            return sp.do(lambda e, it: e.dma_start(dst, src), *waits, tally=sig, by=16)

        def vec(name, k):
            c = 2 * VECTORS.index(name) + k
            return vecs[:, c:c + 1]

        L0W = KTb
        w_mem = L0W[:, 0:2 * C].rearrange("p (k c) -> p k c", k=2)
        w_memT = L0W[:, 256:512]
        w_gateT = L0W[:, 512:1536].rearrange("p (k n) -> p k n", k=4)
        b_gate = L0W[:, 1536:1792]
        norm_w = L0W[:, 1792:2048]
        x0T = XT[:, 0:2, :].rearrange("p k (b q) -> p k b q", b=B)

        load(w_mem, io["W_mem"].rearrange("(k p) c -> p k c", p=128), s_w["l0"])
        load(XT[:, 0:2, :], io["xT"], s_w["l0"])
        load(ident, io["ident"], s_w["l0"])

        def gated_names(l):
            return {n: f"L{l}_{n}" for n in ("ln_q_g", "ln_q_b", "ln_ff_g", "ln_ff_b")}

        ctx_rows = io["ctx"].rearrange("b (p k) c -> b p (k c)", p=KP)

        def attention(tag, per_trip, units, groups, q_src, dest, kt_buf, kn_buf, scaled_mask,
                      copy_q, peel):
            nb, U, G = per_trip, len(units), len(groups)
            sp.wait(*[q.last for q in p.queues[:4]])
            trips = B // nb
            kt_sig = [p.tally(f"s_{tag}_kt{i}") for i in range(nb)]
            kn_sig = [p.tally(f"s_{tag}_kn{i}") for i in range(nb)]
            m_sig = [p.tally(f"s_{tag}_m{i}") for i in range(nb)] if scaled_mask else None
            s_q = p.tally(f"s_{tag}_q")
            s_mb = p.tally(f"s_{tag}_mb")
            s_sc = p.tally(f"s_{tag}_scores")
            s_mx = p.tally(f"s_{tag}_max")
            s_ex = p.tally(f"s_{tag}_exp")
            s_nm = p.tally(f"s_{tag}_norm")
            s_rc = p.tally(f"s_{tag}_recip")
            s_nx = p.tally(f"s_{tag}_negmax")
            s_tr = p.tally(f"s_{tag}_transposed")
            s_ea = p.tally(f"s_{tag}_evac_act")
            s_ed = p.tally(f"s_{tag}_evac_dve")
            s_pv = p.tally(f"s_{tag}_sums")
            s_ov = p.tally(f"s_{tag}_o_out")
            group_of, col_of = {}, {}
            for g, (us, _, _) in enumerate(groups):
                for n, u in enumerate(us):
                    group_of[u], col_of[u] = g, 128 * n
            last_unit = {b: max(u for u in range(U) for x in units[u] if x[2] == b) for b in range(nb)}
            first_unit = {b: min(u for u in range(U) for x in units[u] if x[2] == b) for b in range(nb)}
            last_group = {b: max(g for g in range(G) for x in groups[g][2] if x[0] == b)
                          for b in range(nb)}
            rows_free = {b: groups[last_group[b]][1][-1] - U for b in range(nb)}

            def trip(depth, drain, carried, loop, index):
                now, missed, first = {}, set(), depth == 0

                def at(name, i):
                    if (name, i) in now:
                        return now[(name, i)]
                    if (name, i) in carried:
                        c = carried[(name, i)]
                        return Point(c.tally, c.value, loop) if loop else c
                    missed.add((name, i))
                    return None

                def loads(b):
                    def batch(it):
                        return index(it) * nb + b

                    scores_done = at("scores", last_unit[b] - U)
                    now[("kt", b)] = sp.do(
                        lambda e, it: e.dma_start(
                            kt_buf(b), io["ctxT"][bass.ds(batch(it), 1)].rearrange("o c k -> (o c) k")),
                        scores_done, tally=kt_sig[b], by=16, apart=True)
                    if scaled_mask:
                        now[("mu", b)] = sp.do(
                            lambda e, it: e.dma_start(
                                MU[:, b * KEYS:(b + 1) * KEYS],
                                io["mask"][bass.ds(batch(it), 1), :].to_broadcast([128, KEYS])),
                            at("mb", b - nb), tally=m_sig[b], by=16, apart=True)

                def load_rows(b):
                    def batch(it):
                        return index(it) * nb + b

                    sums_done = at("sums", last_group[b] - G)
                    for lo, hi in ((0, 112), (112, KP)):
                        now[("kn", b)] = sp.do(
                            lambda e, it, lo=lo, hi=hi: e.dma_start(
                                kn_buf(b)[lo:hi, :],
                                ctx_rows[bass.ds(batch(it), 1), lo:hi, :]
                                .rearrange("o p n -> (o p) n")),
                            sums_done, tally=kn_sig[b], by=16, apart=True)

                def stage(b):
                    if copy_q is not None:
                        now[("q", b)] = pool.do(
                            lambda e, it: copy_q(e, b, index(it)),
                            at("scores", last_unit[b] - U), tally=s_q)
                    if scaled_mask:
                        now[("mb", b)] = pool.do(
                            lambda e, it: e.tensor_scalar(
                                MB[b], MU[:, b * KEYS:(b + 1) * KEYS], -1.0, BIG, ALU.add, ALU.mult),
                            at("mu", b), at("max", last_unit[b] - U), tally=s_mb, apart=True)

                def scores(u):
                    for c in range(CH):
                        for n, (row, m, b, q0) in enumerate(units[u]):
                            now[("scores", u)] = now[("scores%d" % c, u)] = pe.do(
                                lambda e, it, c=c, row=row, m=m, b=b, q0=q0: e.matmul(
                                    p.psum[c][row:row + m, 0:CHK], q_src(b)[:, q0:q0 + m],
                                    kt_buf(b)[:, c * CHK:(c + 1) * CHK], start=True, stop=True),
                                at("kt", b), at("q", b), at("max%d" % c, u - 1),
                                tally=s_sc)

                def maxima(u):
                    mb = MB[units[u][0][2]] if scaled_mask else MB[0]
                    for c in range(CH):
                        now[("max", u)] = now[("max%d" % c, u)] = dve.do(
                            lambda e, it, c=c: e.tensor_tensor_reduce(
                                out=SB[u % 2][:, c * CHK:(c + 1) * CHK], in0=p.psum[c][:, 0:CHK],
                                in1=mb[:, c * CHK:(c + 1) * CHK], scale=1.0, scalar=-BIG,
                                op0=ALU.add, op1=ALU.max, accum_out=mx[:, u % 2, c:c + 1]),
                            at("scores%d" % c, u), at("mb", units[u][0][2]),
                            at("transposed", u - 2), at("exp", u - 2), tally=s_mx, apart=True)
                    now[("negmax", u)] = dve.do(
                        lambda e, it: e.tensor_reduce(mx[:, u % 2, 3:4], mx[:, u % 2, 0:3], AX.X,
                                                      ALU.max, negate=True),
                        now[("max", u)], tally=s_nx)

                def exponentials(u):
                    now[("exp", u)] = act.do(
                        lambda e, it: e.activation(SB[u % 2], SB[u % 2], ACT.Exp,
                                                   bias=mx[:, u % 2, 3:4],
                                                   accum_out=mx[:, u % 2, 4:5]),
                        at("negmax", u), tally=s_ex)

                def normalise(u):
                    now[("recip", u)] = dve.do(
                        lambda e, it: e.reciprocal(mx[:, u % 2, 5:6], mx[:, u % 2, 4:5]),
                        at("exp", u), tally=s_rc)
                    now[("norm", u)] = dve.do(
                        lambda e, it: e.tensor_scalar(SB[u % 2], SB[u % 2], mx[:, u % 2, 5:6], None,
                                                      ALU.mult),
                        now[("recip", u)], tally=s_nm)

                def transposes(u):
                    for c in range(CH):
                        for k in range(4):
                            x = pe.do(
                                lambda e, it, c=c, k=k: e.transpose(
                                    p.psum[3 + c][0:KP, 128 * k:128 * k + 128],
                                    SB[u % 2][:, (4 * c + k) * KP:(4 * c + k + 1) * KP], ident),
                                at("norm", u), at("evac%d" % c, u - 1),
                                tally=s_tr, quiet=(k < 3))
                        now[("transposed", u)] = now[("transposed%d" % c, u)] = x

                def evacuate(u, c):
                    g = group_of[u % U]
                    gi = g if u >= 0 else g - G
                    dst = PT[g % 2][0:KP, 4 * c:4 * c + 4, col_of[u % U]:col_of[u % U] + 128]
                    src = p.psum[3 + c][0:KP, :].rearrange("p (k r) -> p k r", k=4)
                    if c < 2:
                        fn, q, s = (lambda e, it: e.copy(dst, src)), act, s_ea
                    else:
                        fn, q, s = (lambda e, it: e.tensor_copy(dst, src)), dve, s_ed
                    now[("evac%d" % c, u)] = q.do(fn, at("transposed%d" % c, u), at("sums", gi - 2),
                                                  tally=s)

                def sums(g, part, parts):
                    us, _, work = groups[g % G]
                    todo = [(k, w) for w in work for k in range(KT)]
                    n = len(todo)
                    for i in range(n * part // parts, n * (part + 1) // parts):
                        k, (b, c0, width, o0) = todo[i]
                        bi, ui = b + (g // G) * nb, us[-1] + (g // G) * U
                        x = pe.do(
                            lambda e, it, k=k, b=b, c0=c0, width=width, o0=o0: e.matmul(
                                p.psum[6 + g % 2][:, o0:o0 + width], kn_buf(b)[0:KP, k * C:(k + 1) * C],
                                PT[g % 2][0:KP, k, c0:c0 + width], start=(k == 0), stop=(k == KT - 1)),
                            at("kn", bi), at("evac0", ui), at("evac1", ui), at("evac2", ui),
                            at("o_out", g - 2), tally=s_pv, quiet=(i < n - 1))
                    if part == parts - 1:
                        now[("sums", g)] = x

                def o_out(g):
                    work = groups[g % G][2]
                    width = max(o0 + w for _, _, w, o0 in work)
                    back = -(g // G)
                    now[("o_out", g)] = dve.do(
                        lambda e, it: e.tensor_copy(dest(g % G, index(it) - back),
                                                    p.psum[6 + g % 2][:, 0:width]),
                        at("sums", g), tally=s_ov)

                def in_slot(s):
                    for g, (_, slots, _) in enumerate(groups):
                        for n, x in enumerate(slots):
                            for back in range(min(depth, 2) + 1):
                                if x == s + back * U:
                                    yield g - back * G, n, len(slots)

                def out_in_slot(s):
                    for g, (_, slots, _) in enumerate(groups):
                        for back in range(min(depth, 2) + 1):
                            if slots[-1] + 1 == s + back * U:
                                yield g - back * G

                slots_here = max(x[1][-1] for x in groups) + 2 - U if drain else U
                if not drain:
                    for b in range(nb):
                        loads(b)
                        if first or rows_free[b] < 0:
                            load_rows(b)
                for s in range(slots_here):
                    if not drain:
                        for b in range(nb):
                            if first_unit[b] == s:
                                stage(b)
                        scores(s)
                        maxima(s)
                        exponentials(s)
                    for g, part, parts in in_slot(s):
                        if g < 0 or not drain:
                            sums(g, part, parts)
                    for b in range(nb):
                        if not (first or drain) and rows_free[b] == s:
                            load_rows(b)
                    for g in out_in_slot(s):
                        if g < 0 or not drain:
                            o_out(g)
                    if not drain:
                        normalise(s)
                    if (s == 0 and not first) or (s > 0 and not drain):
                        transposes(s - 1)
                        for c in range(CH):
                            evacuate(s - 1, c)
                return now, missed

            def shifted(now):
                size = {"q": nb, "mb": nb, "kt": nb, "kn": nb, "mu": nb, "sums": G, "o_out": G}
                return {(n, i - size.get(n, U)): v for (n, i), v in now.items()}

            carried = {}
            for j in range(peel):
                before = carried
                now, _ = trip(j, False, carried, None, lambda it, j=j: j)
                carried = {**{(n, i - {"q": nb, "mb": nb, "kt": nb, "kn": nb, "mu": nb, "sums": G,
                                       "o_out": G}.get(n, U)): v for (n, i), v in before.items()},
                           **shifted(now)}
            loop = p.open_loop(trips - peel)
            now, missed = trip(peel, False, carried, loop, lambda it: it + peel)
            p.close_loop(loop)
            after = shifted(now)
            for key, point in after.items():
                assert key not in missed, key
                if key in carried:
                    assert point.value == carried[key].value + loop.per[point.tally], key
            trip(trips, True, after, None, lambda it: trips)
            p.join()

        turn = [0]

        def either(*engines):
            turn[0] += 1
            return (act, dve)[turn[0] % 2]

        def scale_out(dst, src, scale, *waits, q=None):
            q = q or either()
            if q is act:
                return act.do(lambda e, it: e.activation(dst, src, ACT.Copy, scale=scale), *waits)
            return dve.do(lambda e, it: e.tensor_scalar(dst, src, scale, None, ALU.mult), *waits)

        def product(steps, width, *waits, rows=128, row0=0, shape=None):
            i, bank, free = p.bank()
            for n, (lhsT, rhs) in enumerate(steps):
                o = bank[row0:row0 + rows, 0:width]
                x = pe.do(lambda e, it, lhsT=lhsT, rhs=rhs, o=o, n=n: e.matmul(
                    o, lhsT, rhs, start=(n == 0), stop=(n == len(steps) - 1)),
                    free, *waits, quiet=(n < len(steps) - 1))
            return i, bank, x

        def tokens(arr, k, half):
            return arr[:, k, :].rearrange("p (b q) -> p b q", b=B)[:, HALF * half:HALF * half + HALF, 0:S]

        def real(ap):
            return ap.rearrange("p (b q) -> p b q", q=S)

        def rstd(src, eps, scale, *waits):
            a = dve.do(lambda e, it: e.tensor_scalar(st[:, 0, :], src, scale, eps, ALU.mult, ALU.add),
                       *waits)
            r = act.do(lambda e, it: e.activation(st[:, 1, :], st[:, 0, :], ACT.Sqrt), a)
            return dve.do(lambda e, it: e.reciprocal(st[:, 2, :], st[:, 1, :]), r)

        XN = A[:, 8192:12288].rearrange("p (k t d) -> p k t d", k=2, t=NT)

        def transposed_norm(kind, g, bias, masked, *waits):
            if kind == "layer":
                done = None
                for t in range(NT):
                    a = dve.do(lambda e, it, t=t: e.bn_stats(mv[:, t, :], X[:, t, :]), *waits)
                    done = dve.do(lambda e, it, t=t: e.bn_aggr(mean_var[:, t, :], mv[:, t, :]), a)
                r = rstd(mean_var[:, :, 1], 1e-5, 1.0, done)
            else:
                for t in range(NT):
                    done = dve.do(lambda e, it, t=t: e.tensor_tensor_reduce(
                        out=XN[:, 1, t, :], in0=X[:, t, :], in1=X[:, t, :], scale=1.0, scalar=0.0,
                        op0=ALU.mult, op1=ALU.add, accum_out=st[:, 3, t:t + 1]), *waits)
                r = rstd(st[:, 3, :], 1e-6, 1.0 / D, done)
            if masked:
                for m in range(2):
                    r2 = dve.do(lambda e, it, m=m: e.tensor_tensor(
                        st[:, 4 + m, :], st[:, 2, :], expert[:, m, :], ALU.mult), r)
            n_k = 4 if masked else 2
            for m in range(2 if masked else 1):
                for t in range(NT):
                    if kind == "layer":
                        x = dve.do(lambda e, it, t=t: e.tensor_scalar(
                            XN[:, 0, t, :], X[:, t, :], mean_var[:, t, 0:1], st[:, 2, t:t + 1],
                            ALU.subtract, ALU.mult), r)
                    else:
                        s = (4 + m) if masked else 2
                        x = dve.do(lambda e, it, t=t, m=m, s=s: e.tensor_scalar(
                            XN[:, m, t, :], X[:, t, :], st[:, s, t:t + 1], None, ALU.mult),
                            r2 if masked else r)
            return transpose_in(n_k // 2, lambda k: vec(g, k), (lambda k: vec(bias, k)) if bias else None, x)

        def transpose_in(n_m, g, bias, x):
            outs = []
            for m in range(n_m):
                for k in range(2):
                    for h in range(2):
                        i, bank, free = p.bank()
                        for j in range(4):
                            y = pe.do(lambda e, it, m=m, k=k, h=h, j=j, bank=bank: e.transpose(
                                bank[:, 128 * j:128 * j + 128],
                                XN[:, m, 4 * h + j, 128 * k:128 * k + 128], ident), x, free,
                                quiet=(j < 3))
                        dst = XT[:, 2 * m + k, 512 * h:512 * h + 512]
                        if bias:
                            z = act.do(lambda e, it, dst=dst, bank=bank, k=k: e.activation(
                                dst, bank[:, :], ACT.Identity, scale=g(k), bias=bias(k)), y)
                        elif g:
                            z = dve.do(lambda e, it, dst=dst, bank=bank, k=k: e.tensor_scalar(
                                dst, bank[:, :], g(k), None, ALU.mult), y)
                        else:
                            z = dve.do(lambda e, it, dst=dst, bank=bank: e.tensor_copy(
                                dst, bank[:, :]), y)
                        p.bank_free[i] = z
                        outs.append(z)
            return outs

        def pads(arr, k):
            return pool.do(lambda e, it: e.memset(
                arr.rearrange("p (x q) -> p x q", q=PAD)[:, 0:k * B, S:PAD], 0.0))

        kt0 = [QO_flat[:, i * KEYS:(i + 1) * KEYS] for i in range(4)]
        kn0 = [QO_flat[:, 4 * KEYS + i * KT * C:4 * KEYS + (i + 1) * KT * C] for i in range(4)]
        at0 = 4 * KEYS + 4 * KT * C
        q0T = QO_flat[:, at0:at0 + B * PAD].rearrange("p (b q) -> p b q", b=B)
        mcT = QO_flat[:, at0 + B * PAD:at0 + 2 * B * PAD]

        zero_q = pool.do(lambda e, it: e.memset(q0T, 0.0))
        pool.do(lambda e, it: e.memset(MB[0], 0.0))
        w0 = Point(s_w["l0"], s_w["l0"].count)
        for half in range(2):
            i, bank, x = product([(w_mem[:, k, :], x0T[:, k, HALF * half:HALF * half + HALF, 0:S])
                                  for k in range(2)], HALF * S, w0)
            p.bank_free[i] = scale_out(q0T[:, HALF * half:HALF * half + HALF, 0:S],
                                       real(bank[:, 0:HALF * S]), 1.0 / 16.0, x, zero_q)
        p.join()

        QS0 = [QS[:, 0:4 * PAD], QS[:, 4 * PAD:8 * PAD]]

        def stage_q0(e, b, j):
            return e.tensor_copy(QS[:, b * PAD:(b + 1) * PAD],
                                 q0T[:, bass.ds(j * 4 + b, 1), :].rearrange("p o q -> p (o q)"))

        def dest0(g, j):
            return mcT.rearrange("p (t r) -> p t r", t=NT)[:, bass.ds(j * 2 + g, 1), :] \
                .rearrange("p o r -> p (o r)")

        attention("l0", 4, [[(0, PAD, 0, 0), (PAD, PAD, 1, 0)], [(0, PAD, 2, 0), (PAD, PAD, 3, 0)]],
                  [([0], [2], [(0, 0, PAD, 0), (1, PAD, PAD, PAD)]),
                   ([1], [3], [(2, 0, PAD, 0), (3, PAD, PAD, PAD)])],
                  lambda b: QS[:, b * PAD:(b + 1) * PAD], dest0,
                  lambda b: kt0[b], lambda b: kn0[b], False, stage_q0, 2)

        load(w_memT, io["W_memT"], s_w["l0b"])
        load(w_gateT, io["W_gateT"].rearrange("(k p) n -> p k n", p=128), s_w["l0b"])
        load(b_gate, io["b_gate"].to_broadcast([128, D]), s_w["l0b"])
        load(norm_w, io["norm_w"].to_broadcast([128, D]), s_w["l0b"])
        load(X, io["x"], s_w["l0b"])
        load(vecs[:, 0:2 * len(VECTORS)], io["vectors"], s_const)
        load(gates, io["gates"].to_broadcast([128, 4]), s_const)

        def w3(lo, k, n):
            return W[:, lo:lo + k * n].rearrange("p (k n) -> p k n", k=k)

        g_wq, g_wkT, g_wv = w3(0, 2, INNER), w3(2048, 8, C), W[:, 3072:4096]
        g_wo, g_w1, g_w2 = w3(4096, 8, D), w3(6144, 2, FF), w3(8192, 8, D)

        def load_gated_a(l, *waits):
            load(g_wq, io[f"L{l}_Wq"].rearrange("(k p) n -> p k n", p=128), s_w[f"l{l}a"], *waits)
            load(g_wkT, io[f"L{l}_WkT"].rearrange("(k p) n -> p k n", p=128), s_w[f"l{l}a"])

        def load_gated_b(l, *waits):
            b = s_w[f"l{l}b"]
            load(g_wv, io[f"L{l}_Wkv"][:, INNER:2 * INNER], b, *waits)
            load(g_wo, io[f"L{l}_Wo"].rearrange("(k p) n -> p k n", p=128), b)
            load(g_w1, io[f"L{l}_W1"].rearrange("(k p) n -> p k n", p=128), b)
            load(g_w2, io[f"L{l}_W2"].rearrange("(k p) n -> p k n", p=128), b)

        load_gated_a(1)
        w0 = Point(s_w["l0b"], s_w["l0b"].count)
        consts = Point(s_const, s_const.count)
        tanh_gates = act.do(lambda e, it: e.activation(gates, gates, ACT.Tanh), consts)

        mc_nat = A[:, 0:2048].rearrange("p (t d) -> p t d", t=NT)
        fused = A[:, 2048:4096].rearrange("p (t d) -> p t d", t=NT)
        junk = A[:, 4096:4352]
        for t in range(NT):
            i, bank, x = product([(mcT[:, 128 * t:128 * t + 128], w_memT)], D, w0)
            p.bank_free[i] = scale_out(mc_nat[:, t, :], bank[:, 0:D], 1.0, x, q=dve)
        for k in range(2):
            for h in range(2):
                i, bank, x = product([(w_memT[:, 128 * k:128 * k + 128], mcT[:, 512 * h:512 * h + 512])],
                                     512)
                p.bank_free[i] = mcTT = scale_out(XT[:, 2 + k, 512 * h:512 * h + 512], bank[:, :], 1.0, x,
                                                  q=act)
        for t in range(NT):
            i, bank, x = product([(XT[:, k, 128 * t:128 * t + 128], w_gateT[:, k, :])
                                  for k in range(4)], D, mcTT)
            a = dve.do(lambda e, it, t=t, bank=bank: e.tensor_tensor(
                fused[:, t, :], bank[:, 0:D], b_gate, ALU.add), x)
            p.bank_free[i] = a
            g = act.do(lambda e, it, t=t: e.activation(fused[:, t, :], fused[:, t, :], ACT.Sigmoid), a)
            m = pool.do(lambda e, it, t=t: e.tensor_tensor(
                fused[:, t, :], fused[:, t, :], mc_nat[:, t, :], ALU.mult), g, dve.last)
            m = pool.do(lambda e, it, t=t: e.tensor_tensor(
                fused[:, t, :], fused[:, t, :], X[:, t, :], ALU.add), m, w0)
        for t in range(NT):
            ss = dve.do(lambda e, it, t=t: e.tensor_tensor_reduce(
                out=junk, in0=fused[:, t, :], in1=fused[:, t, :], scale=1.0, scalar=0.0,
                op0=ALU.mult, op1=ALU.add, accum_out=st[:, 3, t:t + 1]), m, dve.last)
        r = rstd(st[:, 3, :], 1e-6, 1.0 / D, ss)
        for t in range(NT):
            dve.do(lambda e, it, t=t: e.scalar_tensor_tensor(
                X[:, t, :], fused[:, t, :], st[:, 2, t:t + 1], norm_w, ALU.mult, ALU.mult), r)
        p.join()

        ring = [KNb[:, i * KT * C:(i + 1) * KT * C] for i in range(2)]
        kring = [KTb[:, i * KEYS:(i + 1) * KEYS] for i in range(2)]
        tiles = [[(0, 128, b, 128 * t)] for b in range(2) for t in range(RT)]
        sets, slot = [], 3
        for b in range(2):
            for us in ((0, 1), (2, 3), (4, 5), (6,)):
                sets.append(([b * RT + u for u in us], list(range(slot, slot + len(us))),
                             [(b, 0, 128 * len(us), 0)]))
                slot += len(us)

        def stage_q(e, b, j):
            return e.tensor_copy(QS[:, b * HQ:(b + 1) * HQ],
                                 QO[:, bass.ds(j * 2 + b, 1), :].rearrange("p o r -> p (o r)"))

        def dest(g, j):
            us = sets[g][0]
            lo = 128 * (us[0] % RT)
            return QO[:, bass.ds(j * 2 + us[0] // RT, 1), lo:lo + 128 * len(us)] \
                .rearrange("p o r -> p (o r)")

        def cross_attention(tag, masked):
            attention(tag, 2, tiles, sets, lambda b: QS[:, b * HQ:(b + 1) * HQ], dest,
                      lambda b: kring[b], lambda b: ring[b], masked, stage_q, 1)

        def residual(t, bank, x, gate):
            if gate is None:
                return dve.do(lambda e, it: e.tensor_tensor(X[:, t, :], bank[:, 0:D], X[:, t, :],
                                                            ALU.add), x)
            return dve.do(lambda e, it: e.scalar_tensor_tensor(
                X[:, t, :], bank[:, 0:D], gates[:, gate:gate + 1], X[:, t, :], ALU.mult, ALU.add), x)

        def head_queries(q_dst, half, h):
            return QO[:, HALF * half:HALF * half + HALF, S * h:S * h + S]

        def gated_block(l):
            wa = Point(s_w[f"l{l}a"], s_w[f"l{l}a"].count)
            n = gated_names(l)
            xs = transposed_norm("layer", n["ln_q_g"], n["ln_q_b"], False)
            qT = A[:, 0:8 * B * S].rearrange("p (j n) -> p j n", j=8)
            for j in range(8):
                for half in range(2):
                    i, bank, x = product([(g_wq[:, k, 128 * j:128 * j + 128], tokens(XT, k, half))
                                          for k in range(2)], HALF * S, wa, *xs)
                    p.bank_free[i] = qt = scale_out(
                        qT[:, j, HALF * S * half:HALF * S * (half + 1)], bank[:, 0:HALF * S],
                        DH ** -0.5, x)
                both = [act.last, dve.last]
                for half in range(2):
                    for hh in range(2):
                        i, bank, x = product(
                            [(g_wkT[64 * hh:64 * hh + 64, j, :],
                              qT[64 * hh:64 * hh + 64, j, HALF * S * half:HALF * S * (half + 1)])],
                            HALF * S, *both)
                        p.bank_free[i] = scale_out(head_queries(QO, half, 2 * j + hh),
                                                   real(bank[:, 0:HALF * S]), 1.0, x)
            p.join()
            cross_attention(f"l{l}", True)
            load_gated_b(l)
            wb = Point(s_w[f"l{l}b"], s_w[f"l{l}b"].count)

            aoT = A[:, 0:8 * B * PAD].rearrange("p (j n) -> p j n", j=8)
            z = pads(A, 8)
            for j in range(8):
                for half in range(2):
                    i, bank, free = p.bank()
                    for hh in range(2):
                        h = 2 * j + hh
                        x = pe.do(lambda e, it, h=h, hh=hh, half=half, bank=bank: e.matmul(
                            bank[64 * hh:64 * hh + 64, 0:HALF * S], g_wv[:, DH * h:DH * h + DH],
                            head_queries(QO, half, h), start=True, stop=True), free, wb)
                    p.bank_free[i] = scale_out(tokens(aoT, j, half), real(bank[:, 0:HALF * S]), 1.0, x)
            both = [act.last, dve.last, z]
            for t in range(NT):
                i, bank, x = product([(aoT[:, j, 128 * t:128 * t + 128], g_wo[:, j, :])
                                      for j in range(8)], D, *both)
                p.bank_free[i] = residual(t, bank, x, l - 1)
            xs = transposed_norm("layer", n["ln_ff_g"], n["ln_ff_b"], False, dve.last)
            pe_before = pe.last
            for j in range(8):
                for half in range(2):
                    i, bank, x = product([(g_w1[:, k, 128 * j:128 * j + 128], tokens(XT, k, half))
                                          for k in range(2)], HALF * S, *xs)
                    p.bank_free[i] = act.do(lambda e, it, j=j, half=half, bank=bank: e.activation(
                        tokens(aoT, j, half), real(bank[:, 0:HALF * S]), ACT.Gelu), x, pe_before)
            for t in range(NT):
                i, bank, x = product([(aoT[:, j, 128 * t:128 * t + 128], g_w2[:, j, :])
                                      for j in range(8)], D, act.last, z)
                p.bank_free[i] = residual(t, bank, x, l)
            p.join()

        gated_block(1)

        wqkv, wden = w3(0, 4, 3 * D), w3(3072, 4, D)
        wcq, wckT, wcv, wcd = w3(8960, 2, C), W[:, 9216:9344], W[:, 9344:9472], W[:, 9472:9728]
        wgu = W[:, 0:8 * II].rearrange("p (x n) -> p x n", x=8)
        wdown = w3(8 * II, 12, D)
        free = [q.last for q in p.queues[:4]]
        for m, e in enumerate("vl"):
            load(wqkv[:, 2 * m:2 * m + 2, :], io[f"L2_{e}_qkv"].rearrange("(k p) n -> p k n", p=128),
                 s_w["l2a"], *free)
            load(wden[:, 2 * m:2 * m + 2, :], io[f"L2_{e}_dense"].rearrange("(k p) n -> p k n", p=128),
                 s_w["l2a"])
        load(wcq, io["L2_cq_w"].rearrange("(k p) n -> p k n", p=128), s_w["l2a"])
        load(wckT, io["L2_ckT"], s_w["l2a"])
        load(wcv, io["L2_ckv_w"][:, C:2 * C], s_w["l2a"])
        load(wcd, io["L2_cdense_w"], s_w["l2a"])

        types = A[:, 0:2 * NT].bitcast(I32).rearrange("p (a t) -> p a t", a=2)
        s_ty = p.tally("s_types")
        load(types, io["types"], s_ty, *free)
        pos = A[:, 64:64 + S].bitcast(I32)
        posf, onehot = A[:, 128:128 + S], A[:, 256:256 + 128]
        table, tidx = A[:, 448:448 + 2 * HD2], A[:, 512:513]
        load(pos[0:S, :], io["pos"].to_broadcast([S, S]), s_ty)
        load(table[0:S, :], io["rope"], s_ty)
        load(tidx[0:S, :], io["index"], s_ty)
        load(head16, io["head16"], s_ty)
        load(head8, io["head8"], s_ty)
        load(causal, io["causal"], s_ty)
        ty = Point(s_ty, s_ty.count)
        a = dve.do(lambda e, it: e.tensor_scalar(st[:, 6:8, :], types, 1.0, None,
                                                 ALU.is_equal), ty)
        a = dve.do(lambda e, it: e.tensor_tensor(expert[:, 0, :], st[:, 6, :], st[:, 7, :], ALU.mult), a)
        a = dve.do(lambda e, it: e.tensor_scalar(expert[:, 1, :], expert[:, 0, :], -1.0, 1.0,
                                                 ALU.mult, ALU.add), a)
        zo = dve.do(lambda e, it: e.memset(onehot[0:S, :], 0.0))
        b_ = dve.do(lambda e, it: e.tensor_scalar(posf[0:S, :], pos[0:S, :], 0.0, float(S - 1),
                                                  ALU.max, ALU.min), ty)
        oh = onehot[0:S, :].rearrange("p (a q) -> p a q", a=2)
        for par in range(2):
            b2 = dve.do(lambda e, it, par=par: e.tensor_scalar(
                oh[:, par, 0:S], posf[0:S, :], tidx[0:S, 0:1], None, ALU.is_equal), zo, b_)
        i, bank, x = product([(onehot[0:S, :], table[0:S, :])], 2 * HD2, b2)
        p.bank_free[i] = rp = dve.do(lambda e, it, bank=bank: e.tensor_copy(rope,
                                                                            bank[:, 0:2 * HD2]), x)
        cosb = rope[:, 0:HD2]
        sinb = rope[:, HD2:2 * HD2]

        QKT = QO_flat[:, 0:4096].rearrange("p (k n) -> p k n", k=4)
        V = QO_flat[:, 4096:6144].rearrange("p (t d) -> p t d", t=NT)
        QB = QO_flat[:, 6144:8192].rearrange("p (b k h q) -> p b k h q", b=2, k=2, h=8)
        SS = QO_flat[:, 8192:9216].rearrange("p (j b q) -> p j b q", j=8, b=2)
        ST = QO_flat[:, 9216:10240].rearrange("p (j r) -> p j r", j=8)
        VS = QO_flat[:, 10240:10496]
        pool.do(lambda e, it: e.memset(SS, 0.0))
        p.join()
        xs = transposed_norm("rms", "L2_ln_in_w", None, True)
        w2a = Point(s_w["l2a"], s_w["l2a"].count)
        rotA = [A[:, i * 512:(i + 1) * 512] for i in range(2)]
        rotB = [A[:, 1024 + i * 512:1024 + (i + 1) * 512] for i in range(2)]
        before = [pe.last, dve.last, pool.last]
        transposes_done = {}
        for t in range(NT):
            i, bank, x = product([(XT[:, k, 128 * t:128 * t + 128], wqkv[:, k, 0:2 * D])
                                  for k in range(4)], 2 * D, w2a, *xs)
            i2, bank2, x2 = product([(XT[:, k, 128 * t:128 * t + 128], wqkv[:, k, 2 * D:3 * D])
                                     for k in range(4)], D)
            p.bank_free[i2] = scale_out(V[:, t, :], bank2[:, 0:D], 1.0, x2, q=act)
            a_, b_ = rotA[t % 2], rotB[t % 2]
            old = transposes_done.get(t - 2)
            qk = bank[:, :].rearrange("p (h c) -> p h c", c=HD2)
            cb = cosb.rearrange("p (o c) -> p o c", o=1).to_broadcast([128, 32, HD2])
            c1 = dve.do(lambda e, it, a_=a_, qk=qk, cb=cb: e.tensor_tensor(
                a_.rearrange("p (h c) -> p h c", c=HD2), qk, cb, ALU.mult), x, rp, old, *before)
            for d in range(2):
                sb_ = sinb[:, 8 * d:8 * d + 8].rearrange("p (o c) -> p o c", o=1) \
                    .to_broadcast([128, 32, 8])
                c2 = dve.do(lambda e, it, b_=b_, qk=qk, d=d, sb_=sb_: e.tensor_tensor(
                    b_.rearrange("p (h c) -> p h c", c=HD2)[:, :, 8 * d:8 * d + 8],
                    qk[:, :, 8 - 8 * d:16 - 8 * d], sb_, ALU.mult), x)
            p.bank_free[i] = c2
            c3 = pool.do(lambda e, it, a_=a_, b_=b_: e.tensor_tensor(a_, a_, b_, ALU.add), c1, c2)
            i3, bank3, free3 = p.bank()
            for k in range(4):
                y = pe.do(lambda e, it, k=k, a_=a_, bank3=bank3: e.transpose(
                    bank3[:, 128 * k:128 * k + 128], a_[:, 128 * k:128 * k + 128], ident), c3, free3)
            transposes_done[t] = y
            p.bank_free[i3] = scale_out(
                QKT[:, :, 128 * t:128 * t + 128], bank3[:, :].rearrange("p (k n) -> p k n", k=4),
                1.0, y, q=act)
        p.join()

        s_st, s_sc, s_sm, s_se, s_tp, s_cp, s_cx, s_out2 = (p.tally(f"s_self_{n}") for n in (
            "staged", "scores", "softmax", "exp", "transposed", "copied", "sums", "out"))
        CN = A[:, 4096:6144].rearrange("p (t d) -> p t d", t=NT)

        def pair_attention(pair, before_trip):
            for b in range(2):
                for k in range(2):
                    staged = pool.do(lambda e, it, b=b, k=k: e.tensor_tensor(
                        QB[:, b, k], QKT[:, k, bass.ds(pair(it) * 128 + b * 64, 64)]
                        .rearrange("p (o q) -> p o q", o=1).to_broadcast([128, 8, PAD]),
                        head16.rearrange("p (h o) -> p h o", o=1).to_broadcast([128, 8, PAD]),
                        ALU.mult), before_trip(s_sc), tally=s_st)
            staged = pool.do(lambda e, it: e.tensor_copy(
                VS, V[:, bass.ds(pair(it), 1), :].rearrange("p o d -> p (o d)")), before_trip(s_cx), tally=s_st)
            for b in range(2):
                for j in range(8):
                    x = pe.do(lambda e, it, b=b, j=j: e.matmul(
                        p.psum[b][:, 64 * j:64 * j + S],
                        QB[:, b, j // 4, 2 * (j % 4):2 * (j % 4) + 2, :].rearrange("p h q -> p (h q)"),
                        QKT[:, 2 + j // 4, bass.ds(pair(it) * 128 + b * 64, S)], start=True, stop=True),
                        staged, before_trip(s_sm), tally=s_sc)
            for b in range(2):
                d = dve.do(lambda e, it, b=b: e.tensor_tensor(
                    SS[:, :, b, 0:S], p.psum[b][:, :].rearrange("p (j q) -> p j q", j=8)[:, :, 0:S],
                    causal.rearrange("p (o q) -> p o q", o=1).to_broadcast([128, 8, S]), ALU.add),
                    x, before_trip(s_tp), tally=s_sm)
            m_, z_, r_ = (self_st[:, n, :].rearrange("p (j b) -> p j b", j=8) for n in range(3))
            d = dve.do(lambda e, it: e.tensor_reduce(m_, SS[:, :, :, 0:S], AX.X, ALU.max), d, tally=s_sm)
            for b in range(2):
                d2 = dve.do(lambda e, it, b=b: e.tensor_tensor(
                    SS[:, :, b, 0:S], SS[:, :, b, 0:S], m_[:, :, b:b + 1].to_broadcast([128, 8, S]),
                    ALU.subtract), d, tally=s_sm)
            for b in range(2):
                ex = act.do(lambda e, it, b=b: e.activation(SS[:, :, b, 0:S], SS[:, :, b, 0:S], ACT.Exp),
                            d2, tally=s_se)
            d = dve.do(lambda e, it: e.tensor_reduce(z_, SS[:, :, :, 0:S], AX.X, ALU.add), ex, tally=s_sm)
            d = dve.do(lambda e, it: e.reciprocal(self_st[:, 2, :], self_st[:, 1, :]), d, tally=s_sm)
            for b in range(2):
                d2 = dve.do(lambda e, it, b=b: e.tensor_tensor(
                    SS[:, :, b, 0:S], SS[:, :, b, 0:S], r_[:, :, b:b + 1].to_broadcast([128, 8, S]),
                    ALU.mult), d, tally=s_sm)
            for j in range(8):
                y = pe.do(lambda e, it, j=j: e.transpose(
                    p.psum[2 + j // 4][:, 128 * (j % 4):128 * (j % 4) + 128],
                    SS[:, j].rearrange("p b q -> p (b q)"), ident), d2, before_trip(s_cp), tally=s_tp)
            for n in range(2):
                c = act.do(lambda e, it, n=n: e.copy(
                    ST[:, 4 * n:4 * n + 4, :], p.psum[2 + n][:, :].rearrange("p (j r) -> p j r", j=4)),
                    y, before_trip(s_cx), tally=s_cp)
            for b in range(2):
                for h in range(HEADS):
                    x = pe.do(lambda e, it, b=b, h=h: e.matmul(
                        p.psum[4 + b][64 * b:64 * b + 64, HD2 * h:HD2 * h + HD2],
                        ST[64 * b:64 * b + S, h // 2, 64 * (h % 2):64 * (h % 2) + 64],
                        VS[64 * b:64 * b + S, HD2 * h:HD2 * h + HD2], start=True, stop=True),
                        c, before_trip(s_out2), tally=s_cx, apart=True)
            for b in range(2):
                act.do(lambda e, it, b=b: e.copy(
                    CN[64 * b:64 * b + 64, bass.ds(pair(it), 1), :].rearrange("p o d -> p (o d)"),
                    p.psum[4 + b][64 * b:64 * b + 64, 0:D]), x, tally=s_out2)

        pair_attention(lambda it: 0, lambda sig: None)
        loop = p.open_loop(NT - 1)
        pair_attention(lambda it: it + 1, lambda sig: Point(sig, loop.at_start[sig], loop))
        p.close_loop(loop)
        p.join()

        for m in range(2):
            for t in range(NT):
                x = dve.do(lambda e, it, m=m, t=t: e.tensor_scalar(
                    XN[:, m, t, :], CN[:, t, :], expert[:, m, t:t + 1], None, ALU.mult))
        xs = transpose_in(2, None, None, x)
        for t in range(NT):
            i, bank, x = product([(XT[:, k, 128 * t:128 * t + 128], wden[:, k, :])
                                  for k in range(4)], D, *xs)
            p.bank_free[i] = residual(t, bank, x, None)
        xs = transposed_norm("rms", "L2_ln_post_cross_w", None, False, dve.last)
        cqT = A[:, 0:B * S]
        WM = A[:, 1024:3072].rearrange("p (h c) -> p h c", h=HEADS)
        wm = dve.do(lambda e, it: e.tensor_tensor(
            WM, wckT.rearrange("p (o c) -> p o c", o=1).to_broadcast([128, HEADS, C]),
            head8.rearrange("p (h o) -> p h o", o=1).to_broadcast([128, HEADS, C]), ALU.mult))
        for half in range(2):
            i, bank, x = product([(wcq[:, k, :], tokens(XT, k, half)) for k in range(2)], HALF * S, *xs)
            p.bank_free[i] = cq = scale_out(cqT[:, HALF * S * half:HALF * S * (half + 1)],
                                            bank[:, 0:HALF * S], CHD ** -0.5, x, q=dve)
        for h in range(HEADS):
            for half in range(2):
                i, bank, x = product([(WM[:, h, :], cqT[:, HALF * S * half:HALF * S * (half + 1)])],
                                     HALF * S, cq, wm)
                p.bank_free[i] = scale_out(head_queries(QO, half, h), real(bank[:, 0:HALF * S]), 1.0, x)
        p.join()
        z = pool.do(lambda e, it: e.memset(MB[0], 0.0))
        p.join()
        cross_attention("l2", False)
        free = [q.last for q in p.queues[:4]]
        for m, e in enumerate("vl"):
            for g, n in enumerate(("gate", "up")):
                at_ = 4 * m + 2 * g
                load(wgu[:, at_:at_ + 2, :], io[f"L2_{e}_{n}"].rearrange("(k p) n -> p k n", p=128),
                     s_w["l2b"])
            load(wdown[:, 6 * m:6 * m + 5, :],
                 io[f"L2_{e}_down"][0:640, :].rearrange("(k p) n -> p k n", p=128), s_w["l2b"])
            load(wdown[0:II - 640, 6 * m + 5, :], io[f"L2_{e}_down"][640:II, :], s_w["l2b"])
        w2b = Point(s_w["l2b"], s_w["l2b"].count)
        flat = A[:, 0:HEADS * (C + CHD)]
        CV = A[:, 0:HEADS * C].rearrange("p (h c) -> p h c", h=HEADS)
        z = pool.do(lambda e, it: e.memset(flat, 0.0))
        z = pool.do(lambda e, it: e.tensor_copy(
            flat.rearrange("p (h x) -> p h x", h=HEADS)[:, :, 0:CHD],
            wcv.rearrange("p (h x) -> p h x", h=HEADS)), z)
        cxT = A[:, 3072:3072 + B * PAD].rearrange("p (k n) -> p k n", k=1)
        zp = pool.do(lambda e, it: e.memset(
            A[:, 3072:3072 + B * PAD].rearrange("p (x q) -> p x q", q=PAD)[:, :, S:PAD], 0.0))
        for half in range(2):
            i, bank, x = product([(CV[:, h, :], head_queries(QO, half, h)) for h in range(HEADS)],
                                 HALF * S, z)
            p.bank_free[i] = cx = scale_out(tokens(cxT, 0, half), real(bank[:, 0:HALF * S]), 1.0, x,
                                            q=act)
        for t in range(NT):
            i, bank, x = product([(cxT[:, 0, 128 * t:128 * t + 128], wcd)], D, cx, zp)
            p.bank_free[i] = residual(t, bank, x, None)
        xs = transposed_norm("rms", "L2_ln_post_attn_w", None, True, dve.last)
        p.join()
        HT = A.rearrange("p (x n) -> p x n", x=12)
        z = pads(A, 12)
        for m in range(2):
            for n, (i0, rows) in enumerate(IT):
                for half in range(2):
                    dst = tokens(HT[0:rows], 6 * m + n, half)
                    i, bank, x = product([(wgu[:, 4 * m + k, i0:i0 + rows], tokens(XT, 2 * m + k, half))
                                          for k in range(2)], HALF * S, w2b, *xs, rows=rows)
                    p.bank_free[i] = g = act.do(lambda e, it, dst=dst, bank=bank, rows=rows: e.activation(
                        dst, real(bank[0:rows, 0:HALF * S]), ACT.Silu), x)
                    i, bank, x = product([(wgu[:, 4 * m + 2 + k, i0:i0 + rows],
                                           tokens(XT, 2 * m + k, half))
                                          for k in range(2)], HALF * S, rows=rows)
                    p.bank_free[i] = u = dve.do(lambda e, it, dst=dst, bank=bank, rows=rows: e.tensor_tensor(
                        dst, real(bank[0:rows, 0:HALF * S]), dst, ALU.mult), x, g)
        for t in range(NT):
            i, bank, x = product([(HT[0:rows, 6 * m + n, 128 * t:128 * t + 128],
                                   wdown[0:rows, 6 * m + n, :])
                                  for m in range(2) for n, (_, rows) in enumerate(IT)], D, u, z)
            p.bank_free[i] = residual(t, bank, x, None)
        p.join()

        load_gated_a(3, *[q.last for q in p.queues[:4]])
        gated_block(3)
        for par in range(2):
            done = load(out[par], X[64 * par:64 * par + S, :, :], s_out, dve.last)
        sp.do(None, done, quiet=True)

        with nc.Block() as block:
            for name, q in (("sync", sp), ("gpsimd", pool), ("scalar", act), ("tensor", pe),
                            ("vector", dve)):
                def run(eng, q=q):
                    emit(eng, q.items, q.step)
                {"sync": block.sync, "gpsimd": block.gpsimd, "scalar": block.scalar,
                 "tensor": block.tensor, "vector": block.vector}[name](run)


def natural(a):
    z = np.zeros((B, PAD) + a.shape[2:], a.dtype)
    z[:, :S] = a
    return np.ascontiguousarray(z.reshape(NT, 128, *a.shape[2:]).swapaxes(0, 1))


def kernel(**inputs):
    import concourse.bacc as bacc
    from concourse.bass_utils import run_bass_kernel_spmd

    g = {n: np.asarray(v) for n, v in inputs.items()}
    key_order = np.arange(KEYS).reshape(KP, KT).T.reshape(-1)
    pad_T = np.zeros((D, B, PAD), np.float32)
    pad_T[:, :, :S] = g["x"].transpose(2, 0, 1)
    types = np.zeros((B, 2, PAD), np.int32)
    types[:, 0, :S] = g["mask_BxS_ik0"]
    types[:, 1, :S - 1] = g["mask_BxS_ik0"][:, 1:]
    types[:, 0, S - 1] = 0
    angle = np.outer(np.arange(S, dtype=np.float32),
                     (1.0 / 10000.0 ** (np.arange(0, HD2, 2, dtype=np.float32) / HD2)).astype(np.float32))
    part = np.arange(128)
    a = {
        "x": natural(g["x"]),
        "xT": np.ascontiguousarray(pad_T.reshape(2, 128, B * PAD).swapaxes(0, 1)),
        "ctx": g["ctx_1024"],
        "ctxT": np.ascontiguousarray(g["ctx_1024"][:, key_order].transpose(0, 2, 1)),
        "mask": np.ascontiguousarray(g["mask_BxS2_bk0"][:, key_order]),
        "types": np.ascontiguousarray(types.reshape(NT, 2, 2, PAD).transpose(1, 3, 2, 0).reshape(128, 2, NT)),
        "pos": g["pos_1xS"],
        "W_mem": g["L0_xattn_W_mem"], "W_memT": np.ascontiguousarray(g["L0_xattn_W_mem"].T),
        "W_gateT": np.ascontiguousarray(g["L0_xattn_W_gate"].T),
        "b_gate": g["L0_xattn_b_gate"].reshape(1, D), "norm_w": g["L0_xattn_norm_w"].reshape(1, D),
        "vectors": np.ascontiguousarray(np.concatenate(
            [g[n.replace("_", "_xattn_", 1)].reshape(2, 128).T for n in VECTORS], axis=1)),
        "gates": np.concatenate([g[f"L{l}_xattn_{n}_gate"] for l in (1, 3) for n in ("attn", "ff")])
                   .reshape(1, 4),
        "ident": np.eye(128, dtype=np.float32),
        "rope": np.concatenate([np.cos(angle), np.cos(angle), -np.sin(angle), np.sin(angle)],
                               axis=1).astype(np.float32),
        "index": np.arange(S, dtype=np.float32).reshape(S, 1),
        "head16": ((part[:, None] // HD2 == np.arange(8)) * HD2 ** -0.5).astype(np.float32),
        "head8": (part[:, None] // CHD == np.arange(HEADS)).astype(np.float32),
        "causal": np.where(np.arange(S) <= part[:, None] % PAD, 0.0, -BIG).astype(np.float32),
        "L2_ckT": np.ascontiguousarray(g["L2_xattn_ckv_w"][:, :C].T),
    }
    for l in (1, 3):
        for n in ("Wq", "Wkv", "Wo", "W1", "W2"):
            a[f"L{l}_{n}"] = g[f"L{l}_xattn_{n}"]
        a[f"L{l}_WkT"] = np.ascontiguousarray(g[f"L{l}_xattn_Wkv"][:, :INNER].T)
    for n in ("v_qkv", "l_qkv", "v_dense", "l_dense", "cq_w", "ckv_w", "cdense_w", "v_gate", "v_up",
              "v_down", "l_gate", "l_up", "l_down"):
        a[f"L2_{n}"] = g[f"L2_xattn_{n}"]

    nc = bacc.Bacc("TRN2", target_bir_lowering=False, num_devices=1)
    io = {n: nc.dram_tensor(f"in_{n}", v.shape, mybir.dt.from_np(v.dtype), kind="ExternalInput").ap()
          for n, v in a.items()}
    out = nc.dram_tensor("out", (2, S, NT, D), F32, kind="ExternalOutput").ap()
    build(nc, io, out)
    r = run_bass_kernel_spmd(nc, [{f"in_{n}": v for n, v in a.items()}], core_ids=[0])
    o = r.results[0]["out"]
    return np.ascontiguousarray(o.transpose(2, 0, 1, 3).reshape(B, S, D))
```

```python
import numpy as np
import concourse.bass as bass
from concourse import mybir
from concourse.alu_op_type import AluOpType as ALU
from contextlib import ExitStack

F32 = mybir.dt.float32
F32R = mybir.dt.float32r
BF16 = mybir.dt.bfloat16
U8 = mybir.dt.uint8
I32 = mybir.dt.int32
ACT = mybir.ActivationFunctionType
AX = mybir.AxisListType

B, S, D, C, KEYS = 16, 56, 256, 128, 1500
PAD = 64
NT = B * PAD // 128
HEADS = 16
HQ = HEADS * S
RT = HQ // 128
KP, KT = 125, 12
CH = 3
CHK = KEYS // CH
DH = 64
INNER = HEADS * DH
FF = 4 * D
HD2, CHD = 16, 8
II = 688
IT = [(i, min(128, II - i)) for i in range(0, II, 128)]
VECTORS = [f"L{l}_{n}" for l in (1, 3) for n in ("ln_q_g", "ln_q_b", "ln_ff_g", "ln_ff_b")] + [
    "L2_ln_in_w", "L2_ln_post_attn_w", "L2_ln_post_cross_w"]
BIG = 3.3895313892515355e38
HALF = B // 2


class Tally:

    def __init__(self, handle):
        self.handle, self.count = handle, 0


class Point:

    def __init__(self, tally, value, loop=None):
        self.tally, self.value, self.loop = tally, value, loop


class Loop:
    def __init__(self, trips, tallies):
        self.trips, self.at_start, self.per = trips, {s: s.count for s in tallies}, {}

    def close(self):
        for s, c in self.at_start.items():
            self.per[s] = s.count - c
            s.count += (self.trips - 1) * self.per[s]


class Queue:

    def __init__(self, tally, step):
        self.step = step
        self.items, self.stack, self.tally, self.held, self.loop = [], [], tally, [], None
        self.last = None

    def do(self, fn, *waits, tally=None, by=1, quiet=False, apart=False):
        waits = self.held + list(waits)
        self.held = []
        s = None if quiet else (tally or self.tally)
        if s:
            s.count += by
        self.items.append((fn, [w for w in waits if w], s, by, apart))
        p = Point(s, s.count, self.loop) if s else None
        if p:
            self.last = p
        return p

    def wait(self, *points):
        self.held += list(points)


def emit(eng, items, step):

    def write(items, it, loop):
        waited = {}
        for item in items:
            if isinstance(item[0], Loop):
                with eng.Fori(0, item[0].trips) as i:
                    write(item[1], i, item[0])
                waited = {}
                continue
            fn, waits, s, by, apart = item
            need, on_register = {}, False
            for w in waits:
                per, value = 0, w.value
                if w.loop is not None:
                    per = w.loop.per[w.tally]
                    if w.loop is not loop:
                        value, per = value + (w.loop.trips - 1) * per, 0
                assert value > 0 or not per
                key = (w.tally, per)
                need[key] = max(need.get(key, 0), value)
            for (sig, per), value in need.items():
                if waited.get((sig, per), -1) >= value:
                    continue
                waited[(sig, per)] = value
                eng.wait_ge(sig.handle, it * per + value if per else value)
                on_register = on_register or (per and loop is not None)
            if on_register and apart:
                eng.sem_inc(step.handle, 1)
            if fn is None:
                continue
            ins = fn(eng, it)
            if s:
                ins.then_inc(s.handle, by)

    write(items, 0, None)


class Program:

    def __init__(self, nc, ctx):
        self.nc, self.ctx, self.tallies = nc, ctx, []
        self.pe, self.act, self.dve, self.pool, self.sp = (
            Queue(self.tally(n), self.tally(n + "_step")) for n in ("s_pe", "s_act", "s_dve", "s_pool", "s_sp"))
        self.queues = [self.pe, self.act, self.dve, self.pool, self.sp]
        self.psum = [ctx.enter_context(nc.psum_tensor(f"bank{i}", [128, 512], F32)) for i in range(8)]
        self.bank_free = [None] * 8
        self.next_bank = 0

    def tally(self, name):
        s = Tally(self.ctx.enter_context(self.nc.semaphore(name)))
        self.tallies.append(s)
        return s

    def sbuf(self, name, width, dt=F32, scope=None):
        return (scope or self.ctx).enter_context(self.nc.sbuf_tensor(name, [128, width], dt))[:, :]

    def join(self, *more):
        last = [q.last for q in self.queues[:4]]
        for q in self.queues[:4]:
            q.wait(*last, *more)
        return last

    def bank(self):
        i = self.next_bank
        self.next_bank = (i + 1) % 8
        return i, self.psum[i], self.bank_free[i]

    def open_loop(self, trips):
        loop = Loop(trips, self.tallies)
        for q in self.queues:
            q.stack.append(q.items)
            q.items, q.loop = [], loop
        return loop

    def close_loop(self, loop):
        loop.close()
        for q in self.queues:
            body, q.items = q.items, q.stack.pop()
            q.items.append((loop, body))
            q.loop = None


def view(ap, dims, **sizes):
    return ap.rearrange(dims, **sizes)


def build(nc, io, out):
    ctx = ExitStack()
    with ctx:
        p = Program(nc, ctx)
        pe, act, dve, pool, sp = p.queues

        X = p.sbuf("x_nat", NT * D).rearrange("p (t d) -> p t d", t=NT)
        QO_flat = p.sbuf("q_and_o", B * HQ)
        QO = QO_flat.rearrange("p (b r) -> p b r", b=B)
        kt_raw = p.sbuf("ctx_T", KEYS)
        kn_raw = p.sbuf("ctx_nat", KT * C)
        mask_raw = p.sbuf("mask_bytes", KEYS, U8)
        value_w = p.sbuf("value_weights", INNER)
        ident = p.sbuf("ident", 128)
        vecs = p.sbuf("vectors", 2 * len(VECTORS))
        gates = p.sbuf("gates", 4)
        mv = p.sbuf("stats", NT * 6).rearrange("p (t s) -> p t s", t=NT)
        mean_var = p.sbuf("mean_var", NT * 2).rearrange("p (t s) -> p t s", t=NT)
        st = p.sbuf("row_stats", 8 * NT).rearrange("p (a t) -> p a t", t=NT)
        expert = p.sbuf("expert", 2 * NT).rearrange("p (a t) -> p a t", t=NT)
        rope = p.sbuf("rope", 2 * HD2)
        causal = p.sbuf("causal", S)
        head8 = p.sbuf("head8", HEADS)
        head16 = p.sbuf("head16", 8)
        mx = p.sbuf("row_max", 2 * 8).rearrange("p (a c) -> p a c", a=2)
        self_st = p.sbuf("self_stats", 3 * 16).rearrange("p (k c) -> p k c", k=3)

        dense = ExitStack()
        XT = p.sbuf("x_T", 4 * B * PAD, scope=dense).rearrange("p (k n) -> p k n", k=4)
        A = p.sbuf("area", 12 * B * PAD, scope=dense)
        W = p.sbuf("weights", 10240, scope=dense)
        small = p.sbuf("small", 640, scope=dense)
        dense.close()
        l0_p_T = [A[:, i * 3072:(i + 1) * 3072].rearrange("p (k c) -> p k c", k=KT) for i in range(2)]
        l0_scores = [A[:, 6144 + i * KEYS:6144 + (i + 1) * KEYS] for i in range(2)]
        l0_zeros = A[:, 9144:9144 + KEYS]

        att = ExitStack()

        def parts(name, width):
            return [[p.sbuf(f"{name}_{part}{i}", width, F32R, scope=att) for i in range(2)]
                    for part in ("high", "low")]

        KTs, KNs, QSs = parts("keys_T", KEYS), parts("keys_nat", KT * C), parts("q_stage", 256)
        PTs = [[x.rearrange("p (k c) -> p k c", k=KT) for x in both] for both in parts("p_T", KT * 256)]
        SB = [p.sbuf(f"scores{i}", KEYS, scope=att) for i in range(2)]
        MB = [p.sbuf(f"mask{i}", KEYS, BF16, scope=att) for i in range(2)]
        diagonal = [p.sbuf(f"diagonal{i}", 128, scope=att) for i in range(2)]
        inverse = [p.sbuf(f"inverse{i}", 256, scope=att) for i in range(2)]
        ones = p.sbuf("ones", 128, scope=att)
        att.close()

        s_const = p.tally("s_const")
        s_w = {n: p.tally(f"s_w_{n}") for n in ("l0", "l0b", "l1a", "l1b", "l2a", "l2b", "l3a", "l3b")}
        s_out = p.tally("s_out")

        def load(dst, src, sig, *waits):
            return sp.do(lambda e, it: e.dma_start(dst, src), *waits, tally=sig, by=16)

        def vec(name, k):
            c = 2 * VECTORS.index(name) + k
            return vecs[:, c:c + 1]

        L0W = W[:, 8192:10240]
        w_mem = L0W[:, 0:2 * C].rearrange("p (k c) -> p k c", k=2)
        w_memT = L0W[:, 256:512]
        w_gateT = L0W[:, 512:1536].rearrange("p (k n) -> p k n", k=4)
        b_gate = L0W[:, 1536:1792]
        norm_w = L0W[:, 1792:2048]
        x0T = XT[:, 0:2, :].rearrange("p k (b q) -> p k b q", b=B)

        load(w_mem, io["W_mem"].rearrange("(k p) c -> p k c", p=128), s_w["l0"])
        load(XT[:, 0:2, :], io["xT"], s_w["l0"])
        load(ident, io["ident"], s_w["l0"])

        def gated_names(l):
            return {n: f"L{l}_{n}" for n in ("ln_q_g", "ln_q_b", "ln_ff_g", "ln_ff_b")}

        ctx_rows = io["ctx"].rearrange("b (p k) c -> b p (k c)", p=KP)

        def memory_attention(tag, per_trip, units, groups, q_src, dest, kt_buf, kn_buf, copy_q, peel):
            nb, U, G = per_trip, len(units), len(groups)
            sp.wait(*[q.last for q in p.queues[:4]])
            trips = B // nb
            kt_sig = [p.tally(f"s_{tag}_kt{i}") for i in range(nb)]
            kn_sig = [p.tally(f"s_{tag}_kn{i}") for i in range(nb)]
            s_q = p.tally(f"s_{tag}_q")
            s_sc = p.tally(f"s_{tag}_scores")
            s_mx = p.tally(f"s_{tag}_max")
            s_ex = p.tally(f"s_{tag}_exp")
            s_nm = p.tally(f"s_{tag}_norm")
            s_rc = p.tally(f"s_{tag}_recip")
            s_nx = p.tally(f"s_{tag}_negmax")
            s_tr = p.tally(f"s_{tag}_transposed")
            s_ea = p.tally(f"s_{tag}_evac_act")
            s_ed = p.tally(f"s_{tag}_evac_dve")
            s_pv = p.tally(f"s_{tag}_sums")
            s_ov = p.tally(f"s_{tag}_o_out")
            group_of, col_of = {}, {}
            for g, (us, _, _) in enumerate(groups):
                for n, u in enumerate(us):
                    group_of[u], col_of[u] = g, 128 * n
            last_unit = {b: max(u for u in range(U) for x in units[u] if x[2] == b) for b in range(nb)}
            first_unit = {b: min(u for u in range(U) for x in units[u] if x[2] == b) for b in range(nb)}
            last_group = {b: max(g for g in range(G) for x in groups[g][2] if x[0] == b)
                          for b in range(nb)}
            rows_free = {b: groups[last_group[b]][1][-1] - U for b in range(nb)}

            def trip(depth, drain, carried, loop, index):
                now, missed, first = {}, set(), depth == 0

                def at(name, i):
                    if (name, i) in now:
                        return now[(name, i)]
                    if (name, i) in carried:
                        c = carried[(name, i)]
                        return Point(c.tally, c.value, loop) if loop else c
                    missed.add((name, i))
                    return None

                def loads(b):
                    def batch(it):
                        return index(it) * nb + b

                    scores_done = at("scores", last_unit[b] - U)
                    now[("kt", b)] = sp.do(
                        lambda e, it: e.dma_start(
                            kt_buf(b), io["ctxT"][bass.ds(batch(it), 1)].rearrange("o c k -> (o c) k")),
                        scores_done, tally=kt_sig[b], by=16, apart=True)

                def load_rows(b):
                    def batch(it):
                        return index(it) * nb + b

                    sums_done = at("sums", last_group[b] - G)
                    for lo, hi in ((0, 112), (112, KP)):
                        now[("kn", b)] = sp.do(
                            lambda e, it, lo=lo, hi=hi: e.dma_start(
                                kn_buf(b)[lo:hi, :],
                                ctx_rows[bass.ds(batch(it), 1), lo:hi, :]
                                .rearrange("o p n -> (o p) n")),
                            sums_done, tally=kn_sig[b], by=16, apart=True)

                def stage(b):
                    now[("q", b)] = pool.do(
                        lambda e, it: copy_q(e, b, index(it)),
                        at("scores", last_unit[b] - U), tally=s_q)

                def scores(u):
                    for c in range(CH):
                        for n, (row, m, b, q0) in enumerate(units[u]):
                            now[("scores", u)] = now[("scores%d" % c, u)] = pe.do(
                                lambda e, it, c=c, row=row, m=m, b=b, q0=q0: e.matmul(
                                    p.psum[c][row:row + m, 0:CHK], q_src(b)[:, q0:q0 + m],
                                    kt_buf(b)[:, c * CHK:(c + 1) * CHK], start=True, stop=True),
                                at("kt", b), at("q", b), at("max%d" % c, u - 1),
                                tally=s_sc)

                def maxima(u):
                    for c in range(CH):
                        now[("max", u)] = now[("max%d" % c, u)] = dve.do(
                            lambda e, it, c=c: e.tensor_tensor_reduce(
                                out=l0_scores[u % 2][:, c * CHK:(c + 1) * CHK], in0=p.psum[c][:, 0:CHK],
                                in1=l0_zeros[:, c * CHK:(c + 1) * CHK], scale=1.0, scalar=-BIG,
                                op0=ALU.add, op1=ALU.max, accum_out=mx[:, u % 2, c:c + 1]),
                            at("scores%d" % c, u),
                            at("transposed", u - 2), at("exp", u - 2), tally=s_mx, apart=True)
                    now[("negmax", u)] = dve.do(
                        lambda e, it: e.tensor_reduce(mx[:, u % 2, 3:4], mx[:, u % 2, 0:3], AX.X,
                                                      ALU.max, negate=True),
                        now[("max", u)], tally=s_nx)

                def exponentials(u):
                    now[("exp", u)] = act.do(
                        lambda e, it: e.activation(l0_scores[u % 2], l0_scores[u % 2], ACT.Exp,
                                                   bias=mx[:, u % 2, 3:4],
                                                   accum_out=mx[:, u % 2, 4:5]),
                        at("negmax", u), tally=s_ex)

                def normalise(u):
                    now[("recip", u)] = dve.do(
                        lambda e, it: e.reciprocal(mx[:, u % 2, 5:6], mx[:, u % 2, 4:5]),
                        at("exp", u), tally=s_rc)
                    now[("norm", u)] = dve.do(
                        lambda e, it: e.tensor_scalar(l0_scores[u % 2], l0_scores[u % 2], mx[:, u % 2, 5:6], None,
                                                      ALU.mult),
                        now[("recip", u)], tally=s_nm)

                def transposes(u):
                    for c in range(CH):
                        for k in range(4):
                            x = pe.do(
                                lambda e, it, c=c, k=k: e.transpose(
                                    p.psum[3 + c][0:KP, 128 * k:128 * k + 128],
                                    l0_scores[u % 2][:, (4 * c + k) * KP:(4 * c + k + 1) * KP], ident),
                                at("norm", u), at("evac%d" % c, u - 1),
                                tally=s_tr, quiet=(k < 3))
                        now[("transposed", u)] = now[("transposed%d" % c, u)] = x

                def evacuate(u, c):
                    g = group_of[u % U]
                    gi = g if u >= 0 else g - G
                    dst = l0_p_T[g % 2][0:KP, 4 * c:4 * c + 4, col_of[u % U]:col_of[u % U] + 128]
                    src = p.psum[3 + c][0:KP, :].rearrange("p (k r) -> p k r", k=4)
                    if c < 2:
                        fn, q, s = (lambda e, it: e.copy(dst, src)), act, s_ea
                    else:
                        fn, q, s = (lambda e, it: e.tensor_copy(dst, src)), dve, s_ed
                    now[("evac%d" % c, u)] = q.do(fn, at("transposed%d" % c, u), at("sums", gi - 2),
                                                  tally=s)

                def sums(g, part, parts):
                    us, _, work = groups[g % G]
                    todo = [(k, w) for w in work for k in range(KT)]
                    n = len(todo)
                    for i in range(n * part // parts, n * (part + 1) // parts):
                        k, (b, c0, width, o0) = todo[i]
                        bi, ui = b + (g // G) * nb, us[-1] + (g // G) * U
                        x = pe.do(
                            lambda e, it, k=k, b=b, c0=c0, width=width, o0=o0: e.matmul(
                                p.psum[6 + g % 2][:, o0:o0 + width], kn_buf(b)[0:KP, k * C:(k + 1) * C],
                                l0_p_T[g % 2][0:KP, k, c0:c0 + width], start=(k == 0), stop=(k == KT - 1)),
                            at("kn", bi), at("evac0", ui), at("evac1", ui), at("evac2", ui),
                            at("o_out", g - 2), tally=s_pv, quiet=(i < n - 1))
                    if part == parts - 1:
                        now[("sums", g)] = x

                def o_out(g):
                    work = groups[g % G][2]
                    width = max(o0 + w for _, _, w, o0 in work)
                    back = -(g // G)
                    now[("o_out", g)] = dve.do(
                        lambda e, it: e.tensor_copy(dest(g % G, index(it) - back),
                                                    p.psum[6 + g % 2][:, 0:width]),
                        at("sums", g), tally=s_ov)

                def in_slot(s):
                    for g, (_, slots, _) in enumerate(groups):
                        for n, x in enumerate(slots):
                            for back in range(min(depth, 2) + 1):
                                if x == s + back * U:
                                    yield g - back * G, n, len(slots)

                def out_in_slot(s):
                    for g, (_, slots, _) in enumerate(groups):
                        for back in range(min(depth, 2) + 1):
                            if slots[-1] + 1 == s + back * U:
                                yield g - back * G

                slots_here = max(x[1][-1] for x in groups) + 2 - U if drain else U
                if not drain:
                    for b in range(nb):
                        loads(b)
                        if first or rows_free[b] < 0:
                            load_rows(b)
                for s in range(slots_here):
                    if not drain:
                        for b in range(nb):
                            if first_unit[b] == s:
                                stage(b)
                        scores(s)
                        maxima(s)
                        exponentials(s)
                    for g, part, parts in in_slot(s):
                        if g < 0 or not drain:
                            sums(g, part, parts)
                    for b in range(nb):
                        if not (first or drain) and rows_free[b] == s:
                            load_rows(b)
                    for g in out_in_slot(s):
                        if g < 0 or not drain:
                            o_out(g)
                    if not drain:
                        normalise(s)
                    if (s == 0 and not first) or (s > 0 and not drain):
                        transposes(s - 1)
                        for c in range(CH):
                            evacuate(s - 1, c)
                return now, missed

            def shifted(now):
                size = {"q": nb, "kt": nb, "kn": nb, "sums": G, "o_out": G}
                return {(n, i - size.get(n, U)): v for (n, i), v in now.items()}

            carried = {}
            for j in range(peel):
                before = carried
                now, _ = trip(j, False, carried, None, lambda it, j=j: j)
                carried = {**{(n, i - {"q": nb, "kt": nb, "kn": nb, "sums": G,
                                       "o_out": G}.get(n, U)): v for (n, i), v in before.items()},
                           **shifted(now)}
            loop = p.open_loop(trips - peel)
            now, missed = trip(peel, False, carried, loop, lambda it: it + peel)
            p.close_loop(loop)
            after = shifted(now)
            for key, point in after.items():
                assert key not in missed, key
                if key in carried:
                    assert point.value == carried[key].value + loop.per[point.tally], key
            trip(trips, True, after, None, lambda it: trips)
            p.join()

        raw_free = {"kt": None, "kn": None, "mask": None}
        GROUPS = [[2 * g + n for n in range(2) if 2 * g + n < RT] for g in range((RT + 1) // 2)]
        NG = len(GROUPS)

        def cross_attention(tag, masked):
            nb, U, G, trips = 2, 2 * RT, 2 * NG, B // 2
            s_ktl, s_knl, s_ml = (p.tally(f"s_{tag}_{n}_loaded") for n in ("keysT", "keys", "mask"))
            s_kt, s_kn, s_mb, s_q = (p.tally(f"s_{tag}_{n}") for n in ("keysT", "keys", "mask", "q"))
            s_sc, s_mx, s_nx = (p.tally(f"s_{tag}_{n}") for n in ("scores", "max", "negmax"))
            s_ex, s_rc, s_dg = (p.tally(f"s_{tag}_{n}") for n in ("exp", "recip", "diagonal"))
            s_tr, s_eh, s_el = (p.tally(f"s_{tag}_{n}") for n in ("transposed", "high", "low"))
            s_pv, s_ov = (p.tally(f"s_{tag}_{n}") for n in ("sums", "o_out"))
            s_sp, s_in = (p.tally(f"s_{tag}_{n}") for n in ("spread", "inverse"))
            size = {"scores": U, "max": U, "negmax": U, "exp": U, "recip": U, "diagonal": U, "spread": G, "inverse": G,
                    "transposed": U, "high": U, "low": U, "sums": G, "o_out": G, "q": G}
            slots_of = [[3 + u for u in us] for us in GROUPS]
            kn_slots = range(3, 3 + CH)

            def group_of(u):
                return u // RT * NG + (u % RT) // 2

            def shifted(now):
                return {(n, i - size.get(n.rstrip("012"), nb)): v for (n, i), v in now.items()}

            def trip(carried, loop, index, kind):
                now, missed = {}, set()

                def at(name, i):
                    if (name, i) in now:
                        return now[(name, i)]
                    if (name, i) in carried:
                        c = carried[(name, i)]
                        return Point(c.tally, c.value, loop) if loop else c
                    missed.add((name, i))
                    return None

                def batch(it, v):
                    return bass.ds(index(it) * nb + v, 1)

                def load_kt(v):
                    now[("kt_raw", v)] = sp.do(
                        lambda e, it: e.dma_start(
                            kt_raw, io["ctxT"][batch(it, v)].rearrange("o c k -> (o c) k")),
                        at("kt2", v - 1), raw_free["kt"] if kind == "start" else None,
                        tally=s_ktl, by=16, apart=True)

                def load_kn(v):
                    for lo, hi in ((0, 112), (112, KP)):
                        now[("kn_raw", v)] = sp.do(
                            lambda e, it, lo=lo, hi=hi: e.dma_start(
                                kn_raw[lo:hi, :],
                                ctx_rows[batch(it, v), lo:hi, :].rearrange("o p n -> (o p) n")),
                            at("kn2", v - 1), raw_free["kn"] if kind == "start" else None,
                            tally=s_knl, by=16, apart=True)

                def load_mask(v):
                    if masked:
                        now[("mask_raw", v)] = sp.do(
                            lambda e, it: e.dma_start(
                                mask_raw, io["mask"][batch(it, v), :].to_broadcast([128, KEYS])),
                            at("mask", v - 1), raw_free["mask"] if kind == "start" else None,
                            tally=s_ml, by=16, apart=True)

                def cut(high, low, src, sig, *waits, moving=False):
                    if moving:
                        h = pool.do(lambda e, it: e.tensor_copy(high, src(it)), *waits, tally=sig)
                    else:
                        h = pool.do(lambda e, it: e.tensor_scalar(high, src(it), 1.0, 1.0,
                                                                  ALU.mult, ALU.mult),
                                    *waits, tally=sig, apart=True)
                    return pool.do(lambda e, it: e.tensor_tensor(
                        low, src(it), high.bitcast(F32), ALU.subtract), h, tally=sig, apart=True)

                def cut_kt(v, c):
                    cols = slice(c * CHK, (c + 1) * CHK)
                    now[("kt%d" % c, v)] = cut(
                        KTs[0][v % 2][:, cols], KTs[1][v % 2][:, cols], lambda it: kt_raw[:, cols], s_kt,
                        at("kt_raw", v), at("scores", (v - 1) * RT - 1))

                def cut_kn(v, c):
                    cols = slice(4 * c * C, 4 * (c + 1) * C)
                    now[("kn%d" % c, v)] = cut(
                        KNs[0][v % 2][0:KP, cols], KNs[1][v % 2][0:KP, cols],
                        lambda it: kn_raw[0:KP, cols], s_kn,
                        at("kn_raw", v), at("sums", (v - 1) * NG - 1))

                def cut_q(g):
                    v, us = g // NG, GROUPS[g % NG]
                    lo, n = 128 * us[0], 128 * len(us)
                    now[("q", g)] = cut(
                        QSs[0][g % 2][:, 0:n], QSs[1][g % 2][:, 0:n],
                        lambda it: QO[:, batch(it, v), lo:lo + n].rearrange("p o r -> p (o r)"), s_q,
                        at("scores", (g - 2) // NG * RT + GROUPS[(g - 2) % NG][-1]), moving=True)

                def bias(v):
                    if masked:
                        now[("mask", v)] = pool.do(
                            lambda e, it: e.tensor_scalar(MB[v % 2], mask_raw, -1.0, BIG,
                                                          ALU.add, ALU.mult),
                            at("mask_raw", v), at("max", (v - 1) * RT - 1), tally=s_mb, apart=True)


                def scores(u):
                    g, b = group_of(u), u // RT
                    lo = 128 * ((u % RT) % 2)
                    for c in range(CH):
                        cols = slice(c * CHK, (c + 1) * CHK)
                        for n, (i, j) in enumerate(((0, 0), (0, 1), (1, 0))):
                            x = pe.do(lambda e, it, c=c, i=i, j=j, n=n, cols=cols: e.matmul(
                                p.psum[c][:, 0:CHK], QSs[i][g % 2][:, lo:lo + 128], KTs[j][b][:, cols],
                                start=(n == 0), stop=(n == 2)),
                                at("kt%d" % c, b), at("q", g), at("max%d" % c, u - 1),
                                tally=s_sc, quiet=(n < 2))
                        now[("scores", u)] = now[("scores%d" % c, u)] = x

                def maxima(u):
                    b = u // RT
                    mb = MB[b] if masked else MB[0]
                    for c in range(CH):
                        now[("max", u)] = now[("max%d" % c, u)] = dve.do(
                            lambda e, it, c=c: e.tensor_tensor_reduce(
                                out=SB[u % 2][:, c * CHK:(c + 1) * CHK], in0=p.psum[c][:, 0:CHK],
                                in1=mb[:, c * CHK:(c + 1) * CHK], scale=1.0, scalar=-BIG,
                                op0=ALU.add, op1=ALU.max, accum_out=mx[:, u % 2, c:c + 1]),
                            at("scores%d" % c, u), at("mask", b if masked else 0),
                            at("transposed", u - 2), at("exp", u - 2), tally=s_mx, apart=True)
                    now[("negmax", u)] = dve.do(
                        lambda e, it: e.tensor_reduce(mx[:, u % 2, 3:4], mx[:, u % 2, 0:3], AX.X,
                                                      ALU.max, negate=True),
                        now[("max", u)], tally=s_nx)

                def exponentials(u):
                    now[("exp", u)] = act.do(
                        lambda e, it: e.activation(SB[u % 2], SB[u % 2], ACT.Exp,
                                                   bias=mx[:, u % 2, 3:4],
                                                   accum_out=mx[:, u % 2, 4:5]),
                        at("negmax", u), tally=s_ex)

                def reciprocals(u):
                    now[("recip", u)] = dve.do(
                        lambda e, it: e.reciprocal(mx[:, u % 2, 5:6], mx[:, u % 2, 4:5]),
                        at("exp", u), at("diagonal", u - 2), tally=s_rc)
                    now[("diagonal", u)] = act.do(
                        lambda e, it: e.activation(diagonal[u % 2], ident, ACT.Copy,
                                                   scale=mx[:, u % 2, 5:6]),
                        now[("recip", u)], at("spread", group_of(u - 2)), tally=s_dg)

                def spread(g):
                    us, bank = GROUPS[g % NG], p.psum[6 + g % 2]
                    n = 128 * len(us)
                    for i, u in enumerate(us):
                        u += g // NG * RT
                        x = pe.do(
                            lambda e, it, i=i, u=u: e.matmul(
                                bank[:, 128 * i:128 * i + 128], ones, diagonal[u % 2],
                                start=True, stop=True),
                            at("diagonal", u), at("o_out", g - 2), tally=s_sp)
                    now[("spread", g)] = x
                    now[("inverse", g)] = act.do(
                        lambda e, it: e.copy(inverse[g % 2][:, 0:n], bank[:, 0:n]), x, tally=s_in)

                def transposes(u):
                    for c in range(CH):
                        for k in range(4):
                            x = pe.do(
                                lambda e, it, c=c, k=k: e.transpose(
                                    p.psum[3 + c][0:KP, 128 * k:128 * k + 128],
                                    SB[u % 2][:, (4 * c + k) * KP:(4 * c + k + 1) * KP], ident),
                                at("exp", u), at("low%d" % c, u - 1),
                                tally=s_tr, quiet=(k < 3))
                        now[("transposed", u)] = now[("transposed%d" % c, u)] = x

                def evacuate(u, c):
                    g = group_of(u)
                    lo = 128 * ((u % RT) % 2)
                    high, low = (PTs[i][g % 2][0:KP, 4 * c:4 * c + 4, lo:lo + 128] for i in range(2))
                    src = p.psum[3 + c][0:KP, :].rearrange("p (k r) -> p k r", k=4)
                    h = act.do(lambda e, it: e.copy(high, src),
                               at("transposed%d" % c, u), at("sums", g - 2), tally=s_eh)
                    now[("low%d" % c, u)] = now[("low", u)] = dve.do(
                        lambda e, it: e.tensor_tensor(low, src, high.bitcast(F32), ALU.subtract),
                        h, tally=s_el)

                def sums(g, part, of):
                    us = GROUPS[g % NG]
                    b, width = g // NG, 128 * len(us)
                    last_u = b * RT + us[-1]
                    for k in range(KT * part // of, KT * (part + 1) // of):
                        cols = slice(k * C, (k + 1) * C)
                        for n, (i, j) in enumerate(((0, 0), (0, 1), (1, 0))):
                            stop = k == KT - 1 and n == 2
                            x = pe.do(
                                lambda e, it, k=k, i=i, j=j, n=n, cols=cols, stop=stop: e.matmul(
                                    p.psum[6 + g % 2][:, 0:width], KNs[i][b % 2][0:KP, cols],
                                    PTs[j][g % 2][0:KP, k, 0:width], start=(k == 0 and n == 0),
                                    stop=stop),
                                at("kn%d" % (k // 4), b), at("low%d" % (k // 4), last_u), at("inverse", g),
                                tally=s_pv, quiet=not stop)
                    if part == of - 1:
                        now[("sums", g)] = x

                def o_out(g):
                    us = GROUPS[g % NG]
                    lo, n = 128 * us[0], 128 * len(us)
                    now[("o_out", g)] = dve.do(
                        lambda e, it: e.tensor_tensor(
                            QO[:, batch(it, g // NG), lo:lo + n].rearrange("p o r -> p (o r)"),
                            p.psum[6 + g % 2][:, 0:n], inverse[g % 2][:, 0:n], ALU.mult),
                        at("sums", g), at("inverse", g), tally=s_ov, apart=True)

                if kind == "start":
                    load_kt(0), load_kn(0), load_mask(0)
                    now[("ones", 0)] = pool.do(lambda e, it: e.memset(ones, 1.0), tally=s_q)
                    if not masked:
                        now[("mask", 0)] = now[("mask", -nb)] = pool.do(
                            lambda e, it: e.memset(MB[0], 0.0), tally=s_mb)
                    cut_kt(0, 0), cut_q(0), bias(0), cut_kt(0, 1), cut_kt(0, 2)
                    load_kt(1), load_mask(1)
                    for c in range(CH):
                        cut_kn(0, c)
                    load_kn(1)
                    return now, missed
                first, last, drain = kind == "first", kind == "last", kind == "drain"
                work = {}
                for g in range(0 if first else -NG, 0 if drain else G):
                    ss = [g // NG * RT + x for x in slots_of[g % NG]]
                    for n, x in enumerate(ss):
                        if 0 <= x < (3 if drain else U):
                            work.setdefault(x, []).append((g, n, len(ss)))
                for s in range(3 if drain else U):
                    b, j = s // RT, s % RT
                    ahead = not drain and not (last and b == nb - 1)
                    ahead2 = not drain and not last
                    before = s > 0 if first else s == 0 if drain else True
                    if not drain:
                        scores(s)
                        maxima(s)
                    if before:
                        reciprocals(s - 1)
                    for g, n, of in work.get(s, []):
                        sums(g, n, of)
                        if n == of - 1:
                            o_out(g)
                    if before:
                        transposes(s - 1)
                        for c in range(CH):
                            evacuate(s - 1, c)
                        if (s - 1) % RT % 2 == 1 or (s - 1) % RT == RT - 1:
                            spread(group_of(s - 1))
                    if not drain:
                        exponentials(s)
                    if not drain:
                        if j % 2 == 0 and (ahead or j // 2 < NG - 1):
                            cut_q(b * NG + j // 2 + 1)
                        if j < CH and ahead:
                            cut_kt(b + 1, j)
                        if j in kn_slots and ahead:
                            cut_kn(b + 1, j - 3)
                        if j == RT - 1 and ahead:
                            bias(b + 1)
                        if ahead2 and j == CH - 1:
                            load_kt(b + 2)
                        if ahead2 and j == kn_slots[-1]:
                            load_kn(b + 2)
                        if ahead2 and j == RT - 1:
                            load_mask(b + 2)
                return now, missed

            def whole(index, kind, carried):
                now, _ = trip(carried, None, index, kind)
                return {**shifted(carried), **shifted(now)}

            carried, _ = trip({}, None, lambda it: 0, "start")
            carried = whole(lambda it: 0, "first", carried)
            loop = p.open_loop(trips - 2)
            now, missed = trip(carried, loop, lambda it: it + 1, "more")
            p.close_loop(loop)
            after = shifted(now)
            for key, point in after.items():
                assert key not in missed, key
                if key in carried:
                    assert point.value == carried[key].value + loop.per[point.tally], key
            if not masked:
                after[("mask", 0)] = carried[("mask", -nb)]
            after = whole(lambda it: trips - 1, "last", after)
            raw_free["kt"], raw_free["kn"] = after[("kt2", -1)], after[("kn2", -1)]
            if masked:
                raw_free["mask"] = after[("mask", -1)]
            trip(after, None, lambda it: trips, "drain")
            p.join()

        turn = [0]

        def either(*engines):
            turn[0] += 1
            return (act, dve)[turn[0] % 2]

        def scale_out(dst, src, scale, *waits, q=None):
            q = q or either()
            if q is act:
                return act.do(lambda e, it: e.activation(dst, src, ACT.Copy, scale=scale), *waits)
            return dve.do(lambda e, it: e.tensor_scalar(dst, src, scale, None, ALU.mult), *waits)

        def product(steps, width, *waits, rows=128, row0=0, shape=None):
            i, bank, free = p.bank()
            for n, (lhsT, rhs) in enumerate(steps):
                o = bank[row0:row0 + rows, 0:width]
                x = pe.do(lambda e, it, lhsT=lhsT, rhs=rhs, o=o, n=n: e.matmul(
                    o, lhsT, rhs, start=(n == 0), stop=(n == len(steps) - 1)),
                    free, *waits, quiet=(n < len(steps) - 1))
            return i, bank, x

        def tokens(arr, k, half):
            return arr[:, k, :].rearrange("p (b q) -> p b q", b=B)[:, HALF * half:HALF * half + HALF, 0:S]

        def real(ap):
            return ap.rearrange("p (b q) -> p b q", q=S)

        def rstd(src, eps, scale, *waits):
            a = dve.do(lambda e, it: e.tensor_scalar(st[:, 0, :], src, scale, eps, ALU.mult, ALU.add),
                       *waits)
            r = act.do(lambda e, it: e.activation(st[:, 1, :], st[:, 0, :], ACT.Sqrt), a)
            return dve.do(lambda e, it: e.reciprocal(st[:, 2, :], st[:, 1, :]), r)

        XN = A[:, 8192:12288].rearrange("p (k t d) -> p k t d", k=2, t=NT)

        def transposed_norm(kind, g, bias, masked, *waits):
            if kind == "layer":
                done = None
                for t in range(NT):
                    a = dve.do(lambda e, it, t=t: e.bn_stats(mv[:, t, :], X[:, t, :]), *waits)
                    done = dve.do(lambda e, it, t=t: e.bn_aggr(mean_var[:, t, :], mv[:, t, :]), a)
                r = rstd(mean_var[:, :, 1], 1e-5, 1.0, done)
            else:
                for t in range(NT):
                    done = dve.do(lambda e, it, t=t: e.tensor_tensor_reduce(
                        out=XN[:, 1, t, :], in0=X[:, t, :], in1=X[:, t, :], scale=1.0, scalar=0.0,
                        op0=ALU.mult, op1=ALU.add, accum_out=st[:, 3, t:t + 1]), *waits)
                r = rstd(st[:, 3, :], 1e-6, 1.0 / D, done)
            if masked:
                for m in range(2):
                    r2 = dve.do(lambda e, it, m=m: e.tensor_tensor(
                        st[:, 4 + m, :], st[:, 2, :], expert[:, m, :], ALU.mult), r)
            n_k = 4 if masked else 2
            for m in range(2 if masked else 1):
                for t in range(NT):
                    if kind == "layer":
                        x = dve.do(lambda e, it, t=t: e.tensor_scalar(
                            XN[:, 0, t, :], X[:, t, :], mean_var[:, t, 0:1], st[:, 2, t:t + 1],
                            ALU.subtract, ALU.mult), r)
                    else:
                        s = (4 + m) if masked else 2
                        x = dve.do(lambda e, it, t=t, m=m, s=s: e.tensor_scalar(
                            XN[:, m, t, :], X[:, t, :], st[:, s, t:t + 1], None, ALU.mult),
                            r2 if masked else r)
            return transpose_in(n_k // 2, lambda k: vec(g, k), (lambda k: vec(bias, k)) if bias else None, x)

        def transpose_in(n_m, g, bias, x):
            outs = []
            for m in range(n_m):
                for k in range(2):
                    for h in range(2):
                        i, bank, free = p.bank()
                        for j in range(4):
                            y = pe.do(lambda e, it, m=m, k=k, h=h, j=j, bank=bank: e.transpose(
                                bank[:, 128 * j:128 * j + 128],
                                XN[:, m, 4 * h + j, 128 * k:128 * k + 128], ident), x, free,
                                quiet=(j < 3))
                        dst = XT[:, 2 * m + k, 512 * h:512 * h + 512]
                        if bias:
                            z = act.do(lambda e, it, dst=dst, bank=bank, k=k: e.activation(
                                dst, bank[:, :], ACT.Identity, scale=g(k), bias=bias(k)), y)
                        elif g:
                            z = dve.do(lambda e, it, dst=dst, bank=bank, k=k: e.tensor_scalar(
                                dst, bank[:, :], g(k), None, ALU.mult), y)
                        else:
                            z = dve.do(lambda e, it, dst=dst, bank=bank: e.tensor_copy(
                                dst, bank[:, :]), y)
                        p.bank_free[i] = z
                        outs.append(z)
            return outs

        def pads(arr, k):
            return pool.do(lambda e, it: e.memset(
                arr.rearrange("p (x q) -> p x q", q=PAD)[:, 0:k * B, S:PAD], 0.0))

        kt0 = [QO_flat[:, i * KEYS:(i + 1) * KEYS] for i in range(4)]
        kn0 = [QO_flat[:, 4 * KEYS + i * KT * C:4 * KEYS + (i + 1) * KT * C] for i in range(4)]
        at0 = 4 * KEYS + 4 * KT * C
        q0T = QO_flat[:, at0:at0 + B * PAD].rearrange("p (b q) -> p b q", b=B)
        mcT = QO_flat[:, at0 + B * PAD:at0 + 2 * B * PAD]

        zero_q = pool.do(lambda e, it: e.memset(q0T, 0.0))
        pool.do(lambda e, it: e.memset(l0_zeros, 0.0))
        w0 = Point(s_w["l0"], s_w["l0"].count)
        for half in range(2):
            i, bank, x = product([(w_mem[:, k, :], x0T[:, k, HALF * half:HALF * half + HALF, 0:S])
                                  for k in range(2)], HALF * S, w0)
            p.bank_free[i] = scale_out(q0T[:, HALF * half:HALF * half + HALF, 0:S],
                                       real(bank[:, 0:HALF * S]), 1.0 / 16.0, x, zero_q)
        p.join()

        QS = W[:, 4096:4096 + 4 * PAD]

        def stage_q0(e, b, j):
            return e.tensor_copy(QS[:, b * PAD:(b + 1) * PAD],
                                 q0T[:, bass.ds(j * 4 + b, 1), :].rearrange("p o q -> p (o q)"))

        def dest0(g, j):
            return mcT.rearrange("p (t r) -> p t r", t=NT)[:, bass.ds(j * 2 + g, 1), :] \
                .rearrange("p o r -> p (o r)")

        memory_attention("l0", 4, [[(0, PAD, 0, 0), (PAD, PAD, 1, 0)], [(0, PAD, 2, 0), (PAD, PAD, 3, 0)]],
                  [([0], [2], [(0, 0, PAD, 0), (1, PAD, PAD, PAD)]),
                   ([1], [3], [(2, 0, PAD, 0), (3, PAD, PAD, PAD)])],
                  lambda b: QS[:, b * PAD:(b + 1) * PAD], dest0,
                  lambda b: kt0[b], lambda b: kn0[b], stage_q0, 2)

        load(w_memT, io["W_memT"], s_w["l0b"])
        load(w_gateT, io["W_gateT"].rearrange("(k p) n -> p k n", p=128), s_w["l0b"])
        load(b_gate, io["b_gate"].to_broadcast([128, D]), s_w["l0b"])
        load(norm_w, io["norm_w"].to_broadcast([128, D]), s_w["l0b"])
        load(X, io["x"], s_w["l0b"])
        load(vecs, io["vectors"], s_const)
        load(gates, io["gates"].to_broadcast([128, 4]), s_const)

        def w3(lo, k, n):
            return W[:, lo:lo + k * n].rearrange("p (k n) -> p k n", k=k)

        g_wq, g_wkT = w3(0, 2, INNER), w3(2048, 8, C)
        g_wo, g_w1, g_w2 = w3(4096, 8, D), w3(6144, 2, FF), w3(8192, 8, D)

        def load_gated_a(l, *waits):
            load(g_wq, io[f"L{l}_Wq"].rearrange("(k p) n -> p k n", p=128), s_w[f"l{l}a"], *waits)
            load(g_wkT, io[f"L{l}_WkT"].rearrange("(k p) n -> p k n", p=128), s_w[f"l{l}a"])
            load(value_w, io[f"L{l}_Wkv"][:, INNER:2 * INNER], s_w[f"l{l}a"])

        def load_gated_b(l, *waits):
            b = s_w[f"l{l}b"]
            load(g_wo, io[f"L{l}_Wo"].rearrange("(k p) n -> p k n", p=128), b, *waits)
            load(g_w1, io[f"L{l}_W1"].rearrange("(k p) n -> p k n", p=128), b)
            load(g_w2, io[f"L{l}_W2"].rearrange("(k p) n -> p k n", p=128), b)

        load_gated_a(1)
        w0 = Point(s_w["l0b"], s_w["l0b"].count)
        consts = Point(s_const, s_const.count)
        tanh_gates = act.do(lambda e, it: e.activation(gates, gates, ACT.Tanh), consts)

        mc_nat = A[:, 0:2048].rearrange("p (t d) -> p t d", t=NT)
        fused = A[:, 2048:4096].rearrange("p (t d) -> p t d", t=NT)
        junk = A[:, 4096:4352]
        for t in range(NT):
            i, bank, x = product([(mcT[:, 128 * t:128 * t + 128], w_memT)], D, w0)
            p.bank_free[i] = scale_out(mc_nat[:, t, :], bank[:, 0:D], 1.0, x, q=dve)
        for k in range(2):
            for h in range(2):
                i, bank, x = product([(w_memT[:, 128 * k:128 * k + 128], mcT[:, 512 * h:512 * h + 512])],
                                     512)
                p.bank_free[i] = mcTT = scale_out(XT[:, 2 + k, 512 * h:512 * h + 512], bank[:, :], 1.0, x,
                                                  q=act)
        for t in range(NT):
            i, bank, x = product([(XT[:, k, 128 * t:128 * t + 128], w_gateT[:, k, :])
                                  for k in range(4)], D, mcTT)
            a = dve.do(lambda e, it, t=t, bank=bank: e.tensor_tensor(
                fused[:, t, :], bank[:, 0:D], b_gate, ALU.add), x)
            p.bank_free[i] = a
            g = act.do(lambda e, it, t=t: e.activation(fused[:, t, :], fused[:, t, :], ACT.Sigmoid), a)
            m = pool.do(lambda e, it, t=t: e.tensor_tensor(
                fused[:, t, :], fused[:, t, :], mc_nat[:, t, :], ALU.mult), g, dve.last)
            m = pool.do(lambda e, it, t=t: e.tensor_tensor(
                fused[:, t, :], fused[:, t, :], X[:, t, :], ALU.add), m, w0)
        for t in range(NT):
            ss = dve.do(lambda e, it, t=t: e.tensor_tensor_reduce(
                out=junk, in0=fused[:, t, :], in1=fused[:, t, :], scale=1.0, scalar=0.0,
                op0=ALU.mult, op1=ALU.add, accum_out=st[:, 3, t:t + 1]), m, dve.last)
        r = rstd(st[:, 3, :], 1e-6, 1.0 / D, ss)
        for t in range(NT):
            dve.do(lambda e, it, t=t: e.scalar_tensor_tensor(
                X[:, t, :], fused[:, t, :], st[:, 2, t:t + 1], norm_w, ALU.mult, ALU.mult), r)
        p.join()

        def residual(t, bank, x, gate):
            if gate is None:
                return dve.do(lambda e, it: e.tensor_tensor(X[:, t, :], bank[:, 0:D], X[:, t, :],
                                                            ALU.add), x)
            return dve.do(lambda e, it: e.scalar_tensor_tensor(
                X[:, t, :], bank[:, 0:D], gates[:, gate:gate + 1], X[:, t, :], ALU.mult, ALU.add), x)

        def head_queries(q_dst, half, h):
            return QO[:, HALF * half:HALF * half + HALF, S * h:S * h + S]

        def gated_block(l):
            wa = Point(s_w[f"l{l}a"], s_w[f"l{l}a"].count)
            n = gated_names(l)
            xs = transposed_norm("layer", n["ln_q_g"], n["ln_q_b"], False)
            qT = A[:, 0:8 * B * S].rearrange("p (j n) -> p j n", j=8)
            for j in range(8):
                for half in range(2):
                    i, bank, x = product([(g_wq[:, k, 128 * j:128 * j + 128], tokens(XT, k, half))
                                          for k in range(2)], HALF * S, wa, *xs)
                    p.bank_free[i] = qt = scale_out(
                        qT[:, j, HALF * S * half:HALF * S * (half + 1)], bank[:, 0:HALF * S],
                        DH ** -0.5, x)
                both = [act.last, dve.last]
                for half in range(2):
                    for hh in range(2):
                        i, bank, x = product(
                            [(g_wkT[64 * hh:64 * hh + 64, j, :],
                              qT[64 * hh:64 * hh + 64, j, HALF * S * half:HALF * S * (half + 1)])],
                            HALF * S, *both)
                        p.bank_free[i] = scale_out(head_queries(QO, half, 2 * j + hh),
                                                   real(bank[:, 0:HALF * S]), 1.0, x)
            p.join()
            cross_attention(f"l{l}", True)
            load_gated_b(l, *[q.last for q in p.queues[:4]])
            wb = Point(s_w[f"l{l}b"], s_w[f"l{l}b"].count)

            aoT = A[:, 0:8 * B * PAD].rearrange("p (j n) -> p j n", j=8)
            z = pads(A, 8)
            for j in range(8):
                for half in range(2):
                    i, bank, free = p.bank()
                    for hh in range(2):
                        h = 2 * j + hh
                        x = pe.do(lambda e, it, h=h, hh=hh, half=half, bank=bank: e.matmul(
                            bank[64 * hh:64 * hh + 64, 0:HALF * S], value_w[:, DH * h:DH * h + DH],
                            head_queries(QO, half, h), start=True, stop=True), free, wa)
                    p.bank_free[i] = scale_out(tokens(aoT, j, half), real(bank[:, 0:HALF * S]), 1.0, x)
            both = [act.last, dve.last, z]
            for t in range(NT):
                i, bank, x = product([(aoT[:, j, 128 * t:128 * t + 128], g_wo[:, j, :])
                                      for j in range(8)], D, *both, wb)
                p.bank_free[i] = residual(t, bank, x, l - 1)
            xs = transposed_norm("layer", n["ln_ff_g"], n["ln_ff_b"], False, dve.last)
            pe_before = pe.last
            for j in range(8):
                for half in range(2):
                    i, bank, x = product([(g_w1[:, k, 128 * j:128 * j + 128], tokens(XT, k, half))
                                          for k in range(2)], HALF * S, *xs)
                    p.bank_free[i] = act.do(lambda e, it, j=j, half=half, bank=bank: e.activation(
                        tokens(aoT, j, half), real(bank[:, 0:HALF * S]), ACT.Gelu), x, pe_before)
            for t in range(NT):
                i, bank, x = product([(aoT[:, j, 128 * t:128 * t + 128], g_w2[:, j, :])
                                      for j in range(8)], D, act.last, z)
                p.bank_free[i] = residual(t, bank, x, l)
            p.join()

        gated_block(1)

        wqkv, wden = w3(0, 4, 3 * D), w3(3072, 4, D)
        wcq, wckT, wcv, wcd = w3(8960, 2, C), W[:, 9216:9344], value_w[:, 0:C], value_w[:, C:C + D]
        wgu = W[:, 0:8 * II].rearrange("p (x n) -> p x n", x=8)
        wdown = w3(8 * II, 12, D)
        free = [q.last for q in p.queues[:4]]
        for m, e in enumerate("vl"):
            load(wqkv[:, 2 * m:2 * m + 2, :], io[f"L2_{e}_qkv"].rearrange("(k p) n -> p k n", p=128),
                 s_w["l2a"], *free)
            load(wden[:, 2 * m:2 * m + 2, :], io[f"L2_{e}_dense"].rearrange("(k p) n -> p k n", p=128),
                 s_w["l2a"])
        load(wcq, io["L2_cq_w"].rearrange("(k p) n -> p k n", p=128), s_w["l2a"])
        load(wckT, io["L2_ckT"], s_w["l2a"])
        load(wcv, io["L2_ckv_w"][:, C:2 * C], s_w["l2a"])
        load(wcd, io["L2_cdense_w"], s_w["l2a"])

        types = small[:, 0:2 * NT].bitcast(I32).rearrange("p (a t) -> p a t", a=2)
        s_ty = p.tally("s_types")
        load(types, io["types"], s_ty, *free)
        pos = small[:, 64:64 + S].bitcast(I32)
        posf, onehot = small[:, 128:128 + S], small[:, 256:256 + 128]
        table, tidx = small[:, 448:448 + 2 * HD2], small[:, 512:513]
        load(pos[0:S, :], io["pos"].to_broadcast([S, S]), s_ty)
        load(table[0:S, :], io["rope"], s_ty)
        load(tidx[0:S, :], io["index"], s_ty)
        load(head16, io["head16"], s_ty)
        load(head8, io["head8"], s_ty)
        load(causal, io["causal"], s_ty)
        ty = Point(s_ty, s_ty.count)
        a = dve.do(lambda e, it: e.tensor_scalar(st[:, 6:8, :], types, 1.0, None,
                                                 ALU.is_equal), ty)
        a = dve.do(lambda e, it: e.tensor_tensor(expert[:, 0, :], st[:, 6, :], st[:, 7, :], ALU.mult), a)
        a = dve.do(lambda e, it: e.tensor_scalar(expert[:, 1, :], expert[:, 0, :], -1.0, 1.0,
                                                 ALU.mult, ALU.add), a)
        zo = dve.do(lambda e, it: e.memset(onehot[0:S, :], 0.0))
        b_ = dve.do(lambda e, it: e.tensor_scalar(posf[0:S, :], pos[0:S, :], 0.0, float(S - 1),
                                                  ALU.max, ALU.min), ty)
        oh = onehot[0:S, :].rearrange("p (a q) -> p a q", a=2)
        for par in range(2):
            b2 = dve.do(lambda e, it, par=par: e.tensor_scalar(
                oh[:, par, 0:S], posf[0:S, :], tidx[0:S, 0:1], None, ALU.is_equal), zo, b_)
        i, bank, x = product([(onehot[0:S, :], table[0:S, :])], 2 * HD2, b2)
        p.bank_free[i] = rp = dve.do(lambda e, it, bank=bank: e.tensor_copy(rope,
                                                                            bank[:, 0:2 * HD2]), x)
        cosb = rope[:, 0:HD2]
        sinb = rope[:, HD2:2 * HD2]

        QKT = QO_flat[:, 0:4096].rearrange("p (k n) -> p k n", k=4)
        V = QO_flat[:, 4096:6144].rearrange("p (t d) -> p t d", t=NT)
        QB = QO_flat[:, 6144:8192].rearrange("p (b k h q) -> p b k h q", b=2, k=2, h=8)
        SS = QO_flat[:, 8192:9216].rearrange("p (j b q) -> p j b q", j=8, b=2)
        ST = QO_flat[:, 9216:10240].rearrange("p (j r) -> p j r", j=8)
        VS = QO_flat[:, 10240:10496]
        pool.do(lambda e, it: e.memset(SS, 0.0))
        p.join()
        xs = transposed_norm("rms", "L2_ln_in_w", None, True)
        w2a = Point(s_w["l2a"], s_w["l2a"].count)
        rotA = [A[:, i * 512:(i + 1) * 512] for i in range(2)]
        rotB = [A[:, 1024 + i * 512:1024 + (i + 1) * 512] for i in range(2)]
        before = [pe.last, dve.last, pool.last]
        transposes_done = {}
        for t in range(NT):
            i, bank, x = product([(XT[:, k, 128 * t:128 * t + 128], wqkv[:, k, 0:2 * D])
                                  for k in range(4)], 2 * D, w2a, *xs)
            i2, bank2, x2 = product([(XT[:, k, 128 * t:128 * t + 128], wqkv[:, k, 2 * D:3 * D])
                                     for k in range(4)], D)
            p.bank_free[i2] = scale_out(V[:, t, :], bank2[:, 0:D], 1.0, x2, q=act)
            a_, b_ = rotA[t % 2], rotB[t % 2]
            old = transposes_done.get(t - 2)
            qk = bank[:, :].rearrange("p (h c) -> p h c", c=HD2)
            cb = cosb.rearrange("p (o c) -> p o c", o=1).to_broadcast([128, 32, HD2])
            c1 = dve.do(lambda e, it, a_=a_, qk=qk, cb=cb: e.tensor_tensor(
                a_.rearrange("p (h c) -> p h c", c=HD2), qk, cb, ALU.mult), x, rp, old, *before)
            for d in range(2):
                sb_ = sinb[:, 8 * d:8 * d + 8].rearrange("p (o c) -> p o c", o=1) \
                    .to_broadcast([128, 32, 8])
                c2 = dve.do(lambda e, it, b_=b_, qk=qk, d=d, sb_=sb_: e.tensor_tensor(
                    b_.rearrange("p (h c) -> p h c", c=HD2)[:, :, 8 * d:8 * d + 8],
                    qk[:, :, 8 - 8 * d:16 - 8 * d], sb_, ALU.mult), x)
            p.bank_free[i] = c2
            c3 = pool.do(lambda e, it, a_=a_, b_=b_: e.tensor_tensor(a_, a_, b_, ALU.add), c1, c2)
            i3, bank3, free3 = p.bank()
            for k in range(4):
                y = pe.do(lambda e, it, k=k, a_=a_, bank3=bank3: e.transpose(
                    bank3[:, 128 * k:128 * k + 128], a_[:, 128 * k:128 * k + 128], ident), c3, free3)
            transposes_done[t] = y
            p.bank_free[i3] = scale_out(
                QKT[:, :, 128 * t:128 * t + 128], bank3[:, :].rearrange("p (k n) -> p k n", k=4),
                1.0, y, q=act)
        p.join()

        s_st, s_sc, s_sm, s_se, s_tp, s_cp, s_cx, s_out2 = (p.tally(f"s_self_{n}") for n in (
            "staged", "scores", "softmax", "exp", "transposed", "copied", "sums", "out"))
        CN = A[:, 4096:6144].rearrange("p (t d) -> p t d", t=NT)

        def pair_attention(pair, before_trip):
            for b in range(2):
                for k in range(2):
                    staged = pool.do(lambda e, it, b=b, k=k: e.tensor_tensor(
                        QB[:, b, k], QKT[:, k, bass.ds(pair(it) * 128 + b * 64, 64)]
                        .rearrange("p (o q) -> p o q", o=1).to_broadcast([128, 8, PAD]),
                        head16.rearrange("p (h o) -> p h o", o=1).to_broadcast([128, 8, PAD]),
                        ALU.mult), before_trip(s_sc), tally=s_st)
            staged = pool.do(lambda e, it: e.tensor_copy(
                VS, V[:, bass.ds(pair(it), 1), :].rearrange("p o d -> p (o d)")), before_trip(s_cx), tally=s_st)
            for b in range(2):
                for j in range(8):
                    x = pe.do(lambda e, it, b=b, j=j: e.matmul(
                        p.psum[b][:, 64 * j:64 * j + S],
                        QB[:, b, j // 4, 2 * (j % 4):2 * (j % 4) + 2, :].rearrange("p h q -> p (h q)"),
                        QKT[:, 2 + j // 4, bass.ds(pair(it) * 128 + b * 64, S)], start=True, stop=True),
                        staged, before_trip(s_sm), tally=s_sc)
            for b in range(2):
                d = dve.do(lambda e, it, b=b: e.tensor_tensor(
                    SS[:, :, b, 0:S], p.psum[b][:, :].rearrange("p (j q) -> p j q", j=8)[:, :, 0:S],
                    causal.rearrange("p (o q) -> p o q", o=1).to_broadcast([128, 8, S]), ALU.add),
                    x, before_trip(s_tp), tally=s_sm)
            m_, z_, r_ = (self_st[:, n, :].rearrange("p (j b) -> p j b", j=8) for n in range(3))
            d = dve.do(lambda e, it: e.tensor_reduce(m_, SS[:, :, :, 0:S], AX.X, ALU.max), d, tally=s_sm)
            for b in range(2):
                d2 = dve.do(lambda e, it, b=b: e.tensor_tensor(
                    SS[:, :, b, 0:S], SS[:, :, b, 0:S], m_[:, :, b:b + 1].to_broadcast([128, 8, S]),
                    ALU.subtract), d, tally=s_sm)
            for b in range(2):
                ex = act.do(lambda e, it, b=b: e.activation(SS[:, :, b, 0:S], SS[:, :, b, 0:S], ACT.Exp),
                            d2, tally=s_se)
            d = dve.do(lambda e, it: e.tensor_reduce(z_, SS[:, :, :, 0:S], AX.X, ALU.add), ex, tally=s_sm)
            d = dve.do(lambda e, it: e.reciprocal(self_st[:, 2, :], self_st[:, 1, :]), d, tally=s_sm)
            for b in range(2):
                d2 = dve.do(lambda e, it, b=b: e.tensor_tensor(
                    SS[:, :, b, 0:S], SS[:, :, b, 0:S], r_[:, :, b:b + 1].to_broadcast([128, 8, S]),
                    ALU.mult), d, tally=s_sm)
            for j in range(8):
                y = pe.do(lambda e, it, j=j: e.transpose(
                    p.psum[2 + j // 4][:, 128 * (j % 4):128 * (j % 4) + 128],
                    SS[:, j].rearrange("p b q -> p (b q)"), ident), d2, before_trip(s_cp), tally=s_tp)
            for n in range(2):
                c = act.do(lambda e, it, n=n: e.copy(
                    ST[:, 4 * n:4 * n + 4, :], p.psum[2 + n][:, :].rearrange("p (j r) -> p j r", j=4)),
                    y, before_trip(s_cx), tally=s_cp)
            for b in range(2):
                for h in range(HEADS):
                    x = pe.do(lambda e, it, b=b, h=h: e.matmul(
                        p.psum[4 + b][64 * b:64 * b + 64, HD2 * h:HD2 * h + HD2],
                        ST[64 * b:64 * b + S, h // 2, 64 * (h % 2):64 * (h % 2) + 64],
                        VS[64 * b:64 * b + S, HD2 * h:HD2 * h + HD2], start=True, stop=True),
                        c, before_trip(s_out2), tally=s_cx, apart=True)
            for b in range(2):
                act.do(lambda e, it, b=b: e.copy(
                    CN[64 * b:64 * b + 64, bass.ds(pair(it), 1), :].rearrange("p o d -> p (o d)"),
                    p.psum[4 + b][64 * b:64 * b + 64, 0:D]), x, tally=s_out2)

        pair_attention(lambda it: 0, lambda sig: None)
        loop = p.open_loop(NT - 1)
        pair_attention(lambda it: it + 1, lambda sig: Point(sig, loop.at_start[sig], loop))
        p.close_loop(loop)
        p.join()

        for m in range(2):
            for t in range(NT):
                x = dve.do(lambda e, it, m=m, t=t: e.tensor_scalar(
                    XN[:, m, t, :], CN[:, t, :], expert[:, m, t:t + 1], None, ALU.mult))
        xs = transpose_in(2, None, None, x)
        for t in range(NT):
            i, bank, x = product([(XT[:, k, 128 * t:128 * t + 128], wden[:, k, :])
                                  for k in range(4)], D, *xs)
            p.bank_free[i] = residual(t, bank, x, None)
        xs = transposed_norm("rms", "L2_ln_post_cross_w", None, False, dve.last)
        cqT = A[:, 0:B * S]
        WM = A[:, 1024:3072].rearrange("p (h c) -> p h c", h=HEADS)
        wm = dve.do(lambda e, it: e.tensor_tensor(
            WM, wckT.rearrange("p (o c) -> p o c", o=1).to_broadcast([128, HEADS, C]),
            head8.rearrange("p (h o) -> p h o", o=1).to_broadcast([128, HEADS, C]), ALU.mult))
        for half in range(2):
            i, bank, x = product([(wcq[:, k, :], tokens(XT, k, half)) for k in range(2)], HALF * S, *xs)
            p.bank_free[i] = cq = scale_out(cqT[:, HALF * S * half:HALF * S * (half + 1)],
                                            bank[:, 0:HALF * S], CHD ** -0.5, x, q=dve)
        for h in range(HEADS):
            for half in range(2):
                i, bank, x = product([(WM[:, h, :], cqT[:, HALF * S * half:HALF * S * (half + 1)])],
                                     HALF * S, cq, wm)
                p.bank_free[i] = scale_out(head_queries(QO, half, h), real(bank[:, 0:HALF * S]), 1.0, x)
        p.join()
        cross_attention("l2", False)
        free = [q.last for q in p.queues[:4]]
        for m, e in enumerate("vl"):
            for g, n in enumerate(("gate", "up")):
                at_ = 4 * m + 2 * g
                load(wgu[:, at_:at_ + 2, :], io[f"L2_{e}_{n}"].rearrange("(k p) n -> p k n", p=128),
                     s_w["l2b"], *free)
            load(wdown[:, 6 * m:6 * m + 5, :],
                 io[f"L2_{e}_down"][0:640, :].rearrange("(k p) n -> p k n", p=128), s_w["l2b"])
            load(wdown[0:II - 640, 6 * m + 5, :], io[f"L2_{e}_down"][640:II, :], s_w["l2b"])
        w2b = Point(s_w["l2b"], s_w["l2b"].count)
        flat = A[:, 0:HEADS * (C + CHD)]
        CV = A[:, 0:HEADS * C].rearrange("p (h c) -> p h c", h=HEADS)
        z = pool.do(lambda e, it: e.memset(flat, 0.0))
        z = pool.do(lambda e, it: e.tensor_copy(
            flat.rearrange("p (h x) -> p h x", h=HEADS)[:, :, 0:CHD],
            wcv.rearrange("p (h x) -> p h x", h=HEADS)), z)
        cxT = A[:, 3072:3072 + B * PAD].rearrange("p (k n) -> p k n", k=1)
        zp = pool.do(lambda e, it: e.memset(
            A[:, 3072:3072 + B * PAD].rearrange("p (x q) -> p x q", q=PAD)[:, :, S:PAD], 0.0))
        for half in range(2):
            i, bank, x = product([(CV[:, h, :], head_queries(QO, half, h)) for h in range(HEADS)],
                                 HALF * S, z)
            p.bank_free[i] = cx = scale_out(tokens(cxT, 0, half), real(bank[:, 0:HALF * S]), 1.0, x,
                                            q=act)
        for t in range(NT):
            i, bank, x = product([(cxT[:, 0, 128 * t:128 * t + 128], wcd)], D, cx, zp)
            p.bank_free[i] = residual(t, bank, x, None)
        xs = transposed_norm("rms", "L2_ln_post_attn_w", None, True, dve.last)
        p.join()
        HT = A.rearrange("p (x n) -> p x n", x=12)
        z = pads(A, 12)
        for m in range(2):
            for n, (i0, rows) in enumerate(IT):
                for half in range(2):
                    dst = tokens(HT[0:rows], 6 * m + n, half)
                    i, bank, x = product([(wgu[:, 4 * m + k, i0:i0 + rows], tokens(XT, 2 * m + k, half))
                                          for k in range(2)], HALF * S, w2b, *xs, rows=rows)
                    p.bank_free[i] = g = act.do(lambda e, it, dst=dst, bank=bank, rows=rows: e.activation(
                        dst, real(bank[0:rows, 0:HALF * S]), ACT.Silu), x)
                    i, bank, x = product([(wgu[:, 4 * m + 2 + k, i0:i0 + rows],
                                           tokens(XT, 2 * m + k, half))
                                          for k in range(2)], HALF * S, rows=rows)
                    p.bank_free[i] = u = dve.do(lambda e, it, dst=dst, bank=bank, rows=rows: e.tensor_tensor(
                        dst, real(bank[0:rows, 0:HALF * S]), dst, ALU.mult), x, g)
        for t in range(NT):
            i, bank, x = product([(HT[0:rows, 6 * m + n, 128 * t:128 * t + 128],
                                   wdown[0:rows, 6 * m + n, :])
                                  for m in range(2) for n, (_, rows) in enumerate(IT)], D, u, z)
            p.bank_free[i] = residual(t, bank, x, None)
        p.join()

        load_gated_a(3, *[q.last for q in p.queues[:4]])
        gated_block(3)
        for par in range(2):
            done = load(out[par], X[64 * par:64 * par + S, :, :], s_out, dve.last)
        sp.do(None, done, quiet=True)

        with nc.Block() as block:
            for name, q in (("sync", sp), ("gpsimd", pool), ("scalar", act), ("tensor", pe),
                            ("vector", dve)):
                def run(eng, q=q):
                    emit(eng, q.items, q.step)
                {"sync": block.sync, "gpsimd": block.gpsimd, "scalar": block.scalar,
                 "tensor": block.tensor, "vector": block.vector}[name](run)


def natural(a):
    z = np.zeros((B, PAD) + a.shape[2:], a.dtype)
    z[:, :S] = a
    return np.ascontiguousarray(z.reshape(NT, 128, *a.shape[2:]).swapaxes(0, 1))


def kernel(**inputs):
    import concourse.bacc as bacc
    from concourse.bass_utils import run_bass_kernel_spmd

    g = {n: np.asarray(v) for n, v in inputs.items()}
    key_order = np.arange(KEYS).reshape(KP, KT).T.reshape(-1)
    pad_T = np.zeros((D, B, PAD), np.float32)
    pad_T[:, :, :S] = g["x"].transpose(2, 0, 1)
    types = np.zeros((B, 2, PAD), np.int32)
    types[:, 0, :S] = g["mask_BxS_ik0"]
    types[:, 1, :S - 1] = g["mask_BxS_ik0"][:, 1:]
    types[:, 0, S - 1] = 0
    angle = np.outer(np.arange(S, dtype=np.float32),
                     (1.0 / 10000.0 ** (np.arange(0, HD2, 2, dtype=np.float32) / HD2)).astype(np.float32))
    part = np.arange(128)
    a = {
        "x": natural(g["x"]),
        "xT": np.ascontiguousarray(pad_T.reshape(2, 128, B * PAD).swapaxes(0, 1)),
        "ctx": g["ctx_1024"],
        "ctxT": np.ascontiguousarray(g["ctx_1024"][:, key_order].transpose(0, 2, 1)),
        "mask": np.ascontiguousarray(g["mask_BxS2_bk0"][:, key_order]),
        "types": np.ascontiguousarray(types.reshape(NT, 2, 2, PAD).transpose(1, 3, 2, 0).reshape(128, 2, NT)),
        "pos": g["pos_1xS"],
        "W_mem": g["L0_xattn_W_mem"], "W_memT": np.ascontiguousarray(g["L0_xattn_W_mem"].T),
        "W_gateT": np.ascontiguousarray(g["L0_xattn_W_gate"].T),
        "b_gate": g["L0_xattn_b_gate"].reshape(1, D), "norm_w": g["L0_xattn_norm_w"].reshape(1, D),
        "vectors": np.ascontiguousarray(np.concatenate(
            [g[n.replace("_", "_xattn_", 1)].reshape(2, 128).T for n in VECTORS], axis=1)),
        "gates": np.concatenate([g[f"L{l}_xattn_{n}_gate"] for l in (1, 3) for n in ("attn", "ff")])
                   .reshape(1, 4),
        "ident": np.eye(128, dtype=np.float32),
        "rope": np.concatenate([np.cos(angle), np.cos(angle), -np.sin(angle), np.sin(angle)],
                               axis=1).astype(np.float32),
        "index": np.arange(S, dtype=np.float32).reshape(S, 1),
        "head16": ((part[:, None] // HD2 == np.arange(8)) * HD2 ** -0.5).astype(np.float32),
        "head8": (part[:, None] // CHD == np.arange(HEADS)).astype(np.float32),
        "causal": np.where(np.arange(S) <= part[:, None] % PAD, 0.0, -BIG).astype(np.float32),
        "L2_ckT": np.ascontiguousarray(g["L2_xattn_ckv_w"][:, :C].T),
    }
    for l in (1, 3):
        for n in ("Wq", "Wkv", "Wo", "W1", "W2"):
            a[f"L{l}_{n}"] = g[f"L{l}_xattn_{n}"]
        a[f"L{l}_WkT"] = np.ascontiguousarray(g[f"L{l}_xattn_Wkv"][:, :INNER].T)
    for n in ("v_qkv", "l_qkv", "v_dense", "l_dense", "cq_w", "ckv_w", "cdense_w", "v_gate", "v_up",
              "v_down", "l_gate", "l_up", "l_down"):
        a[f"L2_{n}"] = g[f"L2_xattn_{n}"]

    nc = bacc.Bacc("TRN2", target_bir_lowering=False, num_devices=1)
    io = {n: nc.dram_tensor(f"in_{n}", v.shape, mybir.dt.from_np(v.dtype), kind="ExternalInput").ap()
          for n, v in a.items()}
    out = nc.dram_tensor("out", (2, S, NT, D), F32, kind="ExternalOutput").ap()
    build(nc, io, out)
    r = run_bass_kernel_spmd(nc, [{f"in_{n}": v for n, v in a.items()}], core_ids=[0])
    o = r.results[0]["out"]
    return np.ascontiguousarray(o.transpose(2, 0, 1, 3).reshape(B, S, D))
```

```python
import numpy as np
import concourse.bass as bass
from concourse import mybir
from concourse.alu_op_type import AluOpType as ALU
from contextlib import ExitStack

F32 = mybir.dt.float32
F32R = mybir.dt.float32r
BF16 = mybir.dt.bfloat16
U8 = mybir.dt.uint8
I32 = mybir.dt.int32
ACT = mybir.ActivationFunctionType
AX = mybir.AxisListType

B, S, D, C, KEYS = 16, 56, 256, 128, 1500
PAD = 64
NT = B * PAD // 128
HEADS = 16
HQ = HEADS * S
RT = HQ // 128
KP, KT = 125, 12
CH = 3
CHK = KEYS // CH
DH = 64
INNER = HEADS * DH
FF = 4 * D
HD2, CHD = 16, 8
II = 688
IT = [(i, min(128, II - i)) for i in range(0, II, 128)]
VECTORS = [f"L{l}_{n}" for l in (1, 3) for n in ("ln_q_g", "ln_q_b", "ln_ff_g", "ln_ff_b")] + [
    "L2_ln_in_w", "L2_ln_post_attn_w", "L2_ln_post_cross_w"]
BIG = 3.3895313892515355e38
HALF = B // 2


class Tally:

    def __init__(self, handle):
        self.handle, self.count = handle, 0


class Point:

    def __init__(self, tally, value, loop=None):
        self.tally, self.value, self.loop = tally, value, loop


class Loop:
    def __init__(self, trips, tallies):
        self.trips, self.at_start, self.per = trips, {s: s.count for s in tallies}, {}

    def close(self):
        for s, c in self.at_start.items():
            self.per[s] = s.count - c
            s.count += (self.trips - 1) * self.per[s]


class Queue:

    def __init__(self, tally, step):
        self.step = step
        self.items, self.stack, self.tally, self.held, self.loop = [], [], tally, [], None
        self.last = None

    def do(self, fn, *waits, tally=None, by=1, quiet=False, apart=False):
        waits = self.held + list(waits)
        self.held = []
        s = None if quiet else (tally or self.tally)
        if s:
            s.count += by
        self.items.append((fn, [w for w in waits if w], s, by, apart))
        p = Point(s, s.count, self.loop) if s else None
        if p:
            self.last = p
        return p

    def wait(self, *points):
        self.held += list(points)


def emit(eng, items, step):

    def write(items, it, loop):
        waited = {}
        for item in items:
            if isinstance(item[0], Loop):
                with eng.Fori(0, item[0].trips) as i:
                    write(item[1], i, item[0])
                waited = {}
                continue
            fn, waits, s, by, apart = item
            need, on_register = {}, False
            for w in waits:
                per, value = 0, w.value
                if w.loop is not None:
                    per = w.loop.per[w.tally]
                    if w.loop is not loop:
                        value, per = value + (w.loop.trips - 1) * per, 0
                assert value > 0 or not per
                key = (w.tally, per)
                need[key] = max(need.get(key, 0), value)
            for (sig, per), value in need.items():
                if waited.get((sig, per), -1) >= value:
                    continue
                waited[(sig, per)] = value
                eng.wait_ge(sig.handle, it * per + value if per else value)
                on_register = on_register or (per and loop is not None)
            if on_register and apart:
                eng.sem_inc(step.handle, 1)
            if fn is None:
                continue
            ins = fn(eng, it)
            if s:
                ins.then_inc(s.handle, by)

    write(items, 0, None)


class Program:

    def __init__(self, nc, ctx):
        self.nc, self.ctx, self.tallies = nc, ctx, []
        self.pe, self.act, self.dve, self.pool, self.sp = (
            Queue(self.tally(n), self.tally(n + "_step"))
            for n in ("s_pe", "s_act", "s_dve", "s_pool", "s_sp"))
        self.queues = [self.pe, self.act, self.dve, self.pool, self.sp]
        self.psum = [ctx.enter_context(nc.psum_tensor(f"bank{i}", [128, 512], F32)) for i in range(8)]
        self.bank_free = [None] * 8
        self.next_bank = 0

    def tally(self, name):
        s = Tally(self.ctx.enter_context(self.nc.semaphore(name)))
        self.tallies.append(s)
        return s

    def sbuf(self, name, width, dt=F32, scope=None):
        return (scope or self.ctx).enter_context(self.nc.sbuf_tensor(name, [128, width], dt))[:, :]

    def join(self, *more):
        last = [q.last for q in self.queues[:4]]
        for q in self.queues[:4]:
            q.wait(*last, *more)
        return last

    def bank(self):
        i = self.next_bank
        self.next_bank = (i + 1) % 8
        return i, self.psum[i], self.bank_free[i]

    def open_loop(self, trips):
        loop = Loop(trips, self.tallies)
        for q in self.queues:
            q.stack.append(q.items)
            q.items, q.loop = [], loop
        return loop

    def close_loop(self, loop):
        loop.close()
        for q in self.queues:
            body, q.items = q.items, q.stack.pop()
            q.items.append((loop, body))
            q.loop = None


def view(ap, dims, **sizes):
    return ap.rearrange(dims, **sizes)


def build(nc, io, out):
    ctx = ExitStack()
    with ctx:
        p = Program(nc, ctx)
        pe, act, dve, pool, sp = p.queues

        X = p.sbuf("x_nat", NT * D).rearrange("p (t d) -> p t d", t=NT)
        QO_flat = p.sbuf("q_and_o", B * HQ)
        QO = QO_flat.rearrange("p (b r) -> p b r", b=B)
        kt_raw = p.sbuf("ctx_T", KEYS)
        kn_raw = p.sbuf("ctx_nat", KT * C)
        mask_raw = p.sbuf("mask_bytes", KEYS, U8)
        value_w = p.sbuf("value_weights", INNER)
        ident = p.sbuf("ident", 128)
        vecs = p.sbuf("vectors", 2 * len(VECTORS))
        gates = p.sbuf("gates", 4)
        mv = p.sbuf("stats", NT * 6).rearrange("p (t s) -> p t s", t=NT)
        mean_var = p.sbuf("mean_var", NT * 2).rearrange("p (t s) -> p t s", t=NT)
        st = p.sbuf("row_stats", 8 * NT).rearrange("p (a t) -> p a t", t=NT)
        expert = p.sbuf("expert", 2 * NT).rearrange("p (a t) -> p a t", t=NT)
        rope = p.sbuf("rope", 2 * HD2)
        causal = p.sbuf("causal", S)
        head8 = p.sbuf("head8", HEADS)
        head16 = p.sbuf("head16", 8)
        mx = p.sbuf("row_max", 2 * 8).rearrange("p (a c) -> p a c", a=2)
        self_st = p.sbuf("self_stats", 2 * 3 * 16).rearrange("p (i k c) -> p i k c", i=2, k=3)

        dense = ExitStack()
        XT = p.sbuf("x_T", 4 * B * PAD, scope=dense).rearrange("p (k n) -> p k n", k=4)
        A = p.sbuf("area", 12 * B * PAD, scope=dense)
        W = p.sbuf("weights", 10240, scope=dense)
        small = p.sbuf("small", 640, scope=dense)
        dense.close()
        l0_p_T = [A[:, i * 3072:(i + 1) * 3072].rearrange("p (k c) -> p k c", k=KT) for i in range(2)]
        l0_scores = [A[:, 6144 + i * KEYS:6144 + (i + 1) * KEYS] for i in range(2)]
        l0_zeros = A[:, 9144:9144 + KEYS]

        att = ExitStack()

        def parts(name, width):
            return [[p.sbuf(f"{name}_{part}{i}", width, F32R, scope=att) for i in range(2)]
                    for part in ("high", "low")]

        KTs, KNs, QSs = parts("keys_T", KEYS), parts("keys_nat", KT * C), parts("q_stage", 256)
        PTs = [[x.rearrange("p (k c) -> p k c", k=KT) for x in both] for both in parts("p_T", KT * 256)]
        SB = [p.sbuf(f"scores{i}", KEYS, scope=att) for i in range(2)]
        MB = [p.sbuf(f"mask{i}", KEYS, BF16, scope=att) for i in range(2)]
        diagonal = [p.sbuf(f"diagonal{i}", 128, scope=att) for i in range(2)]
        inverse = [p.sbuf(f"inverse{i}", 256, scope=att) for i in range(2)]
        ones = p.sbuf("ones", 128, scope=att)
        att.close()

        s_const = p.tally("s_const")
        s_w = {n: p.tally(f"s_w_{n}") for n in ("l0", "l0b", "l1a", "l1b", "l2q", "l2a", "l2b", "l3a", "l3b")}
        s_out = p.tally("s_out")

        def load(dst, src, sig, *waits):
            return sp.do(lambda e, it: e.dma_start(dst, src), *waits, tally=sig, by=16)

        def vec(name, k):
            c = 2 * VECTORS.index(name) + k
            return vecs[:, c:c + 1]

        L0W = W[:, 8192:10240]
        w_mem = L0W[:, 0:2 * C].rearrange("p (k c) -> p k c", k=2)
        w_memT = L0W[:, 256:512]
        w_gateT = L0W[:, 512:1536].rearrange("p (k n) -> p k n", k=4)
        b_gate = L0W[:, 1536:1792]
        norm_w = L0W[:, 1792:2048]
        x0T = XT[:, 0:2, :].rearrange("p k (b q) -> p k b q", b=B)

        load(w_mem, io["W_mem"].rearrange("(k p) c -> p k c", p=128), s_w["l0"])
        load(XT[:, 0:2, :], io["xT"], s_w["l0"])
        load(ident, io["ident"], s_w["l0"])

        def gated_names(l):
            return {n: f"L{l}_{n}" for n in ("ln_q_g", "ln_q_b", "ln_ff_g", "ln_ff_b")}

        ctx_rows = io["ctx"].rearrange("b (p k) c -> b p (k c)", p=KP)

        def memory_attention(tag, per_trip, units, groups, q_src, dest, kt_buf, kn_buf, copy_q, peel):
            nb, U, G = per_trip, len(units), len(groups)
            trips = B // nb
            kt_sig = [p.tally(f"s_{tag}_kt{i}") for i in range(nb)]
            kn_sig = [p.tally(f"s_{tag}_kn{i}") for i in range(nb)]
            s_q = p.tally(f"s_{tag}_q")
            s_sc = p.tally(f"s_{tag}_scores")
            s_mx = p.tally(f"s_{tag}_max")
            s_ex = p.tally(f"s_{tag}_exp")
            s_nm = p.tally(f"s_{tag}_norm")
            s_rc = p.tally(f"s_{tag}_recip")
            s_nx = p.tally(f"s_{tag}_negmax")
            s_tr = p.tally(f"s_{tag}_transposed")
            s_ea = p.tally(f"s_{tag}_evac_act")
            s_ed = p.tally(f"s_{tag}_evac_dve")
            s_pv = p.tally(f"s_{tag}_sums")
            s_ov = p.tally(f"s_{tag}_o_out")
            group_of, col_of = {}, {}
            for g, (us, _, _) in enumerate(groups):
                for n, u in enumerate(us):
                    group_of[u], col_of[u] = g, 128 * n
            last_unit = {b: max(u for u in range(U) for x in units[u] if x[2] == b) for b in range(nb)}
            first_unit = {b: min(u for u in range(U) for x in units[u] if x[2] == b) for b in range(nb)}
            last_group = {b: max(g for g in range(G) for x in groups[g][2] if x[0] == b)
                          for b in range(nb)}
            rows_free = {b: groups[last_group[b]][1][-1] - U for b in range(nb)}

            def trip(depth, drain, carried, loop, index):
                now, missed, first = {}, set(), depth == 0

                def at(name, i):
                    if (name, i) in now:
                        return now[(name, i)]
                    if (name, i) in carried:
                        c = carried[(name, i)]
                        return Point(c.tally, c.value, loop) if loop else c
                    missed.add((name, i))
                    return None

                def loads(b):
                    def batch(it):
                        return index(it) * nb + b

                    scores_done = at("scores", last_unit[b] - U)
                    now[("kt", b)] = sp.do(
                        lambda e, it: e.dma_start(
                            kt_buf(b), io["ctxT"][bass.ds(batch(it), 1)].rearrange("o c k -> (o c) k")),
                        scores_done, tally=kt_sig[b], by=16, apart=True)

                def load_rows(b):
                    def batch(it):
                        return index(it) * nb + b

                    sums_done = at("sums", last_group[b] - G)
                    for lo, hi in ((0, 112), (112, KP)):
                        now[("kn", b)] = act.do(
                            lambda e, it, lo=lo, hi=hi: e.dma_start(
                                kn_buf(b)[lo:hi, :],
                                ctx_rows[bass.ds(batch(it), 1), lo:hi, :]
                                .rearrange("o p n -> (o p) n")),
                            sums_done, tally=kn_sig[b], by=16, apart=True)

                def stage(b):
                    now[("q", b)] = pool.do(
                        lambda e, it: copy_q(e, b, index(it)),
                        at("scores", last_unit[b] - U), tally=s_q)

                def scores(u):
                    for c in range(CH):
                        for n, (row, m, b, q0) in enumerate(units[u]):
                            now[("scores", u)] = now[("scores%d" % c, u)] = pe.do(
                                lambda e, it, c=c, row=row, m=m, b=b, q0=q0: e.matmul(
                                    p.psum[c][row:row + m, 0:CHK], q_src(b)[:, q0:q0 + m],
                                    kt_buf(b)[:, c * CHK:(c + 1) * CHK], start=True, stop=True),
                                at("kt", b), at("q", b), at("max%d" % c, u - 1),
                                tally=s_sc)

                def maxima(u):
                    for c in range(CH):
                        now[("max", u)] = now[("max%d" % c, u)] = dve.do(
                            lambda e, it, c=c: e.tensor_tensor_reduce(
                                out=l0_scores[u % 2][:, c * CHK:(c + 1) * CHK], in0=p.psum[c][:, 0:CHK],
                                in1=l0_zeros[:, c * CHK:(c + 1) * CHK], scale=1.0, scalar=-BIG,
                                op0=ALU.add, op1=ALU.max, accum_out=mx[:, u % 2, c:c + 1]),
                            at("scores%d" % c, u),
                            at("transposed", u - 2), at("exp", u - 2), tally=s_mx, apart=True)
                    now[("negmax", u)] = dve.do(
                        lambda e, it: e.tensor_reduce(mx[:, u % 2, 3:4], mx[:, u % 2, 0:3], AX.X,
                                                      ALU.max, negate=True),
                        now[("max", u)], tally=s_nx)

                def exponentials(u):
                    now[("exp", u)] = act.do(
                        lambda e, it: e.activation(l0_scores[u % 2], l0_scores[u % 2], ACT.Exp,
                                                   bias=mx[:, u % 2, 3:4],
                                                   accum_out=mx[:, u % 2, 4:5]),
                        at("negmax", u), tally=s_ex)

                def normalise(u):
                    now[("recip", u)] = dve.do(
                        lambda e, it: e.reciprocal(mx[:, u % 2, 5:6], mx[:, u % 2, 4:5]),
                        at("exp", u), tally=s_rc)
                    now[("norm", u)] = dve.do(
                        lambda e, it: e.tensor_scalar(l0_scores[u % 2], l0_scores[u % 2],
                                                      mx[:, u % 2, 5:6], None,
                                                      ALU.mult),
                        now[("recip", u)], tally=s_nm)

                def transposes(u):
                    for c in range(CH):
                        for k in range(4):
                            x = pe.do(
                                lambda e, it, c=c, k=k: e.transpose(
                                    p.psum[3 + c][0:KP, 128 * k:128 * k + 128],
                                    l0_scores[u % 2][:, (4 * c + k) * KP:(4 * c + k + 1) * KP], ident),
                                at("norm", u), at("evac%d" % c, u - 1),
                                tally=s_tr, quiet=(k < 3))
                        now[("transposed", u)] = now[("transposed%d" % c, u)] = x

                def evacuate(u, c):
                    g = group_of[u % U]
                    gi = g if u >= 0 else g - G
                    dst = l0_p_T[g % 2][0:KP, 4 * c:4 * c + 4, col_of[u % U]:col_of[u % U] + 128]
                    src = p.psum[3 + c][0:KP, :].rearrange("p (k r) -> p k r", k=4)
                    if c < 2:
                        fn, q, s = (lambda e, it: e.copy(dst, src)), act, s_ea
                    else:
                        fn, q, s = (lambda e, it: e.tensor_copy(dst, src)), dve, s_ed
                    now[("evac%d" % c, u)] = q.do(fn, at("transposed%d" % c, u), at("sums", gi - 2),
                                                  tally=s)

                def sums(g, part, parts):
                    us, _, work = groups[g % G]
                    todo = [(k, w) for w in work for k in range(KT)]
                    n = len(todo)
                    for i in range(n * part // parts, n * (part + 1) // parts):
                        k, (b, c0, width, o0) = todo[i]
                        bi, ui = b + (g // G) * nb, us[-1] + (g // G) * U
                        x = pe.do(
                            lambda e, it, k=k, b=b, c0=c0, width=width, o0=o0: e.matmul(
                                p.psum[6 + g % 2][:, o0:o0 + width], kn_buf(b)[0:KP, k * C:(k + 1) * C],
                                l0_p_T[g % 2][0:KP, k, c0:c0 + width], start=(k == 0), stop=(k == KT - 1)),
                            at("kn", bi), at("evac%d" % (k // 4), ui),
                            at("o_out", g - 2), tally=s_pv, quiet=(i < n - 1))
                    if part == parts - 1:
                        now[("sums", g)] = x

                def o_out(g):
                    work = groups[g % G][2]
                    width = max(o0 + w for _, _, w, o0 in work)
                    back = -(g // G)
                    now[("o_out", g)] = dve.do(
                        lambda e, it: e.tensor_copy(dest(g % G, index(it) - back),
                                                    p.psum[6 + g % 2][:, 0:width]),
                        at("sums", g), tally=s_ov)

                def in_slot(s):
                    for g, (_, slots, _) in enumerate(groups):
                        for n, x in enumerate(slots):
                            for back in range(min(depth, 2) + 1):
                                if x == s + back * U:
                                    yield g - back * G, n, len(slots)

                def out_in_slot(s):
                    for g, (_, slots, _) in enumerate(groups):
                        for back in range(min(depth, 2) + 1):
                            if slots[-1] + 1 == s + back * U:
                                yield g - back * G

                slots_here = max(x[1][-1] for x in groups) + 2 - U if drain else U
                if not drain:
                    for b in range(nb):
                        loads(b)
                        if first or rows_free[b] < 0:
                            load_rows(b)
                for s in range(slots_here):
                    if not drain:
                        for b in range(nb):
                            if first_unit[b] == s:
                                stage(b)
                        scores(s)
                        maxima(s)
                        exponentials(s)
                    for g, part, parts in in_slot(s):
                        if g < 0 or not drain:
                            sums(g, part, parts)
                    for b in range(nb):
                        if not (first or drain) and rows_free[b] == s:
                            load_rows(b)
                    for g in out_in_slot(s):
                        if g < 0 or not drain:
                            o_out(g)
                    if not drain:
                        normalise(s)
                    if (s == 0 and not first) or (s > 0 and not drain):
                        transposes(s - 1)
                        for c in range(CH):
                            evacuate(s - 1, c)
                return now, missed

            def shifted(now):
                size = {"q": nb, "kt": nb, "kn": nb, "sums": G, "o_out": G}
                return {(n, i - size.get(n, U)): v for (n, i), v in now.items()}

            carried = {}
            for j in range(peel):
                before = carried
                now, _ = trip(j, False, carried, None, lambda it, j=j: j)
                carried = {**{(n, i - {"q": nb, "kt": nb, "kn": nb, "sums": G,
                                       "o_out": G}.get(n, U)): v for (n, i), v in before.items()},
                           **shifted(now)}
            loop = p.open_loop(trips - peel)
            now, missed = trip(peel, False, carried, loop, lambda it: it + peel)
            p.close_loop(loop)
            after = shifted(now)
            for key, point in after.items():
                assert key not in missed, key
                if key in carried:
                    assert point.value == carried[key].value + loop.per[point.tally], key
            trip(trips, True, after, None, lambda it: trips)
            p.join()

        raw_free = {"kt": None, "kn": None, "mask": None}
        GROUPS = [[2 * g + n for n in range(2) if 2 * g + n < RT] for g in range((RT + 1) // 2)]
        NG = len(GROUPS)

        def cross_attention(tag, masked):
            nb, U, G, trips = 2, 2 * RT, 2 * NG, B // 2
            s_ktl, s_knl, s_ml = (p.tally(f"s_{tag}_{n}_loaded") for n in ("keysT", "keys", "mask"))
            s_kt, s_kn, s_mb, s_q = (p.tally(f"s_{tag}_{n}") for n in ("keysT", "keys", "mask", "q"))
            s_sc, s_mx, s_nx = (p.tally(f"s_{tag}_{n}") for n in ("scores", "max", "negmax"))
            s_ex, s_rc, s_dg = (p.tally(f"s_{tag}_{n}") for n in ("exp", "recip", "diagonal"))
            s_tr, s_eh, s_el = (p.tally(f"s_{tag}_{n}") for n in ("transposed", "high", "low"))
            s_sh, s_sl = (p.tally(f"s_{tag}_{n}") for n in ("first_high", "first_low"))
            s_pv, s_os, s_ov = (p.tally(f"s_{tag}_{n}") for n in ("sums", "o_sum", "o_out"))
            s_sp, s_in = (p.tally(f"s_{tag}_{n}") for n in ("spread", "inverse"))
            size = {"scores": U, "max": U, "negmax": U, "exp": U, "recip": U, "diagonal": U,
                    "spread": G, "inverse": G,
                    "transposed": U, "high": U, "low": U, "sums": G, "o_out": G, "q": G}
            slots_of = [[3 + u for u in us] for us in GROUPS]
            kn_slots = range(3, 3 + CH)

            def group_of(u):
                return u // RT * NG + (u % RT) // 2

            def shifted(now):
                return {(n, i - size.get(n.rstrip("012"), nb)): v for (n, i), v in now.items()}

            def trip(carried, loop, index, kind):
                now, missed = {}, set()

                def at(name, i):
                    if (name, i) in now:
                        return now[(name, i)]
                    if (name, i) in carried:
                        c = carried[(name, i)]
                        return Point(c.tally, c.value, loop) if loop else c
                    missed.add((name, i))
                    return None

                def batch(it, v):
                    return bass.ds(index(it) * nb + v, 1)

                def load_kt(v):
                    now[("kt_raw", v)] = sp.do(
                        lambda e, it: e.dma_start(
                            kt_raw, io["ctxT"][batch(it, v)].rearrange("o c k -> (o c) k")),
                        at("kt2", v - 1), raw_free["kt"] if kind == "start" else None,
                        tally=s_ktl, by=16, apart=True)

                def load_kn(v):
                    for lo, hi in ((0, 112), (112, KP)):
                        now[("kn_raw", v)] = sp.do(
                            lambda e, it, lo=lo, hi=hi: e.dma_start(
                                kn_raw[lo:hi, :],
                                ctx_rows[batch(it, v), lo:hi, :].rearrange("o p n -> (o p) n")),
                            at("kn2", v - 1), raw_free["kn"] if kind == "start" else None,
                            tally=s_knl, by=16, apart=True)

                def load_mask(v):
                    if masked:
                        now[("mask_raw", v)] = sp.do(
                            lambda e, it: e.dma_start(
                                mask_raw, io["mask"][batch(it, v), :].to_broadcast([128, KEYS])),
                            at("mask", v - 1), raw_free["mask"] if kind == "start" else None,
                            tally=s_ml, by=16, apart=True)

                def cut(high, low, src, sig, *waits, moving=False):
                    if kind == "start":
                        h = act.do(lambda e, it: e.copy(high, src(it)), *waits, tally=s_sh)
                        return dve.do(lambda e, it: e.tensor_tensor(
                            low, src(it), high.bitcast(F32), ALU.subtract), h, tally=s_sl)
                    if moving:
                        h = pool.do(lambda e, it: e.tensor_copy(high, src(it)), *waits, tally=sig)
                    else:
                        h = pool.do(lambda e, it: e.tensor_scalar(high, src(it), 1.0, 1.0,
                                                                  ALU.mult, ALU.mult),
                                    *waits, tally=sig, apart=True)
                    return pool.do(lambda e, it: e.tensor_tensor(
                        low, src(it), high.bitcast(F32), ALU.subtract), h, tally=sig, apart=True)

                def cut_kt(v, c):
                    cols = slice(c * CHK, (c + 1) * CHK)
                    now[("kt%d" % c, v)] = cut(
                        KTs[0][v % 2][:, cols], KTs[1][v % 2][:, cols], lambda it: kt_raw[:, cols], s_kt,
                        at("kt_raw", v), at("scores", (v - 1) * RT - 1))

                def cut_kn(v, c):
                    cols = slice(4 * c * C, 4 * (c + 1) * C)
                    now[("kn%d" % c, v)] = cut(
                        KNs[0][v % 2][0:KP, cols], KNs[1][v % 2][0:KP, cols],
                        lambda it: kn_raw[0:KP, cols], s_kn,
                        at("kn_raw", v), at("sums", (v - 1) * NG - 1))

                def cut_q(g):
                    v, us = g // NG, GROUPS[g % NG]
                    lo, n = 128 * us[0], 128 * len(us)
                    now[("q", g)] = cut(
                        QSs[0][g % 2][:, 0:n], QSs[1][g % 2][:, 0:n],
                        lambda it: QO[:, batch(it, v), lo:lo + n].rearrange("p o r -> p (o r)"), s_q,
                        at("scores", (g - 2) // NG * RT + GROUPS[(g - 2) % NG][-1]), moving=True)

                def bias(v):
                    if masked:
                        now[("mask", v)] = pool.do(
                            lambda e, it: e.tensor_scalar(MB[v % 2], mask_raw, -1.0, BIG,
                                                          ALU.add, ALU.mult),
                            at("mask_raw", v), at("max", (v - 1) * RT - 1), tally=s_mb, apart=True)


                def scores(u):
                    g, b = group_of(u), u // RT
                    lo = 128 * ((u % RT) % 2)
                    for c in range(CH):
                        cols = slice(c * CHK, (c + 1) * CHK)
                        for n, (i, j) in enumerate(((0, 0), (0, 1), (1, 0))):
                            x = pe.do(lambda e, it, c=c, i=i, j=j, n=n, cols=cols: e.matmul(
                                p.psum[c][:, 0:CHK], QSs[i][g % 2][:, lo:lo + 128], KTs[j][b][:, cols],
                                start=(n == 0), stop=(n == 2)),
                                at("kt%d" % c, b), at("q", g), at("max%d" % c, u - 1),
                                tally=s_sc, quiet=(n < 2))
                        now[("scores", u)] = now[("scores%d" % c, u)] = x

                def maxima(u):
                    b = u // RT
                    mb = MB[b] if masked else MB[0]
                    for c in range(CH):
                        now[("max", u)] = now[("max%d" % c, u)] = dve.do(
                            lambda e, it, c=c: e.tensor_tensor_reduce(
                                out=SB[u % 2][:, c * CHK:(c + 1) * CHK], in0=p.psum[c][:, 0:CHK],
                                in1=mb[:, c * CHK:(c + 1) * CHK], scale=1.0, scalar=-BIG,
                                op0=ALU.add, op1=ALU.max, accum_out=mx[:, u % 2, c:c + 1]),
                            at("scores%d" % c, u), at("mask", b if masked else 0),
                            at("transposed", u - 2), at("exp", u - 2), tally=s_mx, apart=True)
                    now[("negmax", u)] = dve.do(
                        lambda e, it: e.tensor_reduce(mx[:, u % 2, 3:4], mx[:, u % 2, 0:3], AX.X,
                                                      ALU.max, negate=True),
                        now[("max", u)], tally=s_nx)

                def exponentials(u):
                    now[("exp", u)] = act.do(
                        lambda e, it: e.activation(SB[u % 2], SB[u % 2], ACT.Exp,
                                                   bias=mx[:, u % 2, 3:4],
                                                   accum_out=mx[:, u % 2, 4:5]),
                        at("negmax", u), tally=s_ex)

                def reciprocals(u):
                    now[("recip", u)] = dve.do(
                        lambda e, it: e.reciprocal(mx[:, u % 2, 5:6], mx[:, u % 2, 4:5]),
                        at("exp", u), at("diagonal", u - 2), tally=s_rc)
                    now[("diagonal", u)] = act.do(
                        lambda e, it: e.activation(diagonal[u % 2], ident, ACT.Copy,
                                                   scale=mx[:, u % 2, 5:6]),
                        now[("recip", u)], at("spread", group_of(u - 2)), tally=s_dg)

                def spread(g):
                    us, bank = GROUPS[g % NG], p.psum[6 + g % 2]
                    n = 128 * len(us)
                    for i, u in enumerate(us):
                        u += g // NG * RT
                        x = pe.do(
                            lambda e, it, i=i, u=u: e.matmul(
                                bank[:, 128 * i:128 * i + 128], ones, diagonal[u % 2],
                                start=True, stop=True),
                            at("diagonal", u), at("o_out", g - 2), tally=s_sp)
                    now[("spread", g)] = x
                    now[("inverse", g)] = act.do(
                        lambda e, it: e.copy(inverse[g % 2][:, 0:n], bank[:, 0:n]), x, tally=s_in)

                def transposes(u):
                    for c in range(CH):
                        for k in range(4):
                            x = pe.do(
                                lambda e, it, c=c, k=k: e.transpose(
                                    p.psum[3 + c][0:KP, 128 * k:128 * k + 128],
                                    SB[u % 2][:, (4 * c + k) * KP:(4 * c + k + 1) * KP], ident),
                                at("exp", u), at("low%d" % c, u - 1),
                                tally=s_tr, quiet=(k < 3))
                        now[("transposed", u)] = now[("transposed%d" % c, u)] = x

                def evacuate(u, c):
                    g = group_of(u)
                    lo = 128 * ((u % RT) % 2)
                    high, low = (PTs[i][g % 2][0:KP, 4 * c:4 * c + 4, lo:lo + 128] for i in range(2))
                    if len(GROUPS[g % NG]) == 1:
                        low = PTs[0][g % 2][0:KP, 4 * c:4 * c + 4, 128:256]
                    src = p.psum[3 + c][0:KP, :].rearrange("p (k r) -> p k r", k=4)
                    h = act.do(lambda e, it: e.copy(high, src),
                               at("transposed%d" % c, u), at("sums", g - 2), tally=s_eh)
                    now[("low%d" % c, u)] = now[("low", u)] = dve.do(
                        lambda e, it: e.tensor_tensor(low, src, high.bitcast(F32), ALU.subtract),
                        h, tally=s_el)

                def sums(g, part, of):
                    us = GROUPS[g % NG]
                    b, last_u = g // NG, g // NG * RT + us[-1]
                    steps = ((0, 0), (0, 1), (1, 0)) if len(us) == 2 else ((0, 0), (1, 0))
                    for k in range(KT * part // of, KT * (part + 1) // of):
                        cols = slice(k * C, (k + 1) * C)
                        for n, (i, j) in enumerate(steps):
                            stop = k == KT - 1 and n == len(steps) - 1
                            x = pe.do(
                                lambda e, it, k=k, i=i, j=j, n=n, cols=cols, stop=stop: e.matmul(
                                    p.psum[6 + g % 2][:, 0:256], KNs[i][b % 2][0:KP, cols],
                                    PTs[j][g % 2][0:KP, k, :], start=(k == 0 and n == 0),
                                    stop=stop),
                                at("kn%d" % (k // 4), b), at("low%d" % (k // 4), last_u), at("inverse", g),
                                tally=s_pv, quiet=not stop)
                    if part == of - 1:
                        now[("sums", g)] = x

                def o_out(g):
                    us = GROUPS[g % NG]
                    lo, n = 128 * us[0], 128 * len(us)
                    bank, x = p.psum[6 + g % 2], at("sums", g)
                    src = bank[:, 0:n]
                    if len(us) == 1:
                        src = inverse[g % 2][:, 128:256]
                        x = dve.do(lambda e, it: e.tensor_copy(src, bank[:, 128:256]), x, tally=s_os)
                        x = dve.do(lambda e, it: e.tensor_tensor(src, bank[:, 0:128], src, ALU.add),
                                   x, tally=s_os, apart=True)
                    now[("o_out", g)] = dve.do(
                        lambda e, it: e.tensor_tensor(
                            QO[:, batch(it, g // NG), lo:lo + n].rearrange("p o r -> p (o r)"),
                            src, inverse[g % 2][:, 0:n], ALU.mult),
                        x, at("inverse", g), tally=s_ov, apart=True)

                if kind == "start":
                    load_kt(0), load_kn(0), load_mask(0)
                    now[("ones", 0)] = pool.do(lambda e, it: e.memset(ones, 1.0), tally=s_q)
                    if not masked:
                        now[("mask", 0)] = now[("mask", -nb)] = pool.do(
                            lambda e, it: e.memset(MB[0], 0.0), tally=s_mb)
                    cut_kt(0, 0), cut_q(0), bias(0), cut_kt(0, 1), cut_kt(0, 2)
                    load_kt(1), load_mask(1)
                    for c in range(CH):
                        cut_kn(0, c)
                    load_kn(1)
                    return now, missed
                first, last, drain = kind == "first", kind == "last", kind == "drain"
                work = {}
                for g in range(0 if first else -NG, 0 if drain else G):
                    ss = [g // NG * RT + x for x in slots_of[g % NG]]
                    for n, x in enumerate(ss):
                        if 0 <= x < (3 if drain else U):
                            work.setdefault(x, []).append((g, n, len(ss)))
                for s in range(3 if drain else U):
                    b, j = s // RT, s % RT
                    ahead = not drain and not (last and b == nb - 1)
                    ahead2 = not drain and not last
                    before = s > 0 if first else s == 0 if drain else True
                    if not drain:
                        scores(s)
                        maxima(s)
                    if before:
                        reciprocals(s - 1)
                    for g, n, of in work.get(s, []):
                        sums(g, n, of)
                        if n == of - 1:
                            o_out(g)
                    if before:
                        transposes(s - 1)
                        for c in range(CH):
                            evacuate(s - 1, c)
                        if (s - 1) % RT % 2 == 1 or (s - 1) % RT == RT - 1:
                            spread(group_of(s - 1))
                    if not drain:
                        exponentials(s)
                    if not drain:
                        if j % 2 == 0 and (ahead or j // 2 < NG - 1):
                            cut_q(b * NG + j // 2 + 1)
                        if j < CH and ahead:
                            cut_kt(b + 1, j)
                        if j in kn_slots and ahead:
                            cut_kn(b + 1, j - 3)
                        if j == RT - 1 and ahead:
                            bias(b + 1)
                        if ahead2 and j == CH - 1:
                            load_kt(b + 2)
                        if ahead2 and j == kn_slots[-1]:
                            load_kn(b + 2)
                        if ahead2 and j == RT - 1:
                            load_mask(b + 2)
                return now, missed

            def whole(index, kind, carried):
                now, _ = trip(carried, None, index, kind)
                return {**shifted(carried), **shifted(now)}

            carried, _ = trip({}, None, lambda it: 0, "start")
            carried = whole(lambda it: 0, "first", carried)
            loop = p.open_loop(trips - 2)
            now, missed = trip(carried, loop, lambda it: it + 1, "more")
            p.close_loop(loop)
            after = shifted(now)
            for key, point in after.items():
                assert key not in missed, key
                if key in carried:
                    assert point.value == carried[key].value + loop.per[point.tally], key
            if not masked:
                after[("mask", 0)] = carried[("mask", -nb)]
            after = whole(lambda it: trips - 1, "last", after)
            raw_free["kt"], raw_free["kn"] = after[("kt2", -1)], after[("kn2", -1)]
            if masked:
                raw_free["mask"] = after[("mask", -1)]
            trip(after, None, lambda it: trips, "drain")
            p.join()

        turn = [0]

        def either(*engines):
            turn[0] += 1
            return (act, dve)[turn[0] % 2]

        def scale_out(dst, src, scale, *waits, q=None):
            q = q or either()
            if q is act:
                return act.do(lambda e, it: e.activation(dst, src, ACT.Copy, scale=scale), *waits)
            return dve.do(lambda e, it: e.tensor_scalar(dst, src, scale, None, ALU.mult), *waits)

        def product(steps, width, *waits, rows=128, row0=0, shape=None):
            i, bank, free = p.bank()
            for n, (lhsT, rhs) in enumerate(steps):
                o = bank[row0:row0 + rows, 0:width]
                x = pe.do(lambda e, it, lhsT=lhsT, rhs=rhs, o=o, n=n: e.matmul(
                    o, lhsT, rhs, start=(n == 0), stop=(n == len(steps) - 1)),
                    free, *waits, quiet=(n < len(steps) - 1))
            return i, bank, x

        def tokens(arr, k, half):
            return arr[:, k, :].rearrange("p (b q) -> p b q", b=B)[:, HALF * half:HALF * half + HALF, 0:S]

        def real(ap):
            return ap.rearrange("p (b q) -> p b q", q=S)

        def rstd(src, eps, scale, *waits):
            a = dve.do(lambda e, it: e.tensor_scalar(st[:, 0, :], src, scale, eps, ALU.mult, ALU.add),
                       *waits)
            r = act.do(lambda e, it: e.activation(st[:, 1, :], st[:, 0, :], ACT.Sqrt), a)
            return dve.do(lambda e, it: e.reciprocal(st[:, 2, :], st[:, 1, :]), r)

        XN = A[:, 8192:12288].rearrange("p (k t d) -> p k t d", k=2, t=NT)

        def tile_stats(kind, t, x):
            if kind == "layer":
                a = dve.do(lambda e, it: e.bn_stats(mv[:, t, :], X[:, t, :]), x)
                return dve.do(lambda e, it: e.bn_aggr(mean_var[:, t, :], mv[:, t, :]), a)
            return dve.do(lambda e, it: e.tensor_tensor_reduce(
                out=XN[:, 1, t, :], in0=X[:, t, :], in1=X[:, t, :], scale=1.0, scalar=0.0,
                op0=ALU.mult, op1=ALU.add, accum_out=st[:, 3, t:t + 1]), x)

        def transposed_norm(kind, g, bias, masked, stats):
            if kind == "layer":
                r = rstd(mean_var[:, :, 1], 1e-5, 1.0, stats)
            else:
                r = rstd(st[:, 3, :], 1e-6, 1.0 / D, stats)
            if masked:
                for m in range(2):
                    r2 = dve.do(lambda e, it, m=m: e.tensor_tensor(
                        st[:, 4 + m, :], st[:, 2, :], expert[:, m, :], ALU.mult), r)
            ready = {}
            for m in range(2 if masked else 1):
                for t in range(NT):
                    if kind == "layer":
                        ready[m, t] = dve.do(lambda e, it, t=t: e.tensor_scalar(
                            XN[:, 0, t, :], X[:, t, :], mean_var[:, t, 0:1], st[:, 2, t:t + 1],
                            ALU.subtract, ALU.mult), r)
                    elif m == 0:
                        s = 4 if masked else 2
                        ready[m, t] = dve.do(lambda e, it, t=t, s=s: e.tensor_scalar(
                            XN[:, 0, t, :], X[:, t, :], st[:, s, t:t + 1], None, ALU.mult),
                            r2 if masked else r)
                    else:
                        ready[m, t] = act.do(lambda e, it, t=t: e.activation(
                            XN[:, 1, t, :], X[:, t, :], ACT.Copy, scale=st[:, 5, t:t + 1]), r2)
            return transpose_in(2 if masked else 1, lambda k: vec(g, k),
                                (lambda k: vec(bias, k)) if bias else None, ready)

        def transpose_in(n_m, g, bias, ready):
            outs = []
            for m in range(n_m):
                for h in range(2):
                    for k in range(2):
                        i, bank, free = p.bank()
                        for j in range(4):
                            y = pe.do(lambda e, it, m=m, k=k, h=h, j=j, bank=bank: e.transpose(
                                bank[:, 128 * j:128 * j + 128],
                                XN[:, m, 4 * h + j, 128 * k:128 * k + 128], ident),
                                ready[m, 4 * h + j], free,
                                quiet=(j < 3))
                        dst = XT[:, 2 * m + k, 512 * h:512 * h + 512]
                        if bias:
                            z = act.do(lambda e, it, dst=dst, bank=bank, k=k: e.activation(
                                dst, bank[:, :], ACT.Identity, scale=g(k), bias=bias(k)), y)
                        elif g:
                            z = dve.do(lambda e, it, dst=dst, bank=bank, k=k: e.tensor_scalar(
                                dst, bank[:, :], g(k), None, ALU.mult), y)
                        else:
                            z = dve.do(lambda e, it, dst=dst, bank=bank: e.tensor_copy(
                                dst, bank[:, :]), y)
                        p.bank_free[i] = z
                        outs.append(z)
            return outs

        def pads(arr, k):
            return pool.do(lambda e, it: e.memset(
                arr.rearrange("p (x q) -> p x q", q=PAD)[:, 0:k * B, S:PAD], 0.0))

        kt0 = [QO_flat[:, i * KEYS:(i + 1) * KEYS] for i in range(4)]
        kn0 = [QO_flat[:, 4 * KEYS + i * KT * C:4 * KEYS + (i + 1) * KT * C] for i in range(4)]
        at0 = 4 * KEYS + 4 * KT * C
        q0T = QO_flat[:, at0:at0 + B * PAD].rearrange("p (b q) -> p b q", b=B)
        mcT = QO_flat[:, at0 + B * PAD:at0 + 2 * B * PAD]

        zero_q = pool.do(lambda e, it: e.memset(q0T, 0.0))
        pool.do(lambda e, it: e.memset(l0_zeros, 0.0))
        w0 = Point(s_w["l0"], s_w["l0"].count)
        for half in range(2):
            i, bank, x = product([(w_mem[:, k, :], x0T[:, k, HALF * half:HALF * half + HALF, 0:S])
                                  for k in range(2)], HALF * S, w0)
            p.bank_free[i] = scale_out(q0T[:, HALF * half:HALF * half + HALF, 0:S],
                                       real(bank[:, 0:HALF * S]), 1.0 / 16.0, x, zero_q)
        p.join()

        QS = W[:, 4096:4096 + 4 * PAD]

        def stage_q0(e, b, j):
            return e.tensor_copy(QS[:, b * PAD:(b + 1) * PAD],
                                 q0T[:, bass.ds(j * 4 + b, 1), :].rearrange("p o q -> p (o q)"))

        def dest0(g, j):
            return mcT.rearrange("p (t r) -> p t r", t=NT)[:, bass.ds(j * 2 + g, 1), :] \
                .rearrange("p o r -> p (o r)")

        memory_attention("l0", 4, [[(0, PAD, 0, 0), (PAD, PAD, 1, 0)], [(0, PAD, 2, 0), (PAD, PAD, 3, 0)]],
                  [([0], [2], [(0, 0, PAD, 0), (1, PAD, PAD, PAD)]),
                   ([1], [3], [(2, 0, PAD, 0), (3, PAD, PAD, PAD)])],
                  lambda b: QS[:, b * PAD:(b + 1) * PAD], dest0,
                  lambda b: kt0[b], lambda b: kn0[b], stage_q0, 2)

        load(w_memT, io["W_memT"], s_w["l0b"])
        load(w_gateT, io["W_gateT"].rearrange("(k p) n -> p k n", p=128), s_w["l0b"])
        load(b_gate, io["b_gate"].to_broadcast([128, D]), s_w["l0b"])
        load(norm_w, io["norm_w"].to_broadcast([128, D]), s_w["l0b"])
        load(X, io["x"], s_w["l0b"])
        load(vecs, io["vectors"], s_const)
        load(gates, io["gates"].to_broadcast([128, 4]), s_const)

        def w3(lo, k, n):
            return W[:, lo:lo + k * n].rearrange("p (k n) -> p k n", k=k)

        g_wq, g_wkT = w3(0, 2, INNER), w3(2048, 8, C)
        g_wo, g_w1, g_w2 = w3(4096, 8, D), w3(6144, 2, FF), w3(8192, 8, D)

        def load_gated_a(l, *waits):
            load(g_wq, io[f"L{l}_Wq"].rearrange("(k p) n -> p k n", p=128), s_w[f"l{l}a"], *waits)
            load(g_wkT, io[f"L{l}_WkT"].rearrange("(k p) n -> p k n", p=128), s_w[f"l{l}a"])
            load(value_w, io[f"L{l}_Wkv"][:, INNER:2 * INNER], s_w[f"l{l}a"])

        def load_gated_b(l, *waits):
            b = s_w[f"l{l}b"]
            load(g_wo, io[f"L{l}_Wo"].rearrange("(k p) n -> p k n", p=128), b, *waits)
            load(g_w1, io[f"L{l}_W1"].rearrange("(k p) n -> p k n", p=128), b)
            load(g_w2, io[f"L{l}_W2"].rearrange("(k p) n -> p k n", p=128), b)

        load_gated_a(1)
        w0 = Point(s_w["l0b"], s_w["l0b"].count)
        consts = Point(s_const, s_const.count)
        tanh_gates = act.do(lambda e, it: e.activation(gates, gates, ACT.Tanh), consts)

        mc_nat = A[:, 0:2048].rearrange("p (t d) -> p t d", t=NT)
        fused = A[:, 2048:4096].rearrange("p (t d) -> p t d", t=NT)
        junk = A[:, 4096:4352]
        for t in range(NT):
            i, bank, x = product([(mcT[:, 128 * t:128 * t + 128], w_memT)], D, w0)
            p.bank_free[i] = scale_out(mc_nat[:, t, :], bank[:, 0:D], 1.0, x, q=dve)
        for k in range(2):
            for h in range(2):
                i, bank, x = product([(w_memT[:, 128 * k:128 * k + 128], mcT[:, 512 * h:512 * h + 512])],
                                     512)
                p.bank_free[i] = mcTT = scale_out(XT[:, 2 + k, 512 * h:512 * h + 512], bank[:, :], 1.0, x,
                                                  q=act)
        fused_done = {}

        def square_sums(t):
            dve.do(lambda e, it: e.tensor_tensor_reduce(
                out=junk, in0=fused[:, t, :], in1=fused[:, t, :], scale=1.0, scalar=0.0,
                op0=ALU.mult, op1=ALU.add, accum_out=st[:, 3, t:t + 1]), fused_done[t], dve.last)

        for t in range(NT):
            i, bank, x = product([(XT[:, k, 128 * t:128 * t + 128], w_gateT[:, k, :])
                                  for k in range(4)], D, mcTT)
            a = dve.do(lambda e, it, t=t, bank=bank: e.tensor_tensor(
                fused[:, t, :], bank[:, 0:D], b_gate, ALU.add), x)
            p.bank_free[i] = a
            g = act.do(lambda e, it, t=t: e.activation(fused[:, t, :], fused[:, t, :], ACT.Sigmoid), a)
            m = pool.do(lambda e, it, t=t: e.tensor_tensor(
                fused[:, t, :], fused[:, t, :], mc_nat[:, t, :], ALU.mult), g, dve.last)
            m = pool.do(lambda e, it, t=t: e.tensor_tensor(
                fused[:, t, :], fused[:, t, :], X[:, t, :], ALU.add), m, w0)
            fused_done[t] = m
            if t:
                square_sums(t - 1)
        square_sums(NT - 1)
        ss = dve.last
        r = rstd(st[:, 3, :], 1e-6, 1.0 / D, ss)
        for t in range(NT):
            x = dve.do(lambda e, it, t=t: e.scalar_tensor_tensor(
                X[:, t, :], fused[:, t, :], st[:, 2, t:t + 1], norm_w, ALU.mult, ALU.mult), r)
            stats = tile_stats("layer", t, x)
        p.join()

        def residual(t, bank, x, gate):
            if gate is None:
                return dve.do(lambda e, it: e.tensor_tensor(X[:, t, :], bank[:, 0:D], X[:, t, :],
                                                            ALU.add), x)
            return dve.do(lambda e, it: e.scalar_tensor_tensor(
                X[:, t, :], bank[:, 0:D], gates[:, gate:gate + 1], X[:, t, :], ALU.mult, ALU.add), x)

        def head_queries(q_dst, half, h):
            return QO[:, HALF * half:HALF * half + HALF, S * h:S * h + S]

        wqkv, wden = w3(0, 4, 3 * D), w3(3072, 4, D)
        s_ty = p.tally("s_types")
        types = small[:, 0:2 * NT].bitcast(I32).rearrange("p (a t) -> p a t", a=2)
        pos = small[:, 64:64 + S].bitcast(I32)
        posf, onehot = small[:, 128:128 + S], small[:, 256:256 + 128]
        table, tidx = small[:, 448:448 + 2 * HD2], small[:, 512:513]

        def load_experts():
            for m, e in enumerate("vl"):
                load(wqkv[:, 2 * m:2 * m + 2, :],
                     io[f"L2_{e}_qkv"].rearrange("(k p) n -> p k n", p=128), s_w["l2q"])
                load(wden[:, 2 * m:2 * m + 2, :],
                     io[f"L2_{e}_dense"].rearrange("(k p) n -> p k n", p=128), s_w["l2q"])
            load(types, io["types"], s_ty)
            load(pos[0:S, :], io["pos"].to_broadcast([S, S]), s_ty)
            load(table[0:S, :], io["rope"], s_ty)
            load(tidx[0:S, :], io["index"], s_ty)
            load(head16, io["head16"], s_ty)
            load(head8, io["head8"], s_ty)
            load(causal, io["causal"], s_ty)

        def gated_block(l, stats):
            wa = Point(s_w[f"l{l}a"], s_w[f"l{l}a"].count)
            n = gated_names(l)
            xs = transposed_norm("layer", n["ln_q_g"], n["ln_q_b"], False, stats)
            qT = A[:, 0:8 * B * S].rearrange("p (j n) -> p j n", j=8)
            parts_done = {}
            for j in range(9):
                for half in range(2):
                    if j == 8:
                        continue
                    i, bank, x = product([(g_wq[:, k, 128 * j:128 * j + 128], tokens(XT, k, half))
                                          for k in range(2)], HALF * S, wa, *xs)
                    p.bank_free[i] = parts_done[j, half] = scale_out(
                        qT[:, j, HALF * S * half:HALF * S * (half + 1)], bank[:, 0:HALF * S],
                        DH ** -0.5, x)
                for half in range(2):
                    for hh in range(2):
                        if j == 0:
                            continue
                        i, bank, x = product(
                            [(g_wkT[64 * hh:64 * hh + 64, j - 1, :],
                              qT[64 * hh:64 * hh + 64, j - 1, HALF * S * half:HALF * S * (half + 1)])],
                            HALF * S, parts_done[j - 1, half])
                        p.bank_free[i] = scale_out(head_queries(QO, half, 2 * (j - 1) + hh),
                                                   real(bank[:, 0:HALF * S]), 1.0, x)
            p.join()
            cross_attention(f"l{l}", True)
            load_gated_b(l, *[q.last for q in p.queues[:4]])
            wb = Point(s_w[f"l{l}b"], s_w[f"l{l}b"].count)
            if l == 1:
                load_experts()

            aoT = A[:, 0:8 * B * PAD].rearrange("p (j n) -> p j n", j=8)
            z = pads(A, 8)
            for j in range(8):
                for half in range(2):
                    i, bank, free = p.bank()
                    for hh in range(2):
                        h = 2 * j + hh
                        x = pe.do(lambda e, it, h=h, hh=hh, half=half, bank=bank: e.matmul(
                            bank[64 * hh:64 * hh + 64, 0:HALF * S], value_w[:, DH * h:DH * h + DH],
                            head_queries(QO, half, h), start=True, stop=True), free, wa)
                    p.bank_free[i] = scale_out(tokens(aoT, j, half), real(bank[:, 0:HALF * S]), 1.0, x)
            both = [act.last, dve.last, z]
            for t in range(NT):
                i, bank, x = product([(aoT[:, j, 128 * t:128 * t + 128], g_wo[:, j, :])
                                      for j in range(8)], D, *both, wb)
                p.bank_free[i] = x = residual(t, bank, x, l - 1)
                stats = tile_stats("layer", t, x)
            xs = transposed_norm("layer", n["ln_ff_g"], n["ln_ff_b"], False, stats)
            pe_before = pe.last
            for j in range(8):
                for half in range(2):
                    i, bank, x = product([(g_w1[:, k, 128 * j:128 * j + 128], tokens(XT, k, half))
                                          for k in range(2)], HALF * S, *xs)
                    p.bank_free[i] = act.do(lambda e, it, j=j, half=half, bank=bank: e.activation(
                        tokens(aoT, j, half), real(bank[:, 0:HALF * S]), ACT.Gelu), x, pe_before)
            for t in range(NT):
                i, bank, x = product([(aoT[:, j, 128 * t:128 * t + 128], g_w2[:, j, :])
                                      for j in range(8)], D, act.last, z)
                p.bank_free[i] = x = residual(t, bank, x, l)
                stats = tile_stats("rms", t, x) if l == 1 else None
            p.join()
            return stats

        stats = gated_block(1, stats)

        wcq, wckT, wcv, wcd = w3(8960, 2, C), W[:, 9216:9344], value_w[:, 0:C], value_w[:, C:C + D]
        wgu = W[:, 0:8 * II].rearrange("p (x n) -> p x n", x=8)
        wdown = w3(8 * II, 12, D)
        free = [q.last for q in p.queues[:4]]
        load(wcq, io["L2_cq_w"].rearrange("(k p) n -> p k n", p=128), s_w["l2a"], *free)
        load(wckT, io["L2_ckT"], s_w["l2a"])
        load(wcv, io["L2_ckv_w"][:, C:2 * C], s_w["l2a"])
        load(wcd, io["L2_cdense_w"], s_w["l2a"])

        ty = Point(s_ty, s_ty.count)
        a = dve.do(lambda e, it: e.tensor_scalar(st[:, 6:8, :], types, 1.0, None,
                                                 ALU.is_equal), ty)
        a = dve.do(lambda e, it: e.tensor_tensor(expert[:, 0, :], st[:, 6, :], st[:, 7, :], ALU.mult), a)
        a = dve.do(lambda e, it: e.tensor_scalar(expert[:, 1, :], expert[:, 0, :], -1.0, 1.0,
                                                 ALU.mult, ALU.add), a)
        zo = dve.do(lambda e, it: e.memset(onehot[0:S, :], 0.0))
        b_ = dve.do(lambda e, it: e.tensor_scalar(posf[0:S, :], pos[0:S, :], 0.0, float(S - 1),
                                                  ALU.max, ALU.min), ty)
        oh = onehot[0:S, :].rearrange("p (a q) -> p a q", a=2)
        for par in range(2):
            b2 = dve.do(lambda e, it, par=par: e.tensor_scalar(
                oh[:, par, 0:S], posf[0:S, :], tidx[0:S, 0:1], None, ALU.is_equal), zo, b_)
        i, bank, x = product([(onehot[0:S, :], table[0:S, :])], 2 * HD2, b2)
        p.bank_free[i] = rp = dve.do(lambda e, it, bank=bank: e.tensor_copy(rope,
                                                                            bank[:, 0:2 * HD2]), x)
        cosb = rope[:, 0:HD2]
        sinb = rope[:, HD2:2 * HD2]

        QKT = QO_flat[:, 0:4096].rearrange("p (k n) -> p k n", k=4)
        V = QO_flat[:, 4096:6144].rearrange("p (t d) -> p t d", t=NT)
        QB = [QO_flat[:, at:at + 2048].rearrange("p (b k h q) -> p b k h q", b=2, k=2, h=8)
              for at in (6144, 8192)]
        SS = [QO_flat[:, at:at + 1024].rearrange("p (j b q) -> p j b q", j=8, b=2)
              for at in (10240, 11264)]
        ST = QO_flat[:, 12288:13312].rearrange("p (j r) -> p j r", j=8)
        VS = [QO_flat[:, at:at + D] for at in (13312, 13312 + D)]
        KS = [QO_flat[:, at:at + 2 * 128].rearrange("p (k n) -> p k n", k=2)
              for at in (13312 + 2 * D, 13312 + 3 * D)]
        for i in range(2):
            pool.do(lambda e, it, i=i: e.memset(SS[i], 0.0))
        p.join()
        xs = transposed_norm("rms", "L2_ln_in_w", None, True, stats)
        w2q = Point(s_w["l2q"], s_w["l2q"].count)
        w2a = Point(s_w["l2a"], s_w["l2a"].count)
        rotA = [A[:, i * 512:(i + 1) * 512] for i in range(2)]
        rotB = [A[:, 1024 + i * 512:1024 + (i + 1) * 512] for i in range(2)]
        before = [pe.last, dve.last, pool.last]
        transposes_done, rotated = {}, {}

        def transpose_rotated(t):
            a_, c3 = rotated[t]
            i3, bank3, free3 = p.bank()
            for k in range(4):
                y = pe.do(lambda e, it, k=k: e.transpose(
                    bank3[:, 128 * k:128 * k + 128], a_[:, 128 * k:128 * k + 128], ident), c3, free3)
            transposes_done[t] = y
            p.bank_free[i3] = scale_out(
                QKT[:, :, 128 * t:128 * t + 128], bank3[:, :].rearrange("p (k n) -> p k n", k=4),
                1.0, y, q=act)

        for t in range(NT):
            i, bank, x = product([(XT[:, k, 128 * t:128 * t + 128], wqkv[:, k, 0:2 * D])
                                  for k in range(4)], 2 * D, w2q, *xs)
            i2, bank2, x2 = product([(XT[:, k, 128 * t:128 * t + 128], wqkv[:, k, 2 * D:3 * D])
                                     for k in range(4)], D)
            p.bank_free[i2] = scale_out(V[:, t, :], bank2[:, 0:D], 1.0, x2, q=act)
            a_, b_ = rotA[t % 2], rotB[t % 2]
            old = transposes_done.get(t - 2)
            qk = bank[:, :].rearrange("p (h c) -> p h c", c=HD2)
            cb = cosb.rearrange("p (o c) -> p o c", o=1).to_broadcast([128, 32, HD2])
            c1 = dve.do(lambda e, it, a_=a_, qk=qk, cb=cb: e.tensor_tensor(
                a_.rearrange("p (h c) -> p h c", c=HD2), qk, cb, ALU.mult), x, rp, old, *before)
            for d in range(2):
                sb_ = sinb[:, 8 * d:8 * d + 8].rearrange("p (o c) -> p o c", o=1) \
                    .to_broadcast([128, 32, 8])
                c2 = dve.do(lambda e, it, b_=b_, qk=qk, d=d, sb_=sb_: e.tensor_tensor(
                    b_.rearrange("p (h c) -> p h c", c=HD2)[:, :, 8 * d:8 * d + 8],
                    qk[:, :, 8 - 8 * d:16 - 8 * d], sb_, ALU.mult), x)
            p.bank_free[i] = c2
            c3 = pool.do(lambda e, it, a_=a_, b_=b_: e.tensor_tensor(a_, a_, b_, ALU.add), c1, c2)
            rotated[t] = a_, c3
            if t:
                transpose_rotated(t - 1)
        transpose_rotated(NT - 1)
        p.join()

        CN = A[:, 4096:6144].rearrange("p (t d) -> p t d", t=NT)
        s_sq, s_sv, s_sc, s_se, s_tp, s_cp, s_cx, s_co = (p.tally(f"s_self_{n}") for n in (
            "staged_q", "staged_v", "scores", "exp", "transposed", "copied", "sums", "out"))
        s_s1, s_s2 = p.tally("s_self_shifted"), p.tally("s_self_normed")

        def self_trip(carried, loop, index, kind):
            now, missed = {}, set()

            def at(name, i):
                if (name, i) in now:
                    return now[(name, i)]
                if (name, i) in carried:
                    c = carried[(name, i)]
                    return Point(c.tally, c.value, loop) if loop else c
                missed.add((name, i))
                return None

            def pair(it, i):
                return index(it) * 2 + i

            def stage_queries(i):
                pool.do(lambda e, it: e.tensor_copy(
                    KS[i % 2], QKT[:, 2:4, bass.ds(pair(it, i) * 128, 128)]),
                    at("scores", i - 2), tally=s_sq)
                for b in range(2):
                    for k in range(2):
                        now[("q", i)] = pool.do(lambda e, it, b=b, k=k: e.tensor_tensor(
                            QB[i % 2][:, b, k], QKT[:, k, bass.ds(pair(it, i) * 128 + b * 64, 64)]
                            .rearrange("p (o q) -> p o q", o=1).to_broadcast([128, 8, PAD]),
                            head16.rearrange("p (h o) -> p h o", o=1).to_broadcast([128, 8, PAD]),
                            ALU.mult), at("scores", i - 2), tally=s_sq, apart=True)

            def stage_values(i):
                now[("v", i)] = pool.do(lambda e, it: e.tensor_copy(
                    VS[i % 2], V[:, bass.ds(pair(it, i), 1), :].rearrange("p o d -> p (o d)")),
                    at("sums", i - 2), tally=s_sv)

            def scores(i):
                for b in range(2):
                    for j in range(8):
                        now[("scores", i)] = pe.do(lambda e, it, b=b, j=j: e.matmul(
                            p.psum[6 * (i % 2) + b][:, 64 * j:64 * j + S],
                            QB[i % 2][:, b, j // 4, 2 * (j % 4):2 * (j % 4) + 2, :]
                            .rearrange("p h q -> p (h q)"),
                            KS[i % 2][:, j // 4, 64 * b:64 * b + S],
                            start=True, stop=True), at("q", i), at("masked", i - 2), tally=s_sc)

            def stats(n, i):
                return self_st[:, i % 2, n, :].rearrange("p (j b) -> p j b", j=8)

            def spread(x):
                return x.rearrange("p j (b o) -> p j b o", o=1).to_broadcast([128, 8, 2, S])

            def shift(i):
                s_ = SS[i % 2][:, :, :, 0:S]
                for b in range(2):
                    x = dve.do(lambda e, it, b=b: e.tensor_tensor(
                        SS[i % 2][:, :, b, 0:S],
                        p.psum[6 * (i % 2) + b][:, :].rearrange("p (j q) -> p j q", j=8)[:, :, 0:S],
                        causal.rearrange("p (o q) -> p o q", o=1).to_broadcast([128, 8, S]), ALU.add),
                        at("scores", i), at("transposed", i - 2), tally=s_s1, apart=True)
                now[("masked", i)] = x
                x = dve.do(lambda e, it: e.tensor_reduce(stats(0, i), s_, AX.X, ALU.max), x, tally=s_s1)
                now[("shifted", i)] = dve.do(lambda e, it: e.tensor_tensor(
                    s_, s_, spread(stats(0, i)), ALU.subtract), x, tally=s_s1, apart=True)

            def exponentials(i):
                now[("exp", i)] = act.do(lambda e, it: e.activation(
                    SS[i % 2][:, :, :, 0:S], SS[i % 2][:, :, :, 0:S], ACT.Exp),
                    at("shifted", i), tally=s_se)

            def normalise(i):
                s_ = SS[i % 2][:, :, :, 0:S]
                x = dve.do(lambda e, it: e.tensor_reduce(stats(1, i), s_, AX.X, ALU.add),
                           at("exp", i), tally=s_s2)
                x = dve.do(lambda e, it: e.reciprocal(self_st[:, i % 2, 2, :], self_st[:, i % 2, 1, :]),
                           x, tally=s_s2)
                now[("normed", i)] = dve.do(lambda e, it: e.tensor_tensor(
                    s_, s_, spread(stats(2, i)), ALU.mult), x, tally=s_s2, apart=True)

            def transposes(i):
                for j in range(8):
                    now[("transposed", i)] = pe.do(lambda e, it, j=j: e.transpose(
                        p.psum[2 + j // 4][:, 128 * (j % 4):128 * (j % 4) + 128],
                        SS[i % 2][:, j].rearrange("p b q -> p (b q)"), ident),
                        at("normed", i), at("copied", i - 1), tally=s_tp)
                for n in range(2):
                    now[("copied", i)] = act.do(lambda e, it, n=n: e.copy(
                        ST[:, 4 * n:4 * n + 4, :], p.psum[2 + n][:, :].rearrange("p (j r) -> p j r", j=4)),
                        at("transposed", i), at("sums", i - 1), tally=s_cp)

            def sums(i):
                for b in range(2):
                    for h in range(HEADS):
                        now[("sums", i)] = pe.do(lambda e, it, b=b, h=h: e.matmul(
                            p.psum[4 + b][64 * b:64 * b + 64, HD2 * h:HD2 * h + HD2],
                            ST[64 * b:64 * b + S, h // 2, 64 * (h % 2):64 * (h % 2) + 64],
                            VS[i % 2][64 * b:64 * b + S, HD2 * h:HD2 * h + HD2], start=True, stop=True),
                            at("copied", i), at("v", i), at("out", i - 1), tally=s_cx, apart=True)

            def outputs(i):
                for b in range(2):
                    now[("out", i)] = act.do(lambda e, it, b=b: e.copy(
                        CN[64 * b:64 * b + 64, bass.ds(pair(it, i), 1), :].rearrange("p o d -> p (o d)"),
                        p.psum[4 + b][64 * b:64 * b + 64, 0:D]), at("sums", i), tally=s_co)

            if kind == "start":
                stage_queries(0), stage_queries(1), scores(0)
                return now, missed
            for i in range(1 if kind == "drain" else 2):
                before = not (kind == "first" and i == 0)
                if kind != "drain":
                    stage_values(i)
                    if kind != "last":
                        stage_queries(i + 2)
                if before:
                    normalise(i - 1)
                    transposes(i - 1)
                if kind != "drain":
                    shift(i)
                    if kind != "last" or i == 0:
                        scores(i + 1)
                    exponentials(i)
                if before:
                    sums(i - 1)
                    outputs(i - 1)
            return now, missed

        def self_shifted(now):
            return {(n, i - 2): v for (n, i), v in now.items()}

        carried, _ = self_trip({}, None, lambda it: 0, "start")
        now, _ = self_trip(carried, None, lambda it: 0, "first")
        carried = {**self_shifted(carried), **self_shifted(now)}
        loop = p.open_loop(NT // 2 - 2)
        now, missed = self_trip(carried, loop, lambda it: it + 1, "more")
        p.close_loop(loop)
        after = self_shifted(now)
        for key, point in after.items():
            assert key not in missed, key
            if key in carried:
                assert point.value == carried[key].value + loop.per[point.tally], key
        now, _ = self_trip(after, None, lambda it: NT // 2 - 1, "last")
        self_trip({**self_shifted(after), **self_shifted(now)}, None, lambda it: NT // 2, "drain")
        p.join()

        ready = {}
        for m in range(2):
            for t in range(NT):
                ready[m, t] = dve.do(lambda e, it, m=m, t=t: e.tensor_scalar(
                    XN[:, m, t, :], CN[:, t, :], expert[:, m, t:t + 1], None, ALU.mult))
        xs = transpose_in(2, None, None, ready)
        for t in range(NT):
            i, bank, x = product([(XT[:, k, 128 * t:128 * t + 128], wden[:, k, :])
                                  for k in range(4)], D, *xs)
            p.bank_free[i] = x = residual(t, bank, x, None)
            stats = tile_stats("rms", t, x)
        xs = transposed_norm("rms", "L2_ln_post_cross_w", None, False, stats)
        cqT = A[:, 0:B * S]
        WM = A[:, 1024:3072].rearrange("p (h c) -> p h c", h=HEADS)
        wm = dve.do(lambda e, it: e.tensor_tensor(
            WM, wckT.rearrange("p (o c) -> p o c", o=1).to_broadcast([128, HEADS, C]),
            head8.rearrange("p (h o) -> p h o", o=1).to_broadcast([128, HEADS, C]), ALU.mult), w2a)
        for half in range(2):
            i, bank, x = product([(wcq[:, k, :], tokens(XT, k, half)) for k in range(2)], HALF * S, w2a,
                                 *xs)
            p.bank_free[i] = cq = scale_out(cqT[:, HALF * S * half:HALF * S * (half + 1)],
                                            bank[:, 0:HALF * S], CHD ** -0.5, x, q=dve)
        for h in range(HEADS):
            for half in range(2):
                i, bank, x = product([(WM[:, h, :], cqT[:, HALF * S * half:HALF * S * (half + 1)])],
                                     HALF * S, cq, wm)
                p.bank_free[i] = scale_out(head_queries(QO, half, h), real(bank[:, 0:HALF * S]), 1.0, x)
        p.join()
        cross_attention("l2", False)
        free = [q.last for q in p.queues[:4]]
        for m, e in enumerate("vl"):
            for g, n in enumerate(("gate", "up")):
                at_ = 4 * m + 2 * g
                load(wgu[:, at_:at_ + 2, :], io[f"L2_{e}_{n}"].rearrange("(k p) n -> p k n", p=128),
                     s_w["l2b"], *free)
            load(wdown[:, 6 * m:6 * m + 5, :],
                 io[f"L2_{e}_down"][0:640, :].rearrange("(k p) n -> p k n", p=128), s_w["l2b"])
            load(wdown[0:II - 640, 6 * m + 5, :], io[f"L2_{e}_down"][640:II, :], s_w["l2b"])
        w2b = Point(s_w["l2b"], s_w["l2b"].count)
        flat = A[:, 0:HEADS * (C + CHD)]
        CV = A[:, 0:HEADS * C].rearrange("p (h c) -> p h c", h=HEADS)
        z = pool.do(lambda e, it: e.memset(flat, 0.0))
        z = pool.do(lambda e, it: e.tensor_copy(
            flat.rearrange("p (h x) -> p h x", h=HEADS)[:, :, 0:CHD],
            wcv.rearrange("p (h x) -> p h x", h=HEADS)), z, w2a)
        cxT = A[:, 3072:3072 + B * PAD].rearrange("p (k n) -> p k n", k=1)
        zp = pool.do(lambda e, it: e.memset(
            A[:, 3072:3072 + B * PAD].rearrange("p (x q) -> p x q", q=PAD)[:, :, S:PAD], 0.0))
        for half in range(2):
            i, bank, x = product([(CV[:, h, :], head_queries(QO, half, h)) for h in range(HEADS)],
                                 HALF * S, z)
            p.bank_free[i] = cx = scale_out(tokens(cxT, 0, half), real(bank[:, 0:HALF * S]), 1.0, x,
                                            q=act)
        for t in range(NT):
            i, bank, x = product([(cxT[:, 0, 128 * t:128 * t + 128], wcd)], D, cx, zp)
            p.bank_free[i] = x = residual(t, bank, x, None)
            stats = tile_stats("rms", t, x)
        xs = transposed_norm("rms", "L2_ln_post_attn_w", None, True, stats)
        p.join()
        HT = A.rearrange("p (x n) -> p x n", x=12)
        z = pads(A, 12)
        for m in range(2):
            for n, (i0, rows) in enumerate(IT):
                for half in range(2):
                    dst = tokens(HT[0:rows], 6 * m + n, half)
                    i, bank, x = product([(wgu[:, 4 * m + k, i0:i0 + rows], tokens(XT, 2 * m + k, half))
                                          for k in range(2)], HALF * S, w2b, *xs, rows=rows)
                    p.bank_free[i] = g = act.do(lambda e, it, dst=dst, bank=bank, rows=rows: e.activation(
                        dst, real(bank[0:rows, 0:HALF * S]), ACT.Silu), x)
                    i, bank, x = product([(wgu[:, 4 * m + 2 + k, i0:i0 + rows],
                                           tokens(XT, 2 * m + k, half))
                                          for k in range(2)], HALF * S, rows=rows)
                    p.bank_free[i] = u = dve.do(lambda e, it, dst=dst, bank=bank, rows=rows: e.tensor_tensor(
                        dst, real(bank[0:rows, 0:HALF * S]), dst, ALU.mult), x, g)
        load_gated_a(3, pe.last)
        for t in range(NT):
            i, bank, x = product([(HT[0:rows, 6 * m + n, 128 * t:128 * t + 128],
                                   wdown[0:rows, 6 * m + n, :])
                                  for m in range(2) for n, (_, rows) in enumerate(IT)], D, u, z)
            p.bank_free[i] = x = residual(t, bank, x, None)
            stats = tile_stats("layer", t, x)
        p.join()

        gated_block(3, stats)
        for par in range(2):
            done = load(out[par], X[64 * par:64 * par + S, :, :], s_out, dve.last)
        sp.do(None, done, quiet=True)

        with nc.Block() as block:
            for name, q in (("sync", sp), ("gpsimd", pool), ("scalar", act), ("tensor", pe),
                            ("vector", dve)):
                def run(eng, q=q):
                    emit(eng, q.items, q.step)
                {"sync": block.sync, "gpsimd": block.gpsimd, "scalar": block.scalar,
                 "tensor": block.tensor, "vector": block.vector}[name](run)


def natural(a):
    z = np.zeros((B, PAD) + a.shape[2:], a.dtype)
    z[:, :S] = a
    return np.ascontiguousarray(z.reshape(NT, 128, *a.shape[2:]).swapaxes(0, 1))


def kernel(**inputs):
    import concourse.bacc as bacc
    from concourse.bass_utils import run_bass_kernel_spmd

    g = {n: np.asarray(v) for n, v in inputs.items()}
    key_order = np.arange(KEYS).reshape(KP, KT).T.reshape(-1)
    pad_T = np.zeros((D, B, PAD), np.float32)
    pad_T[:, :, :S] = g["x"].transpose(2, 0, 1)
    types = np.zeros((B, 2, PAD), np.int32)
    types[:, 0, :S] = g["mask_BxS_ik0"]
    types[:, 1, :S - 1] = g["mask_BxS_ik0"][:, 1:]
    types[:, 0, S - 1] = 0
    angle = np.outer(np.arange(S, dtype=np.float32),
                     (1.0 / 10000.0 ** (np.arange(0, HD2, 2, dtype=np.float32) / HD2)).astype(np.float32))
    part = np.arange(128)
    a = {
        "x": natural(g["x"]),
        "xT": np.ascontiguousarray(pad_T.reshape(2, 128, B * PAD).swapaxes(0, 1)),
        "ctx": g["ctx_1024"],
        "ctxT": np.ascontiguousarray(g["ctx_1024"][:, key_order].transpose(0, 2, 1)),
        "mask": np.ascontiguousarray(g["mask_BxS2_bk0"][:, key_order]),
        "types": np.ascontiguousarray(types.reshape(NT, 2, 2, PAD).transpose(1, 3, 2, 0).reshape(128, 2, NT)),
        "pos": g["pos_1xS"],
        "W_mem": g["L0_xattn_W_mem"], "W_memT": np.ascontiguousarray(g["L0_xattn_W_mem"].T),
        "W_gateT": np.ascontiguousarray(g["L0_xattn_W_gate"].T),
        "b_gate": g["L0_xattn_b_gate"].reshape(1, D), "norm_w": g["L0_xattn_norm_w"].reshape(1, D),
        "vectors": np.ascontiguousarray(np.concatenate(
            [g[n.replace("_", "_xattn_", 1)].reshape(2, 128).T for n in VECTORS], axis=1)),
        "gates": np.concatenate([g[f"L{l}_xattn_{n}_gate"] for l in (1, 3) for n in ("attn", "ff")])
                   .reshape(1, 4),
        "ident": np.eye(128, dtype=np.float32),
        "rope": np.concatenate([np.cos(angle), np.cos(angle), -np.sin(angle), np.sin(angle)],
                               axis=1).astype(np.float32),
        "index": np.arange(S, dtype=np.float32).reshape(S, 1),
        "head16": ((part[:, None] // HD2 == np.arange(8)) * HD2 ** -0.5).astype(np.float32),
        "head8": (part[:, None] // CHD == np.arange(HEADS)).astype(np.float32),
        "causal": np.where(np.arange(S) <= part[:, None] % PAD, 0.0, -BIG).astype(np.float32),
        "L2_ckT": np.ascontiguousarray(g["L2_xattn_ckv_w"][:, :C].T),
    }
    for l in (1, 3):
        for n in ("Wq", "Wkv", "Wo", "W1", "W2"):
            a[f"L{l}_{n}"] = g[f"L{l}_xattn_{n}"]
        a[f"L{l}_WkT"] = np.ascontiguousarray(g[f"L{l}_xattn_Wkv"][:, :INNER].T)
    for n in ("v_qkv", "l_qkv", "v_dense", "l_dense", "cq_w", "ckv_w", "cdense_w", "v_gate", "v_up",
              "v_down", "l_gate", "l_up", "l_down"):
        a[f"L2_{n}"] = g[f"L2_xattn_{n}"]

    nc = bacc.Bacc("TRN2", target_bir_lowering=False, num_devices=1)
    io = {n: nc.dram_tensor(f"in_{n}", v.shape, mybir.dt.from_np(v.dtype), kind="ExternalInput").ap()
          for n, v in a.items()}
    out = nc.dram_tensor("out", (2, S, NT, D), F32, kind="ExternalOutput").ap()
    build(nc, io, out)
    r = run_bass_kernel_spmd(nc, [{f"in_{n}": v for n, v in a.items()}], core_ids=[0])
    o = r.results[0]["out"]
    return np.ascontiguousarray(o.transpose(2, 0, 1, 3).reshape(B, S, D))
```
